# Optimizing a Trainium2 kernel written in Bass

```python
import numpy as np
import jax
import jax.numpy as jnp

def _softmax(x, axis=-1):
    return jax.nn.softmax(x, axis=axis)

def _gelu(x):
    return jax.nn.gelu(x, approximate=True)

def _silu(x):
    return jax.nn.silu(x)

def _sigmoid(x):
    return jax.nn.sigmoid(x)

def _layernorm(x, axis=-1, eps=1e-05):
    m = jnp.mean(x, axis=axis, keepdims=True)
    v = jnp.var(x, axis=axis, keepdims=True)
    return (x - m) / jnp.sqrt(v + eps)

def _scatter_add(tgt, idx, src, axis=0):
    return tgt.at[idx].add(src)

def _segment_sum(src, seg, n):
    return jax.ops.segment_sum(src, seg, n)
kernel_name = 'mk_adj_preln_d4_adj_r2_ad2e75'

def setup_inputs(seed: int=0):
    np.random.seed(seed)
    _w = jnp.asarray

    def _rec_inputs():
        import jax
        import jax.numpy as jnp
        _gk = jax.random.key(seed)
        x = -0.0005207 + 1.001 * jax.random.normal(jax.random.fold_in(_gk, 1), (2048, 128), jnp.float32)
        _w = (1.0 + jnp.arange(2048, dtype=jnp.float32)) ** (-0.5)
        _w = _w / _w.mean()
        _pij = jnp.clip(0.00390625 * _w[:, None] * _w[None, :], 0.0, 1.0)
        _a = jax.random.uniform(jax.random.fold_in(_gk, 2), (2048, 2048)) < _pij
        _a = jnp.logical_or(_a, jnp.eye(2048, dtype=bool))
        _af = _a.astype(jnp.float32)
        adj = _af
        return (x, adj)
    x, adj = _rec_inputs()

    def _L0_gnn_setup():
        import jax, jax.numpy as jnp
        import numpy as np
        N = 4096
        D_IN = 128
        D_OUT = 128
        key = jax.random.key(seed)
        k_x, k_a, k_w, k_bias = jax.random.split(key, 4)
        x = jax.random.normal(k_x, (N, D_IN), dtype=jnp.float32)
        A_shape = jax.random.randint(k_a, (N, N), 0, 2).astype(jnp.float32)
        A_shape = A_shape.at[jnp.arange(N), jnp.arange(N)].set(1.0)
        lim = 1.0 / np.sqrt(D_IN)
        W = jax.random.uniform(k_w, (D_OUT, D_IN), jnp.float32, -lim, lim)
        bias = jax.random.uniform(k_bias, (D_OUT,), jnp.float32, -lim, lim)
        b = jnp.ones((1,), dtype=jnp.float32)
        return {'x': x, 'A_shape': A_shape, 'W': W, 'bias': bias, 'b': b}
    _L0_gnn_all = _L0_gnn_setup()
    _L0_gnn_in = {k: v for k, v in _L0_gnn_all.items() if k in ('W', 'bias', 'b')}
    del _L0_gnn_all

    def _L1_gnn_setup():
        import jax, jax.numpy as jnp
        import numpy as np
        from jax import lax
        D_MODEL = 128
        D_STATE = 16
        D_CONV = 4
        EXPAND = 2
        D_INNER = EXPAND * D_MODEL
        DT_RANK = (D_MODEL + 15) // 16
        N = 2048
        EPS = 1e-05

        def _mamba(h, w_in, conv_w, conv_b, w_xp, w_dt, b_dt, A_log, D_skip, w_out):
            L = h.shape[0]
            xz = h @ w_in
            xc, z = (xz[:, :D_INNER], xz[:, D_INNER:])
            xpad = jnp.pad(xc, ((D_CONV - 1, 0), (0, 0)))
            xconv = sum((xpad[k:k + L] * conv_w[:, k] for k in range(D_CONV))) + conv_b
            u = jax.nn.silu(xconv)
            dbc = u @ w_xp
            dt = jax.nn.softplus(dbc[:, :DT_RANK] @ w_dt + b_dt)
            B = dbc[:, DT_RANK:DT_RANK + D_STATE]
            C = dbc[:, DT_RANK + D_STATE:]
            A = -jnp.exp(A_log)
            dA = jnp.exp(dt[:, :, None] * A[None])
            dBu = dt[:, :, None] * B[:, None, :] * u[:, :, None]

            def step(hst, inp):
                dAt, dBut, Ct = inp
                hst = dAt * hst + dBut
                return (hst, hst @ Ct)
            _, ys = lax.scan(step, jnp.zeros((D_INNER, D_STATE), h.dtype), (dA, dBu, C))
            y = ys + u * D_skip
            y = y * jax.nn.silu(z)
            return y @ w_out
        key = jax.random.key(seed)
        ks = jax.random.split(key, 16)
        x = jax.random.normal(ks[0], (N, D_MODEL), dtype=jnp.float32)
        a = jax.random.uniform(ks[1], (N, N), dtype=jnp.float32)
        adj = a / a.sum(axis=1, keepdims=True)
        s = lambda fi, fo: 1.0 / np.sqrt(fi)
        gcn_w = jax.random.uniform(ks[2], (D_MODEL, D_MODEL), jnp.float32, -s(D_MODEL, 0), s(D_MODEL, 0))
        gcn_b = jnp.zeros((D_MODEL,), jnp.float32)
        ln_g = jnp.ones((D_MODEL,), jnp.float32)
        ln_b = jnp.zeros((D_MODEL,), jnp.float32)
        w_in = jax.random.normal(ks[3], (D_MODEL, 2 * D_INNER), jnp.float32) * s(D_MODEL, 0)
        conv_w = jax.random.normal(ks[4], (D_INNER, D_CONV), jnp.float32) * s(D_CONV, 0)
        conv_b = jnp.zeros((D_INNER,), jnp.float32)
        w_xp = jax.random.normal(ks[5], (D_INNER, DT_RANK + 2 * D_STATE), jnp.float32) * s(D_INNER, 0)
        w_dt = jax.random.normal(ks[6], (DT_RANK, D_INNER), jnp.float32) * s(DT_RANK, 0)
        b_dt = jnp.log(jnp.expm1(jnp.exp(jax.random.uniform(ks[7], (D_INNER,), jnp.float32, np.log(0.001), np.log(0.1)))))
        A_log = jnp.log(jnp.broadcast_to(jnp.arange(1, D_STATE + 1, dtype=jnp.float32), (D_INNER, D_STATE)))
        D_skip = jnp.ones((D_INNER,), jnp.float32)
        w_out = jax.random.normal(ks[8], (D_INNER, D_MODEL), jnp.float32) * s(D_INNER, 0)
        return dict(x=x, adj=adj, gcn_w=gcn_w, gcn_b=gcn_b, ln_g=ln_g, ln_b=ln_b, w_in=w_in, conv_w=conv_w, conv_b=conv_b, w_xp=w_xp, w_dt=w_dt, b_dt=b_dt, A_log=A_log, D_skip=D_skip, w_out=w_out)
    _L1_gnn_all = _L1_gnn_setup()
    _L1_gnn_in = {k: v for k, v in _L1_gnn_all.items() if k in ('gcn_w', 'gcn_b', 'ln_g', 'ln_b', 'w_in', 'conv_w', 'conv_b', 'w_xp', 'w_dt', 'b_dt', 'A_log', 'D_skip', 'w_out')}
    del _L1_gnn_all

    def _L2_gnn_setup():
        import jax, jax.numpy as jnp
        import numpy as np
        N, F_IN, F_OUT, H, ALPHA = (1536, 128, 128, 8, 0.2)
        D = F_OUT // H
        LN_EPS = 1e-05

        def _xavier(key, shape, fan_in, fan_out):
            lim = np.sqrt(6.0 / (fan_in + fan_out))
            return jax.random.uniform(key, shape, jnp.float32, -lim, lim)
        key = jax.random.key(seed)
        ks = jax.random.split(key, 12)
        x = jax.random.normal(ks[0], (N, F_IN), jnp.float32)
        u = jax.random.uniform(ks[1], (N, N), jnp.float32)
        w = jax.random.uniform(ks[2], (N, N), jnp.float32)
        adj_matrix = jnp.where(u < 0.1, w, 0.0)
        W = _xavier(ks[3], (F_OUT, F_IN), F_IN, F_OUT)
        attn_src = _xavier(ks[4], (H, D), H * D, 1)
        attn_dst = _xavier(ks[5], (H, D), H * D, 1)
        edge_W = _xavier(ks[6], (H, 1), 1, H)
        edge_b = jnp.zeros((H,), jnp.float32)
        fuse_W = _xavier(ks[7], (F_OUT, F_OUT), F_OUT, F_OUT)
        fuse_b = jnp.zeros((F_OUT,), jnp.float32)
        ln_g = jnp.ones((F_OUT,), jnp.float32)
        ln_b = jnp.zeros((F_OUT,), jnp.float32)
        return {'x': x, 'adj_matrix': adj_matrix, 'W': W, 'attn_src': attn_src, 'attn_dst': attn_dst, 'edge_W': edge_W, 'edge_b': edge_b, 'fuse_W': fuse_W, 'fuse_b': fuse_b, 'ln_g': ln_g, 'ln_b': ln_b}
    _L2_gnn_all = _L2_gnn_setup()
    _L2_gnn_in = {k: v for k, v in _L2_gnn_all.items() if k in ('W', 'attn_src', 'attn_dst', 'edge_W', 'edge_b', 'fuse_W', 'fuse_b', 'ln_g', 'ln_b')}
    del _L2_gnn_all

    def _L3_gnn_setup():
        import jax, jax.numpy as jnp
        import numpy as np
        N, H, HEADS = (2048, 128, 3)
        ALPHA = 0.2
        NEG_INF = -9000000000000000.0

        def _sign_adj(key, n, density):
            k1, k2 = jax.random.split(key)
            mask = jax.random.uniform(k1, (n, n)) < density
            sign = jnp.where(jax.random.uniform(k2, (n, n)) < 0.5, -1.0, 1.0)
            adj = jnp.where(mask, sign, 0.0).astype(jnp.float32)
            idx = jnp.arange(n)
            return adj.at[idx, idx].set(1.0)

        def _gru_cell(x, hstate, Wih, Whh, bih, bhh):
            gi = x @ Wih.T + bih
            gh = hstate @ Whh.T + bhh
            ir, iz, inn = jnp.split(gi, 3, axis=1)
            hr, hz, hn = jnp.split(gh, 3, axis=1)
            r = jax.nn.sigmoid(ir + hr)
            z = jax.nn.sigmoid(iz + hz)
            n = jnp.tanh(inn + r * hn)
            return (1.0 - z) * n + z * hstate

        def _gat_head(h, node_adj, edge_adj, W, a):
            hW = h @ W
            hp = (node_adj > 0).astype(hW.dtype) @ hW
            hm = (node_adj < 0).astype(hW.dtype) @ hW
            e_plus = jax.nn.leaky_relu(jnp.concatenate([hp, hm], axis=1) @ a, ALPHA)[:, 0]
            e_minus = jax.nn.leaky_relu(jnp.concatenate([hm, hp], axis=1) @ a, ALPHA)[:, 0]
            att = jnp.where(edge_adj > 0, e_plus[None, :], NEG_INF)
            att = jnp.where(edge_adj < 0, e_minus[None, :], att)
            att = jax.nn.softmax(att, axis=1)
            return att * edge_adj @ hW
        key = jax.random.key(seed)
        ks = jax.random.split(key, 16)
        std = 0.01
        gain = 1.414
        return {'h': jax.random.normal(ks[0], (N, H), jnp.float32), 'node_adj': _sign_adj(ks[1], N, 0.005), 'edge_adj': _sign_adj(ks[2], N, 0.005), 'gat_W': jax.random.normal(ks[3], (HEADS, H, H), jnp.float32) * (gain / np.sqrt(H, dtype=np.float32)), 'gat_a': jax.random.normal(ks[4], (HEADS, 2 * H, 1), jnp.float32) * 0.1, 'edge_Wih': jax.random.normal(ks[5], (3 * H, H), jnp.float32) * std, 'edge_Whh': jax.random.normal(ks[6], (3 * H, H), jnp.float32) * std, 'edge_bih': jnp.zeros((3 * H,), jnp.float32), 'edge_bhh': jnp.zeros((3 * H,), jnp.float32), 'node_Wih': jax.random.normal(ks[7], (3 * H, H), jnp.float32) * std, 'node_Whh': jax.random.normal(ks[8], (3 * H, H), jnp.float32) * std, 'node_bih': jnp.zeros((3 * H,), jnp.float32), 'node_bhh': jnp.zeros((3 * H,), jnp.float32)}
    _L3_gnn_all = _L3_gnn_setup()
    _L3_gnn_in = {k: v for k, v in _L3_gnn_all.items() if k in ('gat_W', 'gat_a', 'edge_Wih', 'edge_Whh', 'edge_bih', 'edge_bhh', 'node_Wih', 'node_Whh', 'node_bih', 'node_bhh')}
    del _L3_gnn_all
    return {'x': x, 'adj': adj, 'L0_gnn_W': _L0_gnn_in['W'], 'L0_gnn_bias': _L0_gnn_in['bias'], 'L0_gnn_b': _L0_gnn_in['b'], 'L1_gnn_gcn_w': _L1_gnn_in['gcn_w'], 'L1_gnn_gcn_b': _L1_gnn_in['gcn_b'], 'L1_gnn_ln_g': _L1_gnn_in['ln_g'], 'L1_gnn_ln_b': _L1_gnn_in['ln_b'], 'L1_gnn_w_in': _L1_gnn_in['w_in'], 'L1_gnn_conv_w': _L1_gnn_in['conv_w'], 'L1_gnn_conv_b': _L1_gnn_in['conv_b'], 'L1_gnn_w_xp': _L1_gnn_in['w_xp'], 'L1_gnn_w_dt': _L1_gnn_in['w_dt'], 'L1_gnn_b_dt': _L1_gnn_in['b_dt'], 'L1_gnn_A_log': _L1_gnn_in['A_log'], 'L1_gnn_D_skip': _L1_gnn_in['D_skip'], 'L1_gnn_w_out': _L1_gnn_in['w_out'], 'L2_gnn_W': _L2_gnn_in['W'], 'L2_gnn_attn_src': _L2_gnn_in['attn_src'], 'L2_gnn_attn_dst': _L2_gnn_in['attn_dst'], 'L2_gnn_edge_W': _L2_gnn_in['edge_W'], 'L2_gnn_edge_b': _L2_gnn_in['edge_b'], 'L2_gnn_fuse_W': _L2_gnn_in['fuse_W'], 'L2_gnn_fuse_b': _L2_gnn_in['fuse_b'], 'L2_gnn_ln_g': _L2_gnn_in['ln_g'], 'L2_gnn_ln_b': _L2_gnn_in['ln_b'], 'L3_gnn_gat_W': _L3_gnn_in['gat_W'], 'L3_gnn_gat_a': _L3_gnn_in['gat_a'], 'L3_gnn_edge_Wih': _L3_gnn_in['edge_Wih'], 'L3_gnn_edge_Whh': _L3_gnn_in['edge_Whh'], 'L3_gnn_edge_bih': _L3_gnn_in['edge_bih'], 'L3_gnn_edge_bhh': _L3_gnn_in['edge_bhh'], 'L3_gnn_node_Wih': _L3_gnn_in['node_Wih'], 'L3_gnn_node_Whh': _L3_gnn_in['node_Whh'], 'L3_gnn_node_bih': _L3_gnn_in['node_bih'], 'L3_gnn_node_bhh': _L3_gnn_in['node_bhh']}

def reference(x, adj, L0_gnn_W, L0_gnn_bias, L0_gnn_b, L1_gnn_gcn_w, L1_gnn_gcn_b, L1_gnn_ln_g, L1_gnn_ln_b, L1_gnn_w_in, L1_gnn_conv_w, L1_gnn_conv_b, L1_gnn_w_xp, L1_gnn_w_dt, L1_gnn_b_dt, L1_gnn_A_log, L1_gnn_D_skip, L1_gnn_w_out, L2_gnn_W, L2_gnn_attn_src, L2_gnn_attn_dst, L2_gnn_edge_W, L2_gnn_edge_b, L2_gnn_fuse_W, L2_gnn_fuse_b, L2_gnn_ln_g, L2_gnn_ln_b, L3_gnn_gat_W, L3_gnn_gat_a, L3_gnn_edge_Wih, L3_gnn_edge_Whh, L3_gnn_edge_bih, L3_gnn_edge_bhh, L3_gnn_node_Wih, L3_gnn_node_Whh, L3_gnn_node_bih, L3_gnn_node_bhh):
    import jax
    import jax.numpy as jnp

    def _L0_gnn_ref(x, A_shape, W, bias, b):
        import jax, jax.numpy as jnp
        import numpy as np
        N = 4096
        D_IN = 128
        D_OUT = 128
        y = jnp.linalg.norm(x, axis=-1, keepdims=True)
        A = x @ x.T / (y @ y.T)
        A = A * b
        A = jnp.tanh(A / 8.0) * 8.0
        A = jnp.exp(A) * A_shape
        A = A / jnp.sum(A, axis=-1, keepdims=True)
        x = A @ x
        return x @ W.T + bias

    def _L1_gnn_ref(x, adj, gcn_w, gcn_b, ln_g, ln_b, w_in, conv_w, conv_b, w_xp, w_dt, b_dt, A_log, D_skip, w_out):
        import jax, jax.numpy as jnp
        import numpy as np
        from jax import lax
        D_MODEL = 128
        D_STATE = 16
        D_CONV = 4
        EXPAND = 2
        D_INNER = EXPAND * D_MODEL
        DT_RANK = (D_MODEL + 15) // 16
        N = 2048
        EPS = 1e-05

        def _mamba(h, w_in, conv_w, conv_b, w_xp, w_dt, b_dt, A_log, D_skip, w_out):
            L = h.shape[0]
            xz = h @ w_in
            xc, z = (xz[:, :D_INNER], xz[:, D_INNER:])
            xpad = jnp.pad(xc, ((D_CONV - 1, 0), (0, 0)))
            xconv = sum((xpad[k:k + L] * conv_w[:, k] for k in range(D_CONV))) + conv_b
            u = jax.nn.silu(xconv)
            dbc = u @ w_xp
            dt = jax.nn.softplus(dbc[:, :DT_RANK] @ w_dt + b_dt)
            B = dbc[:, DT_RANK:DT_RANK + D_STATE]
            C = dbc[:, DT_RANK + D_STATE:]
            A = -jnp.exp(A_log)
            dA = jnp.exp(dt[:, :, None] * A[None])
            dBu = dt[:, :, None] * B[:, None, :] * u[:, :, None]

            def step(hst, inp):
                dAt, dBut, Ct = inp
                hst = dAt * hst + dBut
                return (hst, hst @ Ct)
            _, ys = lax.scan(step, jnp.zeros((D_INNER, D_STATE), h.dtype), (dA, dBu, C))
            y = ys + u * D_skip
            y = y * jax.nn.silu(z)
            return y @ w_out
        h = jax.nn.relu(adj @ x @ gcn_w + gcn_b)
        mu = h.mean(-1, keepdims=True)
        var = h.var(-1, keepdims=True)
        h = (h - mu) * lax.rsqrt(var + EPS) * ln_g + ln_b
        return _mamba(h, w_in, conv_w, conv_b, w_xp, w_dt, b_dt, A_log, D_skip, w_out)

    def _L2_gnn_ref(x, adj_matrix, W, attn_src, attn_dst, edge_W, edge_b, fuse_W, fuse_b, ln_g, ln_b):
        import jax, jax.numpy as jnp
        import numpy as np
        N, F_IN, F_OUT, H, ALPHA = (1536, 128, 128, 8, 0.2)
        D = F_OUT // H
        LN_EPS = 1e-05

        def _xavier(key, shape, fan_in, fan_out):
            lim = np.sqrt(6.0 / (fan_in + fan_out))
            return jax.random.uniform(key, shape, jnp.float32, -lim, lim)
        n = x.shape[0]
        h = (x @ W.T).reshape(n, H, D)
        a_src = jnp.einsum('nhd,hd->nh', h, attn_src)
        a_dst = jnp.einsum('nhd,hd->nh', h, attn_dst)
        attn = a_src[:, None, :] + a_dst[None, :, :]
        attn = attn + adj_matrix[:, :, None] * edge_W[:, 0] + edge_b
        mask = (adj_matrix > 0)[:, :, None]
        attn = jnp.where(mask, attn, -jnp.inf)
        attn = jnp.where(attn >= 0, attn, ALPHA * attn)
        attn = jax.nn.softmax(attn, axis=1)
        h_out = jnp.einsum('ijh,jhd->ihd', attn, h).reshape(n, H * D)
        y = h_out @ fuse_W.T + fuse_b
        mu = jnp.mean(y, axis=-1, keepdims=True)
        var = jnp.mean(jnp.square(y - mu), axis=-1, keepdims=True)
        y = (y - mu) * jax.lax.rsqrt(var + LN_EPS) * ln_g + ln_b
        return jax.nn.relu(y)

    def _L3_gnn_ref(h, node_adj, edge_adj, gat_W, gat_a, edge_Wih, edge_Whh, edge_bih, edge_bhh, node_Wih, node_Whh, node_bih, node_bhh):
        import jax, jax.numpy as jnp
        import numpy as np
        N, H, HEADS = (2048, 128, 3)
        ALPHA = 0.2
        NEG_INF = -9000000000000000.0

        def _sign_adj(key, n, density):
            k1, k2 = jax.random.split(key)
            mask = jax.random.uniform(k1, (n, n)) < density
            sign = jnp.where(jax.random.uniform(k2, (n, n)) < 0.5, -1.0, 1.0)
            adj = jnp.where(mask, sign, 0.0).astype(jnp.float32)
            idx = jnp.arange(n)
            return adj.at[idx, idx].set(1.0)

        def _gru_cell(x, hstate, Wih, Whh, bih, bhh):
            gi = x @ Wih.T + bih
            gh = hstate @ Whh.T + bhh
            ir, iz, inn = jnp.split(gi, 3, axis=1)
            hr, hz, hn = jnp.split(gh, 3, axis=1)
            r = jax.nn.sigmoid(ir + hr)
            z = jax.nn.sigmoid(iz + hz)
            n = jnp.tanh(inn + r * hn)
            return (1.0 - z) * n + z * hstate

        def _gat_head(h, node_adj, edge_adj, W, a):
            hW = h @ W
            hp = (node_adj > 0).astype(hW.dtype) @ hW
            hm = (node_adj < 0).astype(hW.dtype) @ hW
            e_plus = jax.nn.leaky_relu(jnp.concatenate([hp, hm], axis=1) @ a, ALPHA)[:, 0]
            e_minus = jax.nn.leaky_relu(jnp.concatenate([hm, hp], axis=1) @ a, ALPHA)[:, 0]
            att = jnp.where(edge_adj > 0, e_plus[None, :], NEG_INF)
            att = jnp.where(edge_adj < 0, e_minus[None, :], att)
            att = jax.nn.softmax(att, axis=1)
            return att * edge_adj @ hW
        dn = jnp.diag(node_adj)
        de = jnp.diag(edge_adj)
        idx = jnp.arange(node_adj.shape[0])
        node_adj_norm = node_adj.at[idx, idx].add(-dn)
        edge_adj_norm = edge_adj.at[idx, idx].add(-de)
        node_support = node_adj_norm @ h
        edge_output = _gru_cell(node_support, h, edge_Wih, edge_Whh, edge_bih, edge_bhh)
        edge_support = _gat_head(h, node_adj_norm, edge_adj_norm, gat_W[0], gat_a[0])
        for i in range(1, HEADS):
            edge_support = edge_support + _gat_head(h, node_adj_norm, edge_adj_norm, gat_W[i], gat_a[i])
        edge_support = edge_support / HEADS
        node_output = _gru_cell(edge_support, h, node_Wih, node_Whh, node_bih, node_bhh)
        return de[:, None] * edge_output + dn[:, None] * node_output
    h = jnp.maximum(_layernorm(x, axis=-1), 0.0)
    x = x + _L0_gnn_ref(h, adj, L0_gnn_W, L0_gnn_bias, L0_gnn_b)
    h = jnp.maximum(_layernorm(x, axis=-1), 0.0)
    x = x + _L1_gnn_ref(h, adj, L1_gnn_gcn_w, L1_gnn_gcn_b, L1_gnn_ln_g, L1_gnn_ln_b, L1_gnn_w_in, L1_gnn_conv_w, L1_gnn_conv_b, L1_gnn_w_xp, L1_gnn_w_dt, L1_gnn_b_dt, L1_gnn_A_log, L1_gnn_D_skip, L1_gnn_w_out)
    h = jnp.maximum(_layernorm(x, axis=-1), 0.0)
    x = x + _L2_gnn_ref(h, adj, L2_gnn_W, L2_gnn_attn_src, L2_gnn_attn_dst, L2_gnn_edge_W, L2_gnn_edge_b, L2_gnn_fuse_W, L2_gnn_fuse_b, L2_gnn_ln_g, L2_gnn_ln_b)
    h = jnp.maximum(_layernorm(x, axis=-1), 0.0)
    x = x + _L3_gnn_ref(h, adj, adj, L3_gnn_gat_W, L3_gnn_gat_a, L3_gnn_edge_Wih, L3_gnn_edge_Whh, L3_gnn_edge_bih, L3_gnn_edge_bhh, L3_gnn_node_Wih, L3_gnn_node_Whh, L3_gnn_node_bih, L3_gnn_node_bhh)
    return x

_drawn_inputs = setup_inputs


def setup_inputs(seed=0):
    import zlib

    import numpy as np

    out = dict(_drawn_inputs(seed))
    spreads = {'L1_gnn_gcn_b': (0.0, 0.1),
     'L1_gnn_ln_g': (1.0, 0.2),
     'L1_gnn_ln_b': (0.0, 0.1),
     'L1_gnn_conv_b': (0.0, 0.1),
     'L1_gnn_D_skip': (1.0, 0.2),
     'L2_gnn_edge_b': (0.0, 2.0),
     'L2_gnn_fuse_b': (0.0, 0.1),
     'L2_gnn_ln_g': (1.0, 0.2),
     'L2_gnn_ln_b': (0.0, 0.1),
     'L3_gnn_edge_bih': (0.0, 0.375),
     'L3_gnn_edge_bhh': (0.0, 0.539),
     'L3_gnn_node_bih': (0.0, 0.321),
     'L3_gnn_node_bhh': (0.0, 0.504)}
    factors = {'L1_gnn_w_dt': 3.752,
     'L2_gnn_attn_src': 10.715,
     'L3_gnn_gat_W': 3.535,
     'L3_gnn_gat_a': 8.0,
     'L3_gnn_edge_Whh': 4.872,
     'L3_gnn_node_Wih': 3.294,
     'L3_gnn_node_Whh': 4.977,
     'L2_gnn_edge_W': 3.405}
    for name, (base, spread) in spreads.items():
        noise = np.random.default_rng([zlib.crc32(name.encode()), seed]).standard_normal(out[name].shape)
        drawn = base * np.exp(spread * noise) if base else spread * noise
        out[name] = jnp.asarray(drawn.astype(out[name].dtype))
    for name, factor in factors.items():
        out[name] = (out[name] * factor).astype(out[name].dtype)
    return out
```

```python
from contextlib import ExitStack

import numpy as np

import concourse.bass as bass
from concourse import mybir

ALU = mybir.AluOpType
ACT = mybir.ActivationFunctionType
F32 = mybir.dt.float32
BF16 = mybir.dt.bfloat16
AX_X = mybir.AxisListType.X
ds = bass.ds

P = 128
N = 2048
D = 128
NB = N // P
CH = 512
NC = N // CH
EPS = 1e-5
DI = 256
CB = DI // P
DS = 16
DTR = 8
KC = 4
XP = DTR + 2 * DS
H2 = 8
HD = D // H2
H3 = 3
BIG = 1e30
ROWB = 3
LAYERS = (0, 1, 2, 3)


class Steps:

    def __init__(self, eng, sem):
        self.eng, self.sem, self.n, self.turn = eng, sem, 0, 0

    def __call__(self, ins):
        ins.then_inc(self.sem, 1)
        self.n += 1
        self.eng.wait_ge(self.sem, self.turn + self.n)

    def begin(self, turn_index, per_turn):
        self.turn = turn_index * per_turn

    def on(self, eng):
        self.eng = eng
        return self

    def end(self, turns, start, per_turn):
        assert self.n - start == per_turn, (self.n, start, per_turn)
        self.n = start + turns * per_turn
        self.turn = 0


class Core:

    def __init__(self, nc, io, ctx):
        self.nc, self.io, self.ctx = nc, io, ctx
        self.adjT = self.sb(ctx, "adjT", [P, NB * N])
        self.x = self.sb(ctx, "x_nat", [P, NB, D])
        self.ident = self.sb(ctx, "ident", [P, P])
        self.ident_b = self.sb(ctx, "ident_b", [P, P], BF16)
        self.zeros = self.sb(ctx, "zeros", [P, CH], BF16)
        self.eps = self.sb(ctx, "eps", [P, 1])
        self.adj_even = self.sem("adj_even")
        self.adj_odd = self.sem("adj_odd")
        self.steps = Steps(None, self.sem("dve_steps"))
        self.act_waits = self.sem("act_waits_carried")
        self.pool_waits = self.sem("pool_waits_carried")

    def sb(self, ctx, name, shape, dt=F32):
        return ctx.enter_context(self.nc.sbuf_tensor(name, shape, dt))

    def ps(self, ctx, name, shape, dt=F32):
        return ctx.enter_context(self.nc.psum_tensor(name, shape, dt))

    def sem(self, name):
        return self.ctx.enter_context(self.nc.semaphore(name))

    def block(self):
        return self.nc.Block(no_gpsimd_drain=True)

    def carry(self, eng, sem):
        eng.sem_inc(sem, 1)

    def adj_rows(self, jb, i0=0, n=N):
        return self.adjT[:, ds(jb * N + i0, n)]


def per_block(t, n=D):
    return t.unsqueeze(2).broadcast_to([t.shape[0], t.shape[1], n])


def row(t, nb=NB):
    return t.unsqueeze(1).broadcast_to([t.shape[0], nb, t.shape[1]])


def center_and_sum(v, step, src, cen, sq, mean, var):
    step(v.tensor_reduce(mean, src, AX_X, ALU.add))
    step(v.tensor_scalar(mean, mean, 1.0 / D, None, ALU.mult))
    step(v.tensor_tensor(cen, src, per_block(mean), ALU.subtract))
    step(v.tensor_tensor(sq, cen, cen, ALU.mult))
    step(v.tensor_reduce(var, sq, AX_X, ALU.add))


def stage_start(k):
    io = k.io
    s_load, s_const = k.sem("start_loaded"), k.sem("start_const")
    with k.block() as block:

        @block.sync
        def _(sp):
            sp.dma_start(k.x[:, :, :], io["x"].rearrange("(b p) f -> p b f", p=P)).then_inc(s_load, 16)
            sp.dma_start(k.ident[:, :], io["ident"]).then_inc(s_load, 16)
            sp.wait_ge(s_load, 32)
            if 0 not in LAYERS:
                load_adjacency(k, sp)

        @block.vector
        def _(v):
            v.memset(k.zeros[:, :], 0.0)
            v.memset(k.eps[:, :], EPS)
            v.wait_ge(s_load, 32)
            v.tensor_copy(k.ident_b[:, :], k.ident[:, :]).then_inc(s_const, 1)


def load_adjacency(k, sp, first=0):
    adj = k.io["adjT"].rearrange("(b p) i -> p b i", p=P)
    for jb in range(first, NB):
        s, n = (k.adj_even, k.adj_odd)[jb % 2], jb // 2
        if n:
            sp.wait_ge(s, 16 * n)
        sp.dma_start(k.adj_rows(jb), adj[:, jb, :]).then_inc(s, 16)


def layer0(k):
    nc, io = k.nc, k.io
    with ExitStack() as ctx:
        gT = k.sb(ctx, "l0_gT", [P, N])
        V = k.sb(ctx, "l0_V", [P, NB, D + 1])
        wT = k.sb(ctx, "l0_wT", [D, D])
        bias = k.sb(ctx, "l0_bias", [P, D])
        b8 = k.sb(ctx, "l0_b8", [P, 1])
        T = k.sb(ctx, "l0_T", [P, 2, N])
        Pm = k.sb(ctx, "l0_P", [P, 2, N])
        stat = k.sb(ctx, "l0_stat", [P, 2, P])
        mean = k.sb(ctx, "l0_mean", [P, NB])
        var = k.sb(ctx, "l0_var", [P, NB])
        norm = k.sb(ctx, "l0_norm", [P, NB])
        rn = k.sb(ctx, "l0_rn", [P, NB])
        h = T[:, 0, :].rearrange("p (b f) -> p b f", f=D)
        sq = T[:, 1, :].rearrange("p (b f) -> p b f", f=D)
        g = Pm[:, 0, :].rearrange("p (b f) -> p b f", f=D)

        s_w, s_var, s_std, s_ss, s_nrm = (k.sem("l0_" + n) for n in ("w_loaded", "var", "std", "sumsq", "norm"))
        s_g, s_gp, s_gt, s_vp = (k.sem("l0_" + n) for n in ("g_ready", "g_turned", "gT_ready", "V_product"))
        with k.block() as block, ExitStack() as pctx:
            tr = k.ps(pctx, "l0_tr", [P, 4, CH])
            vp = k.ps(pctx, "l0_vp", [P, 4, CH])

            @block.sync
            def _(sp):
                sp.dma_start(wT[:, :], io["L0_WT"]).then_inc(s_w, 16)
                sp.dma_start(bias[:, :], io["L0_bias"].partition_broadcast(P)).then_inc(s_w, 16)
                sp.dma_start(b8[:, :], io["L0_b"].partition_broadcast(P)).then_inc(s_w, 16)
                load_adjacency(k, sp)
                sp.wait_ge(s_w, 48)

            @block.vector
            def _(v):
                step = k.steps.on(v)
                center_and_sum(v, step, k.x[:, :, :], h, sq, mean[:, :], var[:, :])
                v.sem_inc(s_var, 1)
                v.wait_ge(s_std, 1)
                step(v.reciprocal(rn[:, :], norm[:, :]))
                step(v.scalar_tensor_tensor(h, h, 0.0, per_block(rn[:, :]), ALU.max, ALU.mult))
                step(v.tensor_tensor(sq, h, h, ALU.mult))
                step(v.tensor_reduce(var[:, :], sq, AX_X, ALU.add))
                v.sem_inc(s_ss, 1)
                v.wait_ge(s_nrm, 1)
                step(v.reciprocal(rn[:, :], norm[:, :]))
                v.tensor_tensor(g, h, per_block(rn[:, :]), ALU.mult).then_inc(s_g, 1)
                v.memset(V[:, :, D:D + 1], 1.0)
                v.wait_ge(s_w, 48)
                v.tensor_scalar(b8[:, :], b8[:, :], 0.125, None, ALU.mult)
                for c in range(4):
                    v.wait_ge(s_vp, 4 * c + 4)
                    v.tensor_tensor(V[:, 4 * c:4 * c + 4, 0:D], vp[:, c, :].rearrange("p (b f) -> p b f", f=D),
                                    per_block(norm[:, 4 * c:4 * c + 4]), ALU.mult)

            @block.scalar
            def _(act):
                act.wait_ge(s_var, 1)
                act.activation(norm[:, :], var[:, :], ACT.Sqrt, bias=k.eps[:, :], scale=1.0 / D).then_inc(s_std, 1)
                act.wait_ge(s_ss, 1)
                act.activation(norm[:, :], var[:, :], ACT.Sqrt).then_inc(s_nrm, 1)
                for c in range(4):
                    act.wait_ge(s_gp, 4 * c + 4)
                    act.activation(gT[:, ds(c * CH, CH)], tr[:, c, :], ACT.Copy).then_inc(s_gt, 1)

            @block.tensor
            def _(pe):
                pe.wait_ge(s_g, 1)
                for b in range(NB):
                    pe.transpose(tr[:, b // 4, ds(b % 4 * P, P)], g[:, b, :], k.ident[:, :]).then_inc(s_gp, 1)
                pe.wait_ge(s_w, 48)
                for b in range(NB):
                    pe.wait_ge(s_gt, b // 4 + 1)
                    pe.matmul(vp[:, b // 4, ds(b % 4 * P, P)], gT[:, ds(b * P, P)], wT[:, :], start=True, stop=True).then_inc(s_vp, 1)

        s_stat, s_score, s_tanh, s_exp, s_p, s_pv = (k.sem("l0_" + n) for n in ("stationary", "score", "tanh", "exp", "probs", "pv"))
        with k.block() as block, ExitStack() as pctx:
            S = k.ps(pctx, "l0_S", [P, 2, CH])
            acc = k.ps(pctx, "l0_acc", [P, 6, CH])

            @block.gpsimd
            def _(pool):
                with pool.Fori(0, NB // 2) as t:
                    for u in range(2):
                        if u == 0:
                            pool.wait_ge(s_score, t * 8 + 4)
                        else:
                            pool.wait_ge(s_score, t * 8 + 8)
                        pool.tensor_copy(stat[:, u, :], gT[:, ds(t * (2 * P) + u * P, P)]).then_inc(s_stat, 1)

            @block.tensor
            def _(pe):
                pe.sem_inc(s_score, 8)
                pe.sem_inc(s_pv, 2)
                for b in range(6):
                    pe.matmul(acc[:, b, 0:ROWB * (D + 1)], k.zeros[:, 0:P], k.zeros[:, 0:ROWB * (D + 1)],
                              start=True, stop=False, skip_group_check=True)

                def scores(t, u):
                    pe.wait_ge(s_stat, t * 2 + u + 1)
                    for c in range(NC):
                        pe.wait_ge(s_tanh, t * 8 + 4 * u + c + 1)
                        pe.matmul(S[:, c % 2, :], stat[:, u % 2, :], gT[:, ds(c * CH, CH)], start=True, stop=True).then_inc(s_score, 1)

                def weigh(t, u):
                    pe.wait_ge(s_p, t * 2 + u + 3)
                    for b in range(NB):
                        mm = pe.matmul(acc[:, b // ROWB, ds(b % ROWB * (D + 1), D + 1)], Pm[:, u, ds(b * P, P)],
                                       V[:, :, :].rearrange("p b f -> p (b f)")[:, ds(t * (2 * (D + 1)) + u * (D + 1), D + 1)],
                                       start=False, stop=False, skip_group_check=True)
                    mm.then_inc(s_pv, 1)

                scores(0, 0)
                with pe.Fori(0, NB // 2 - 1) as t:
                    scores(t, 1)
                    weigh(t, 0)
                    scores(t + 1, 0)
                    weigh(t, 1)
                last = NB // 2 - 1
                scores(last, 1)
                weigh(last, 0)
                weigh(last, 1)

            @block.scalar
            def _(act):
                act.sem_inc(s_tanh, 2)
                act.preload_act_table(ACT.Exp)
                with act.Fori(0, NB // 2) as t:
                    for u in range(2):
                        act.wait_ge(s_p, t * 2 + u + 1)
                        for c in range(NC):
                            act.wait_ge(s_score, t * 8 + 4 * u + c + 9)
                            act.activation(T[:, u, ds(c * CH, CH)], S[:, c % 2, :], ACT.Tanh, scale=b8[:, 0:1]).then_inc(s_tanh, 1)
                        act.wait_ge(s_tanh, t * 8 + 4 * u + NC + 2)
                        act.activation(T[:, u, :], T[:, u, :], ACT.Exp, scale=8.0).then_inc(s_exp, 1)

            @block.vector
            def _(v):
                step = k.steps.on(v)
                v.sem_inc(s_p, 2)
                with v.Fori(0, NB // 2) as t:
                    for u in range(2):
                        v.wait_ge((k.adj_even, k.adj_odd)[u], t * 16 + 16)
                        v.wait_ge(s_exp, t * 2 + u + 1)
                        v.wait_ge(s_pv, t * 2 + u + 1)
                        v.tensor_tensor(Pm[:, u, :], T[:, u, :], k.adj_rows(t * 2 + u), ALU.mult).then_inc(s_p, 1)
                v.wait_ge(s_pv, NB + 2)
                accv = acc[:, :, 0:ROWB * (D + 1)].rearrange("p b (r f) -> p b r f", f=D + 1)
                rv = rn[:, 0:15].rearrange("p (b r) -> p b r", r=ROWB)
                ov = T[:, 0, 0:15 * D].rearrange("p (b r f) -> p b r f", r=ROWB, f=D)
                step(v.reciprocal(rv, accv[:, 0:5, :, D]))
                step(v.reciprocal(rn[:, 15:16], accv[:, 5, 0:1, D]))
                step(v.tensor_tensor(ov, accv[:, 0:5, :, 0:D], rv.unsqueeze(3).broadcast_to([P, 5, ROWB, D]), ALU.mult))
                step(v.tensor_scalar(T[:, 0, 15 * D:16 * D], accv[:, 5, 0, 0:D], rn[:, 15:16], None, ALU.mult))
                step(v.tensor_tensor(k.x[:, :, :], k.x[:, :, :], h, ALU.add))
                step(v.tensor_tensor(k.x[:, :, :], k.x[:, :, :], row(bias[:, :]), ALU.add))


def layer1_gcn(k, hT, wts):
    io = k.io
    with ExitStack() as ctx:
        h1 = k.sb(ctx, "l1_h1", [P, NB, D])
        cen = k.sb(ctx, "l1_cen", [P, NB, D])
        sq = k.sb(ctx, "l1_sq", [P, NB, D])
        axT = k.sb(ctx, "l1_axT", [P, N])
        gw = k.sb(ctx, "l1_gcn_w", [D, D])
        gb = k.sb(ctx, "l1_gcn_b", [P, D])
        mean = k.sb(ctx, "l1_mean", [P, NB])
        var = k.sb(ctx, "l1_var", [P, NB])
        std = k.sb(ctx, "l1_std", [P, NB])
        s_wl = k.sem("l1_all_weights_loaded")
        s_w, s_var, s_std, s_h, s_ax, s_axT, s_aw, s_n, s_tr, s_hT = (
            k.sem("l1_" + n) for n in ("w_loaded", "var", "std", "h1_ready", "ax_product", "axT_ready", "axw_product", "normed", "turned", "hT_ready"))
        with k.block() as block, ExitStack() as pctx:
            ax = k.ps(pctx, "l1_ax", [P, 4, CH])
            aw = k.ps(pctx, "l1_aw", [P, 4, CH])

            @block.sync
            def _(sp):
                sp.dma_start(gw[:, :], io["L1_gcn_w"]).then_inc(s_w, 16)
                sp.dma_start(gb[:, :], io["L1_gcn_b"].partition_broadcast(P)).then_inc(s_w, 16)
                for t, n in wts:
                    sp.dma_start(t, io[n]).then_inc(s_wl, 16)
                sp.wait_ge(s_w, 32)
                sp.wait_ge(s_wl, 16 * len(wts))

            @block.vector
            def _(v):
                step = k.steps.on(v)
                center_and_sum(v, step, k.x[:, :, :], cen[:, :, :], sq[:, :, :], mean[:, :], var[:, :])
                v.sem_inc(s_var, 1)
                v.wait_ge(s_std, 1)
                step(v.reciprocal(var[:, :], std[:, :]))
                v.scalar_tensor_tensor(h1[:, :, :], cen[:, :, :], 0.0, per_block(var[:, :]), ALU.max, ALU.mult).then_inc(s_h, 1)
                v.wait_ge(s_h, 1)
                v.wait_ge(s_w, 32)
                for c in range(4):
                    v.wait_ge(s_aw, 4 * c + 4)
                    v.tensor_tensor(sq[:, 4 * c:4 * c + 4, :], aw[:, c, :].rearrange("p (b f) -> p b f", f=D), row(gb[:, :], 4), ALU.add).then_inc(s_h, 1)
                v.wait_ge(s_h, 5)
                step(v.tensor_scalar(sq[:, :, :], sq[:, :, :], 0.0, None, ALU.max))
                center_and_sum(v, step, sq[:, :, :], cen[:, :, :], h1[:, :, :], mean[:, :], var[:, :])
                v.sem_inc(s_var, 1)
                v.wait_ge(s_std, 2)
                step(v.reciprocal(var[:, :], std[:, :]))
                v.tensor_tensor(cen[:, :, :], cen[:, :, :], per_block(var[:, :]), ALU.mult).then_inc(s_n, 1)

            @block.scalar
            def _(act):
                for r in range(2):
                    act.wait_ge(s_var, r + 1)
                    act.activation(std[:, :], var[:, :], ACT.Sqrt, bias=k.eps[:, :], scale=1.0 / D).then_inc(s_std, 1)
                    if r == 0:
                        for c in range(NC):
                            act.wait_ge(s_ax, c + 1)
                            act.activation(axT[:, ds(c * CH, CH)], ax[:, c, :], ACT.Copy).then_inc(s_axT, 1)
                act.wait_ge(s_wl, 16 * len(wts))
                for c in range(4):
                    act.wait_ge(s_tr, 4 * c + 4)
                    act.activation(hT[:, ds(c * CH, CH)], ax[:, c, :], ACT.Identity, bias=k.l1["ln_b"][:, :], scale=k.l1["ln_g"][:, :]).then_inc(s_hT, 1)

            @block.tensor
            def _(pe):
                pe.wait_ge(s_h, 1)
                for r in range(NB // 2):
                    pe.wait_ge(k.adj_even, 16 * (r + 1))
                    pe.wait_ge(k.adj_odd, 16 * (r + 1))
                for c in range(NC):
                    for jb in range(NB):
                        mm = pe.matmul(ax[:, c, :], h1[:, jb, :], k.adj_rows(jb, c * CH, CH), start=jb == 0, stop=jb == NB - 1)
                    mm.then_inc(s_ax, 1)
                pe.wait_ge(s_w, 32)
                for b in range(NB):
                    pe.wait_ge(s_axT, b // 4 + 1)
                    pe.matmul(aw[:, b // 4, ds(b % 4 * P, P)], axT[:, ds(b * P, P)], gw[:, :], start=True, stop=True).then_inc(s_aw, 1)
                pe.wait_ge(s_n, 1)
                for b in range(NB):
                    pe.transpose(ax[:, b // 4, ds(b % 4 * P, P)], cen[:, b, :], k.ident[:, :]).then_inc(s_tr, 1)


def layer1_ssm(k, hT):
    io, w = k.io, k.l1
    with ExitStack() as ctx:
        t2 = lambda n, dt=F32: k.sb(ctx, "l1_" + n, [P, CB, CH], dt)
        xin = k.sb(ctx, "l1_xin", [P, CB, CH + KC - 1])
        u, sz, dt, du = t2("u"), t2("sz"), t2("dt"), t2("du")
        dA, dBu, hs, hC = t2("dA"), t2("dBu"), t2("hs"), t2("hC")
        bc = k.sb(ctx, "l1_bc", [P, 2, 2, CH])
        dbc = k.sb(ctx, "l1_dbc", [XP, CH])
        state = k.sb(ctx, "l1_state", [P, CB * DS])
        negA = k.sb(ctx, "l1_negA", [P, CB * DS])
        bc_dram = k.nc.dram_tensor("l1_bc_rows", (2 * DS, N), F32, kind="Internal").ap()
        bc_src = bc_dram.rearrange("(a n) t -> a (n t)", a=2)

        names = ("init", "xz_product", "xin_ready", "sz_ready", "conv", "u_ready", "dbc_product", "dbc_ready", "dt_product",
                 "softplus_in", "softplus_e", "softplus_l", "dt_ready", "bc_stored", "bc_even", "bc_odd", "dA_ready", "dBu_ready",
                 "scanned", "hC_ready", "y_summed", "yT_ready", "out_product", "out_added", "negA_exp", "du_free")
        (s_init, s_xz, s_xin, s_sz, s_conv, s_u, s_dbcp, s_dbc, s_dtp, s_spin, s_spe, s_spl, s_dt, s_bcst, s_bce, s_bco, s_dA, s_dBu,
         s_scan, s_hC, s_y, s_yT, s_op, s_oa, s_nA, s_duf) = (k.sem("l1_" + n) for n in names)
        s_bc = (s_bce, s_bco)
        PAIRS = DS // 2
        with k.block() as block, ExitStack() as pctx:
            xp = k.ps(pctx, "l1_xp", [P, CB, CH])
            zp = k.ps(pctx, "l1_zp", [P, CB, CH])
            yp = k.ps(pctx, "l1_yp", [P, CB, CH])
            dp = k.ps(pctx, "l1_dp", [P, CH])
            op = k.ps(pctx, "l1_op", [P, CH])

            @block.sync
            def _(sp):
                sp.sem_inc(s_hC, 4)
                with sp.Fori(0, NC) as q:
                    sp.wait_ge(s_dbc, q + 1)
                    sp.dma_start(bc_dram[:, ds(q * CH, CH)], dbc[DTR:XP, :]).then_inc(s_bcst, 16)
                    with sp.Fori(0, PAIRS) as r:
                        for e in range(2):
                            if e == 0:
                                sp.wait_ge(s_bcst, q * 16 + 16)
                            sp.wait_ge(s_hC, q * (2 * DS) + r * 4 + 2 * e + 2)
                            sp.dma_start(bc[:, e, :, :], bc_src[:, ds((r * 2 + e) * N + q * CH, CH)].partition_broadcast(P)).then_inc(s_bc[e], 16)

            @block.gpsimd
            def _(pool):
                pool.memset(state[:, :], 0.0)
                pool.memset(xin[:, :, 0:KC - 1], 0.0).then_inc(s_init, 1)
                with pool.Fori(0, NC) as q:
                    with pool.Fori(0, PAIRS) as r:
                        for e in range(2):
                            pool.wait_ge(s_dt, q + 1)
                            pool.wait_ge(s_bc[e], q * (16 * PAIRS) + r * 16 + 16)
                            for cb in range(CB):
                                pool.wait_ge(s_scan, q * (2 * DS) + r * 4 + 2 * e + cb + 1)
                                pool.tensor_tensor(dBu[:, cb, :], du[:, cb, :], bc[:, e, 0, :], ALU.mult).then_inc(s_dBu, 1)

            @block.tensor
            def _(pe):
                pe.sem_inc(s_y, 2)
                with pe.Fori(0, NC) as q:
                    pe.wait_ge(s_duf, q + 1)
                    for cb in range(CB):
                        pe.matmul(xp[:, cb, :], w["w_in"][:, ds(cb * P, P)], hT[:, ds(q * CH, CH)], start=True, stop=True).then_inc(s_xz, 1)
                    for cb in range(CB):
                        pe.matmul(zp[:, cb, :], w["w_in"][:, ds(DI + cb * P, P)], hT[:, ds(q * CH, CH)], start=True, stop=True).then_inc(s_xz, 1)
                        pe.matmul(yp[:, cb, :], k.zeros[:, 0:P], k.zeros[:, :], start=True, stop=False, skip_group_check=True)
                    pe.wait_ge(s_u, q * 2 + 2)
                    for cb in range(CB):
                        mm = pe.matmul(dp[0:XP, :], w["w_xp"][:, cb, :], u[:, cb, :], start=cb == 0, stop=cb == 1)
                    mm.then_inc(s_dbcp, 1)
                    pe.wait_ge(s_dbc, q + 1)
                    for cb in range(CB):
                        pe.matmul(xp[:, cb, :], w["w_dt"][:, ds(cb * P, P)], dbc[0:DTR, :], start=True, stop=True).then_inc(s_dtp, 1)
                    with pe.Fori(0, DS) as n:
                        for cb in range(CB):
                            pe.wait_ge(s_hC, q * (2 * DS) + n * 2 + cb + 5)
                            pe.matmul(yp[:, cb, :], k.ident[:, :], hC[:, cb, :], start=False, stop=False, skip_group_check=True).then_inc(s_y, 1)
                    pe.wait_ge(s_yT, q * 2 + 2)
                    for b in range(CH // P):
                        for cb in range(CB):
                            mm = pe.matmul(op[:, ds(b * P, P)], hC[:, cb, ds(b * P, P)], w["w_out"][:, cb, :], start=cb == 0, stop=cb == 1)
                    mm.then_inc(s_op, 1)

            @block.scalar
            def _(act):
                act.activation(negA[:, :], w["A_log"][:, :], ACT.Exp).then_inc(s_nA, 1)
                with act.Fori(0, NC) as q:
                    for cb in range(CB):
                        act.wait_ge(s_xz, q * 4 + cb + 1)
                        act.activation(xin[:, cb, KC - 1:], xp[:, cb, :], ACT.Copy).then_inc(s_xin, 1)
                    for cb in range(CB):
                        act.wait_ge(s_conv, q * 2 + cb + 1)
                        act.activation(u[:, cb, :], hs[:, cb, :], ACT.Silu, bias=w["conv_b"][:, cb:cb + 1]).then_inc(s_u, 1)
                    for cb in range(CB):
                        act.wait_ge(s_xz, q * 4 + cb + 3)
                        act.activation(sz[:, cb, :], zp[:, cb, :], ACT.Silu).then_inc(s_sz, 1)
                    act.wait_ge(s_dbcp, q + 1)
                    act.activation(dbc[:, :], dp[0:XP, :], ACT.Copy).then_inc(s_dbc, 1)
                    act.wait_ge(s_spin, q * 2 + 2)
                    for cb in range(CB):
                        act.activation(hC[:, cb, :], dBu[:, cb, :], ACT.Exp).then_inc(s_spe, 1)
                    act.wait_ge(s_spe, q * 2 + 2)
                    for cb in range(CB):
                        act.activation(du[:, cb, :], hC[:, cb, :], ACT.Ln, bias=1.0).then_inc(s_spl, 1)
                    act.wait_ge(s_dt, q + 1)
                    with act.Fori(0, DS) as n:
                        for cb in range(CB):
                            act.wait_ge(s_scan, q * (2 * DS) + n * 2 + cb + 1)
                            act.activation(dA[:, cb, :], dt[:, cb, :], ACT.Exp, scale=negA[:, ds(n + cb * DS, 1)]).then_inc(s_dA, 1)

            @block.vector
            def _(v):
                step = k.steps.on(v)
                v.wait_ge(s_nA, 1)
                step(v.tensor_scalar(negA[:, :], negA[:, :], -1.0, None, ALU.mult))
                v.sem_inc(s_duf, 1)
                v.sem_inc(s_scan, 2)
                v.wait_ge(s_init, 1)
                first, PER = step.n, 22
                with v.Fori(0, NC) as q:
                    step.begin(q, PER)
                    cv = hs
                    for kk in range(KC):
                        for cb in range(CB):
                            if kk == 0:
                                v.wait_ge(s_xin, q * 2 + cb + 1)
                                ins = v.tensor_scalar(cv[:, cb, :], xin[:, cb, 0:CH], w["conv_w"][:, cb, 0:1], None, ALU.mult)
                            else:
                                ins = v.scalar_tensor_tensor(cv[:, cb, :], xin[:, cb, kk:kk + CH], w["conv_w"][:, cb, kk:kk + 1], cv[:, cb, :], ALU.mult, ALU.add)
                            step(ins)
                            if kk == KC - 1:
                                v.sem_inc(s_conv, 1)
                    for cb in range(CB):
                        step(v.tensor_copy(xin[:, cb, 0:KC - 1], xin[:, cb, CH:CH + KC - 1]))
                    for cb in range(CB):
                        v.wait_ge(s_dtp, q * 2 + cb + 1)
                        step(v.tensor_scalar(dt[:, cb, :], xp[:, cb, :], w["b_dt"][:, cb:cb + 1], None, ALU.add))
                        v.scalar_tensor_tensor(dBu[:, cb, :], dt[:, cb, :], -1.0, dt[:, cb, :], ALU.mult, ALU.min).then_inc(s_spin, 1)
                    for cb in range(CB):
                        v.wait_ge(s_spe, q * 2 + cb + 1)
                        step(v.tensor_scalar(hs[:, cb, :], hC[:, cb, :], 1.0, None, ALU.add))
                        step(v.scalar_tensor_tensor(hs[:, cb, :], hs[:, cb, :], -1.0, hC[:, cb, :], ALU.add, ALU.subtract))
                        v.wait_ge(s_spl, q * 2 + cb + 1)
                        step(v.scalar_tensor_tensor(dt[:, cb, :], dt[:, cb, :], 0.0, du[:, cb, :], ALU.max, ALU.add))
                        step(v.tensor_tensor(dt[:, cb, :], dt[:, cb, :], hs[:, cb, :], ALU.subtract))
                        if cb == 0:
                            step(v.tensor_tensor(du[:, cb, :], dt[:, cb, :], u[:, cb, :], ALU.mult))
                        else:
                            step(v.tensor_tensor(du[:, cb, :], dt[:, cb, :], u[:, cb, :], ALU.mult))
                    step.end(NC, first, PER)
                    v.sem_inc(s_dt, 1)
                    with v.Fori(0, PAIRS) as r:
                        for e in range(2):
                            base = q * (2 * DS) + r * 4 + 2 * e
                            for cb in range(CB):
                                at = state[:, ds(r * 2 + e + cb * DS, 1)]
                                v.wait_ge(s_dA, base + cb + 1)
                                v.wait_ge(s_dBu, base + cb + 1)
                                v.tensor_tensor_scan(hs[:, cb, :], dA[:, cb, :], dBu[:, cb, :], at, ALU.mult, ALU.add).then_inc(s_scan, 1)
                            v.wait_ge(s_bc[e], q * (16 * PAIRS) + r * 16 + 16)
                            for cb in range(CB):
                                at = state[:, ds(r * 2 + e + cb * DS, 1)]
                                v.wait_ge(s_scan, base + cb + 3)
                                v.wait_ge(s_y, base + cb + 1)
                                v.tensor_tensor(hC[:, cb, :], hs[:, cb, :], bc[:, e, 1, :], ALU.mult).then_inc(s_hC, 1)
                                v.tensor_copy(at, hs[:, cb, CH - 1:CH]).then_inc(s_oa, 1)
                            v.wait_ge(s_oa, base + 2)
                            v.wait_ge(s_hC, base + 6)
                    for cb in range(CB):
                        v.wait_ge(s_y, q * (2 * DS) + 2 * DS + 2)
                        v.scalar_tensor_tensor(hs[:, cb, :], u[:, cb, :], w["D"][:, cb:cb + 1], yp[:, cb, :], ALU.mult, ALU.add).then_inc(s_init, 1)
                        v.wait_ge(s_init, q * 2 + cb + 2)
                        v.wait_ge(s_sz, q * 2 + cb + 1)
                        v.tensor_tensor(hC[:, cb, :], hs[:, cb, :], sz[:, cb, :], ALU.mult).then_inc(s_yT, 1)
                    v.wait_ge(s_op, q + 1)
                    xq = k.x[:, :, :].rearrange("p b f -> p (b f)")[:, ds(q * CH, CH)]
                    v.tensor_tensor(xq, xq, op[:, :], ALU.add).then_inc(s_duf, 1)


def layer1(k):
    with ExitStack() as ctx:
        w = k.l1 = {}
        for n, shape in (("w_in", [D, 2 * DI]), ("w_xp", [P, CB, XP]), ("w_dt", [DTR, DI]), ("w_out", [P, CB, D]), ("A_log", [P, CB * DS]),
                         ("conv_w", [P, CB, KC]), ("conv_b", [P, CB]), ("b_dt", [P, CB]), ("D", [P, CB]), ("ln_g", [P, 1]), ("ln_b", [P, 1])):
            w[n] = k.sb(ctx, "l1w_" + n, shape)
        hT = k.sb(ctx, "l1_hT", [P, N])
        layer1_gcn(k, hT, [(w[n][tuple(slice(None) for _ in w[n].shape)], "L1_" + n) for n in w])
        layer1_ssm(k, hT)


def load_weights(k, ctx, sp_list):
    w = {}
    for n, shape in sp_list:
        w[n] = k.sb(ctx, "w_" + n, shape)
    return w


def normed_and_turned(k, tag, w, h, hT, work):
    with ExitStack() as ctx:
        mean, var, std = (k.sb(ctx, tag + n, [P, NB]) for n in ("mean", "var", "std"))
        s_w, s_var, s_std, s_h, s_tr, s_hT = (k.sem(tag + n) for n in ("weights", "var", "std", "h", "turned", "hT"))
        with k.block() as block, ExitStack() as pctx:
            tr = k.ps(pctx, tag + "tr", [P, 4, CH])

            @block.sync
            def _(sp):
                for n in w:
                    t = w[n]
                    sp.dma_start(t[tuple(slice(None) for _ in t.shape)], k.io[n] if len(k.io[n].shape) > 1 else k.io[n].partition_broadcast(P)).then_inc(s_w, 16)
                sp.wait_ge(s_w, 16 * len(w))

            @block.vector
            def _(v):
                step = k.steps.on(v)
                center_and_sum(v, step, k.x[:, :, :], h, work, mean[:, :], var[:, :])
                v.sem_inc(s_var, 1)
                v.wait_ge(s_std, 1)
                step(v.reciprocal(var[:, :], std[:, :]))
                v.scalar_tensor_tensor(h, h, 0.0, per_block(var[:, :]), ALU.max, ALU.mult).then_inc(s_h, 1)

            @block.scalar
            def _(act):
                act.wait_ge(s_var, 1)
                act.activation(std[:, :], var[:, :], ACT.Sqrt, bias=k.eps[:, :], scale=1.0 / D).then_inc(s_std, 1)
                for c in range(NC):
                    act.wait_ge(s_tr, 4 * c + 4)
                    act.activation(hT[:, ds(c * CH, CH)], tr[:, c, :], ACT.Copy).then_inc(s_hT, 1)

            @block.tensor
            def _(pe):
                pe.wait_ge(s_h, 1)
                for b in range(NB):
                    pe.transpose(tr[:, b // 4, ds(b % 4 * P, P)], h[:, b, :], k.ident[:, :]).then_inc(s_tr, 1)


def split_bf16(step, v, src, parts, rest):
    step(v.tensor_copy(parts[0], src))
    step(v.tensor_tensor(rest, src, parts[0], ALU.subtract))
    step(v.tensor_copy(parts[1], rest))
    step(v.tensor_tensor(rest, rest, parts[1], ALU.subtract))
    step(v.tensor_copy(parts[2], rest))


HALF = N // 2
UNITS = 2 * NB
VW = HD + 1
NR = 4 * H2


def layer2(k):
    with ExitStack() as ctx:
        w = load_weights(k, ctx, [("L2_WT", [D, D]), ("L2_src", [D, 1]), ("L2_dst", [D, 1]), ("head_mask", [D, H2]), ("L2_eW", [P, H2]), ("L2_eb", [P, H2]),
                                  ("L2_fuse_WT", [D, D]), ("L2_fuse_b", [P, D]), ("L2_ln_g", [P, D]), ("L2_ln_b", [P, D])])
        V = k.sb(ctx, "l2_V", [P, NB, H2, VW])
        ad = k.sb(ctx, "l2_ad", [P, NB, H2])
        srcn = k.sb(ctx, "l2_as", [P, NB, H2])
        rows = k.sb(ctx, "l2_rows", [P, N], BF16)
        big = k.sb(ctx, "l2_big", [P, P], BF16)
        layer2_project(k, w, V, ad, srcn)
        layer2_maxima(k, w, ad, srcn, rows, big)
        hout = k.sb(ctx, "l2_hout", [P, NB, D])
        layer2_attend(k, w, V, ad, rows, big, hout)
        layer2_fuse(k, w, hout)


def layer2_project(k, w, V, ad, srcn):
    with ExitStack() as ctx:
        h = k.sb(ctx, "l2_h", [P, NB, D])
        hT = k.sb(ctx, "l2_hT", [P, N])
        h2T = k.sb(ctx, "l2_h2T", [P, N])
        att = k.sb(ctx, "l2_att", [D, 2 * H2])
        normed_and_turned(k, "l2_", w, h[:, :, :], hT, h2T[:, :].rearrange("p (b f) -> p b f", f=D))
        s_att, s_h2T, s_h2Tc, s_v, s_vc, s_a, s_a2 = (k.sem("l2p_" + n) for n in ("att", "h2T_product", "h2T", "V_product", "V", "logit_terms", "ones"))
        with k.block() as block, ExitStack() as pctx:
            tp = k.ps(pctx, "l2_tp", [P, 4, CH])
            vp = k.ps(pctx, "l2_vp", [P, 3, CH])
            ap = k.ps(pctx, "l2_ap", [P, NB, 2 * H2])

            @block.tensor
            def _(pe):
                for c in range(NC):
                    pe.matmul(tp[:, c, :], w["L2_WT"][:, :], hT[:, ds(c * CH, CH)], start=True, stop=True).then_inc(s_h2T, 1)
                for b in range(NB):
                    if b >= 12 and b % 4 == 0:
                        pe.wait_ge(s_vc, b // 4 - 2)
                    pe.matmul(vp[:, b // 4 % 3, ds(b % 4 * P, P)], hT[:, ds(b * P, P)], w["L2_WT"][:, :], start=True, stop=True).then_inc(s_v, 1)
                pe.wait_ge(s_att, 2)
                for b in range(NB):
                    pe.wait_ge(s_h2Tc, b // 4 + 1)
                    pe.matmul(ap[:, b, :], h2T[:, ds(b * P, P)], att[:, :], start=True, stop=True).then_inc(s_a, 1)

            @block.scalar
            def _(act):
                for c in range(NC):
                    act.wait_ge(s_h2T, c + 1)
                    act.activation(h2T[:, ds(c * CH, CH)], tp[:, c, :], ACT.Copy).then_inc(s_h2Tc, 1)

            @block.vector
            def _(v):
                for n, name in enumerate(("L2_src", "L2_dst")):
                    v.tensor_scalar(att[:, ds(n * H2, H2)], w["head_mask"][:, :], w[name][:, 0:1], None, ALU.mult).then_inc(s_att, 1)
                v.memset(V[:, :, :, HD:VW], 1.0)
                for c in range(4):
                    v.wait_ge(s_v, 4 * c + 4)
                    v.tensor_copy(V[:, 4 * c:4 * c + 4, :, 0:HD], vp[:, c % 3, :].rearrange("p (b h d) -> p b h d", h=H2, d=HD)).then_inc(s_vc, 1)
                v.wait_ge(s_a, NB)
                v.tensor_copy(srcn[:, :, :], ap[:, :, 0:H2])
                v.tensor_copy(ad[:, :, :], ap[:, :, H2:])


def layer2_maxima(k, w, ad, srcn, rows, big):
    with ExitStack() as ctx:
        R = k.sb(ctx, "l2_R", [P, H2, N], BF16)
        t = k.sb(ctx, "l2_t", [P, 4, N], BF16)
        BT = k.sb(ctx, "l2_BT", [P, N], BF16)
        mx = k.sb(ctx, "l2_mx", [P, H2, NB])
        rn = BT[:, :].rearrange("p (b r) -> p b r", r=P)
        rest = k.sb(ctx, "l2_rest", [P, NB, H2])
        s_t, s_bt, s_m, s_r = (k.sem("l2m_" + n) for n in ("logits", "mask", "masked", "maxed"))
        s_tr, s_red, s_rows, s_rt = (k.sem("l2m_" + n) for n in ("turned", "reduced", "rows", "rows_turned"))
        with k.block() as block, ExitStack() as pctx:
            rt = k.ps(pctx, "l2_rt", [P, 2, N], BF16)
            ro = k.ps(pctx, "l2_ro", [P, N], BF16)

            @block.scalar
            def _(act):
                with act.Fori(0, NB) as jb:
                    for h in range(H2):
                        act.wait_ge(s_r, jb * H2 + h + 1)
                        act.activation(t[:, h % 4, :], k.adj_rows(jb), ACT.Identity, scale=w["L2_eW"][:, h:h + 1],
                                       bias=ad[:, :, :].rearrange("p b h -> p (b h)")[:, ds(jb * H2 + h, 1)]).then_inc(s_t, 1)

            @block.vector
            def _(v):
                step = k.steps.on(v)
                step(v.memset(R[:, :, :], -BIG))
                v.tensor_scalar(big[:, :], k.ident[:, :], -BIG, None, ALU.mult)
                v.sem_inc(s_r, 4)
                with v.Fori(0, NB) as jb:
                    v.tensor_scalar(BT[:, :], k.adj_rows(jb), 0.0, -BIG, ALU.is_le, ALU.mult).then_inc(s_bt, 1)
                    v.wait_ge(s_bt, jb + 1)
                    for h0 in range(0, H2, 2):
                        for h in (h0, h0 + 1):
                            v.wait_ge(s_t, jb * H2 + h + 1)
                            v.tensor_tensor(t[:, h % 4, :], t[:, h % 4, :], BT[:, :], ALU.add).then_inc(s_m, 1)
                        for h in (h0, h0 + 1):
                            v.wait_ge(s_m, jb * H2 + h + 1)
                            v.tensor_tensor(R[:, h, :], R[:, h, :], t[:, h % 4, :], ALU.max).then_inc(s_r, 1)
                    v.wait_ge(s_r, jb * H2 + H2 + 4)
                for h in range(H2):
                    v.wait_ge(s_tr, h + 1)
                    step(v.tensor_reduce(mx[:, h, :], rt[:, h % 2, :].rearrange("p (b q) -> p b q", q=P), AX_X, ALU.max))
                    v.sem_inc(s_red, 1)
                mxv = mx[:, :, :].rearrange("p h b -> p b h")
                step(v.tensor_tensor(rest[:, :, :], srcn[:, :, :], mxv, ALU.add))
                step(v.tensor_tensor(rest[:, :, :], rest[:, :, :], row(w["L2_eb"][:, :]), ALU.add))
                step(v.memset(rn, 0.0))
                step(v.scalar_tensor_tensor(rest[:, :, :], rest[:, :, :], 0.2, rest[:, :, :], ALU.mult, ALU.max))
                step(v.tensor_scalar(rn[:, :, 0:H2], rest[:, :, :], -1.0, None, ALU.mult))
                split_bf16(step, v, srcn[:, :, :], [rn[:, :, ds(H2 * (n + 1), H2)] for n in range(3)], rest[:, :, :])
                v.sem_inc(s_rows, 1)
                step(v.tensor_tensor(ad[:, :, :], ad[:, :, :], row(w["L2_eb"][:, :]), ALU.add))
                v.wait_ge(s_rt, NB)
                v.tensor_copy(rows[:, :], ro[:, :])

            @block.tensor
            def _(pe):
                pe.wait_ge(s_r, NB * H2 + 4)
                for h in range(H2):
                    if h >= 2:
                        pe.wait_ge(s_red, h - 1)
                    for b in range(NB):
                        mm = pe.transpose(rt[:, h % 2, ds(b * P, P)], R[:, h, ds(b * P, P)], k.ident_b[:, :])
                    mm.then_inc(s_tr, 1)
                pe.wait_ge(s_rows, 1)
                for b in range(NB):
                    pe.transpose(ro[:, ds(b * P, P)], rn[:, b, :], k.ident_b[:, :]).then_inc(s_rt, 1)


def layer2_attend(k, w, V, ad, rows, big, hout):
    with ExitStack() as ctx:
        AS = k.sb(ctx, "l2_AS", [P, N])
        nm = k.sb(ctx, "l2_nm", [P, 2, N], BF16)
        U = k.sb(ctx, "l2_U", [P, 4, HALF])
        Rl = k.sb(ctx, "l2_relu", [P, 2, HALF])
        ad8 = k.sb(ctx, "l2_ad8", [P, NB * H2])
        rden = k.sb(ctx, "l2_rden", [P, NB])
        sel = k.sb(ctx, "l2_sel", [P, 2, H2 * P], BF16)
        selr = U[0:NR, 0:2, :].rearrange("p a i -> p (a i)")
        s_sum = k.sem("l2a_leaky_sum")
        s_sel, s_selc = k.sem("l2a_sel_loaded"), k.sem("l2a_sel_ready")
        Vf = V[:, :, :, :].rearrange("p b h d -> p (b h d)")
        adf = ad[:, :, :].rearrange("p b h -> p (b h)")
        names = ("as_product", "as_ready", "logits", "leaky", "shifted", "exp", "pv", "shift", "mask", "head_summed", "rden", "head_out")
        s_asp, s_as, s_u, s_pre, s_add, s_e, s_pv, s_ps, s_nm, s_hs, s_rd, s_ho = (k.sem("l2a_" + n) for n in names)
        with k.block() as block, ExitStack() as pctx:
            ps = k.ps(pctx, "l2_ps", [P, 2, 2, CH])
            acc = k.ps(pctx, "l2_acc", [P, CH])
            asp = k.ps(pctx, "l2_asp", [P, 2, CH])

            @block.sync
            def _(sp):
                sp.dma_start(selr, k.io["sel_rows"].rearrange("r a n -> r (a n)")).then_inc(s_sel, 16)
                sp.wait_ge(s_sel, 16)

            @block.gpsimd
            def _(pool):
                with pool.Fori(0, H2) as h:
                    for jb in range(NB):
                        pool.wait_ge(s_ps, h * UNITS + 2 * jb + 2)
                        k.carry(pool, k.pool_waits)
                        pool.tensor_scalar(nm[:, jb % 2, :], k.adj_rows(jb), 0.0, None, ALU.is_le).then_inc(s_nm, 1)

            @block.tensor
            def _(pe):
                pe.wait_ge(s_selc, 4)
                pe.sem_inc(s_ps, 4)
                pe.sem_inc(s_pv, 4)

                def shift(h, t, u):
                    pe.wait_ge(s_nm, h * NB + t * 2 + u // 2 + 1)
                    joined = u % 2 == 0
                    pe.wait_ge(s_add, h * UNITS + t * 4 + u + 1)
                    for q in range(2):
                        i0 = u % 2 * HALF + q * CH
                        pe.matmul(ps[:, u % 2, q, :], sel[:, 0, ds(h * P, P)], rows[:, ds(i0, CH)], start=True, stop=False)
                        mm = pe.matmul(ps[:, u % 2, q, :], big[:, :], nm[:, u // 2 % 2, ds(i0, CH)], start=False, stop=not joined)
                    if joined:
                        pe.wait_ge(s_pre, h * UNITS + t * 4 + u + 1)
                        for q in range(2):
                            mm = pe.matmul(ps[:, u % 2, q, :], k.ident[:, :], Rl[:, u % 2, ds(q * CH, CH)], start=False, stop=True)
                    mm.then_inc(s_ps, 1)

                def weigh(h, t, u):
                    pe.wait_ge(s_e, h * UNITS + t * 4 + u + 1)
                    for b in range(NB // 2):
                        ib = u % 2 * (NB // 2) + b
                        mm = pe.matmul(acc[:, ds(ib * VW, VW)], U[:, u % 4, ds(b * P, P)],
                                       Vf[:, ds(t * (2 * H2 * VW) + u // 2 * (H2 * VW) + h * VW, VW)], start=False, stop=False, skip_group_check=True)
                    mm.then_inc(s_pv, 1)

                with pe.Fori(0, H2) as h:
                    for c in range(NC):
                        pe.wait_ge(s_as, h * NC + c + 1)
                        pe.matmul(asp[:, c % 2, :], sel[:, 1, ds(h * P, P)], rows[:, ds(c * CH, CH)], start=True, stop=True).then_inc(s_asp, 1)
                    pe.wait_ge(s_ho, h + 1)
                    pe.matmul(acc[:, 0:NB * VW], k.zeros[:, 0:P], k.zeros[:, 0:NB * VW], start=True, stop=False, skip_group_check=True)
                    shift(h, 0, 0)
                    with pe.Fori(0, UNITS // 4 - 1) as t:
                        for u in range(4):
                            if u < 3:
                                shift(h, t, u + 1)
                            else:
                                shift(h, t + 1, 0)
                            weigh(h, t, u)
                    last = UNITS // 4 - 1
                    for u in range(4):
                        if u < 3:
                            shift(h, last, u + 1)
                        weigh(h, last, u)
                    pe.sem_inc(s_hs, 1)

            @block.scalar
            def _(act):
                act.preload_act_table(ACT.Exp)
                act.sem_inc(s_as, 2)

                def leaky(h, t, u):
                    act.wait_ge(s_u, h * UNITS + t * 4 + u + 2)
                    act.wait_ge(s_add, h * UNITS + t * 4 + u + 1)
                    k.carry(act, k.act_waits)
                    act.activation(Rl[:, u % 2, :], U[:, u % 4, :], ACT.Relu, scale=0.8, bias=ad8[:, ds(t * (2 * H2) + u // 2 * H2 + h, 1)]).then_inc(s_pre, 1)

                def exps(h, t, u):
                    act.wait_ge(s_add, h * UNITS + t * 4 + u + 3)
                    k.carry(act, k.act_waits)
                    act.activation(U[:, u, :], U[:, u, :], ACT.Exp, bias=adf[:, ds(t * (2 * H2) + u // 2 * H2 + h, 1)]).then_inc(s_e, 1)

                with act.Fori(0, H2) as h:
                    act.wait_ge(s_u, h * UNITS + 1)
                    for c in range(NC):
                        act.wait_ge(s_asp, h * NC + c + 1)
                        act.activation(AS[:, ds(c * CH, CH)], asp[:, c % 2, :], ACT.Copy).then_inc(s_as, 1)
                    leaky(h, 0, 0)
                    with act.Fori(0, UNITS // 4 - 1) as t:
                        for u in range(4):
                            if u < 3:
                                leaky(h, t, u + 1)
                            else:
                                leaky(h, t + 1, 0)
                            exps(h, t, u)
                    last = UNITS // 4 - 1
                    for u in range(4):
                        if u < 3:
                            leaky(h, last, u + 1)
                        exps(h, last, u)

            @block.vector
            def _(v):
                v.memset(sel[:, :, :], 0.0).then_inc(s_selc, 1)
                v.wait_ge(s_selc, 1)
                v.wait_ge(s_sel, 16)
                v.tensor_copy(sel[0:NR, :, :].rearrange("r a n -> r (a n)"), selr).then_inc(s_selc, 1)
                v.tensor_scalar(ad8[:, :], adf, 0.8, None, ALU.mult).then_inc(s_selc, 1)
                v.wait_ge(s_selc, 3)
                v.tensor_scalar(adf, adf, 0.2, None, ALU.mult).then_inc(s_selc, 1)
                v.wait_ge(s_selc, 4)
                v.sem_inc(s_u, 1)
                v.sem_inc(s_add, 2)
                v.sem_inc(s_ho, 1)

                def logits(h, t, u):
                    v.wait_ge(s_pv, h * UNITS + t * 4 + u + 1)
                    v.scalar_tensor_tensor(U[:, u % 4, :], k.adjT[:, ds(t * (2 * N) + u // 2 * N + u % 2 * HALF, HALF)],
                                           w["L2_eW"][:, ds(h, 1)], AS[:, ds(u % 2 * HALF, HALF)], ALU.mult, ALU.add).then_inc(s_u, 1)

                def shifted(h, t, u):
                    v.wait_ge(s_pre, h * UNITS + t * 4 + u + 1)
                    shift = ps[:, u % 2, :, :].rearrange("p a c -> p (a c)")
                    if u % 2 == 0:
                        v.wait_ge(s_ps, h * UNITS + t * 4 + u + 5)
                        v.scalar_tensor_tensor(U[:, u, :], U[:, u, :], 0.2, shift, ALU.mult, ALU.add).then_inc(s_add, 1)
                    else:
                        v.scalar_tensor_tensor(U[:, u, :], U[:, u, :], 0.2, Rl[:, u % 2, :], ALU.mult, ALU.add).then_inc(s_sum, 1)
                        v.wait_ge(s_ps, h * UNITS + t * 4 + u + 5)
                        v.wait_ge(s_sum, h * (UNITS // 2) + t * 2 + u // 2 + 1)
                        v.tensor_tensor(U[:, u, :], U[:, u, :], shift, ALU.add).then_inc(s_add, 1)

                with v.Fori(0, H2) as h:
                    v.wait_ge(s_as, h * NC + NC + 2)
                    logits(h, 0, 0)
                    with v.Fori(0, UNITS // 4 - 1) as t:
                        for u in range(4):
                            if u < 3:
                                logits(h, t, u + 1)
                            else:
                                logits(h, t + 1, 0)
                            shifted(h, t, u)
                    last = UNITS // 4 - 1
                    for u in range(4):
                        if u < 3:
                            logits(h, last, u + 1)
                        shifted(h, last, u)
                    v.wait_ge(s_pv, h * UNITS + UNITS + 4)
                    av = acc[:, 0:NB * VW].rearrange("p (b d) -> p b d", d=VW)
                    v.reciprocal(rden[:, :], av[:, :, HD]).then_inc(s_rd, 1)
                    v.wait_ge(s_rd, h + 1)
                    v.tensor_tensor(hout[:, :, ds(h * HD, HD)], av[:, :, 0:HD], per_block(rden[:, :], HD), ALU.mult).then_inc(s_ho, 1)


def layer2_fuse(k, w, hout):
    with ExitStack() as ctx:
        hoT = k.sb(ctx, "l2_hoT", [P, N])
        y = k.sb(ctx, "l2_y", [P, NB, D])
        cen = k.sb(ctx, "l2_cen", [P, NB, D])
        mean, var, std = (k.sb(ctx, "l2f_" + n, [P, NB]) for n in ("mean", "var", "std"))
        s_tr, s_hoT, s_y, s_yb, s_var, s_std = (k.sem("l2f_" + n) for n in ("turned", "hoT", "product", "biased", "var", "std"))
        with k.block() as block, ExitStack() as pctx:
            tr = k.ps(pctx, "l2f_tr", [P, 4, CH])
            yp = k.ps(pctx, "l2f_yp", [P, 4, CH])

            @block.tensor
            def _(pe):
                for b in range(NB):
                    pe.transpose(tr[:, b // 4, ds(b % 4 * P, P)], hout[:, b, :], k.ident[:, :]).then_inc(s_tr, 1)
                for b in range(NB):
                    pe.wait_ge(s_hoT, b // 4 + 1)
                    pe.matmul(yp[:, b // 4, ds(b % 4 * P, P)], hoT[:, ds(b * P, P)], w["L2_fuse_WT"][:, :], start=True, stop=True).then_inc(s_y, 1)

            @block.scalar
            def _(act):
                for c in range(NC):
                    act.wait_ge(s_tr, 4 * c + 4)
                    act.activation(hoT[:, ds(c * CH, CH)], tr[:, c, :], ACT.Copy).then_inc(s_hoT, 1)
                act.wait_ge(s_var, 1)
                act.activation(std[:, :], var[:, :], ACT.Sqrt, bias=k.eps[:, :], scale=1.0 / D).then_inc(s_std, 1)

            @block.vector
            def _(v):
                step = k.steps.on(v)
                for c in range(4):
                    v.wait_ge(s_y, 4 * c + 4)
                    step(v.tensor_tensor(y[:, 4 * c:4 * c + 4, :], yp[:, c, :].rearrange("p (b f) -> p b f", f=D), row(w["L2_fuse_b"][:, :], 4), ALU.add))
                center_and_sum(v, step, y[:, :, :], cen[:, :, :], y[:, :, :], mean[:, :], var[:, :])
                v.sem_inc(s_var, 1)
                v.wait_ge(s_std, 1)
                step(v.reciprocal(var[:, :], std[:, :]))
                step(v.tensor_tensor(cen[:, :, :], cen[:, :, :], per_block(var[:, :]), ALU.mult))
                step(v.tensor_tensor(cen[:, :, :], cen[:, :, :], row(w["L2_ln_g"][:, :]), ALU.mult))
                step(v.tensor_tensor(cen[:, :, :], cen[:, :, :], row(w["L2_ln_b"][:, :]), ALU.add))
                step(v.scalar_tensor_tensor(k.x[:, :, :], cen[:, :, :], 0.0, k.x[:, :, :], ALU.max, ALU.add))


NQ = 2 * 3 * H3
UN3 = NB * NC
TINY = 1e-37


def layer3(k):
    with ExitStack() as ctx:
        gru_w = lambda a: [("L3_%s_%s" % (a, n), s) for n, s in (("WihT", [D, 3 * D]), ("WhhT", [D, 3 * D]), ("bih", [D, 3]), ("bhh", [D, 3]))]
        w = load_weights(k, ctx, [("L3_gat_W", [D, H3, D])] + gru_w("node"))
        hT = k.sb(ctx, "l3_hT", [P, N])
        dg = k.sb(ctx, "l3_diag", [P, NB])
        e2 = k.sb(ctx, "l3_e", [P, NB, 2, H3])
        with ExitStack() as c1:
            w.update(load_weights(k, c1, [("L3_gat_WT", [D, H3, D]), ("L3_gat_a", [D, H3, 2])] + gru_w("edge")))
            q2 = k.sb(c1, "l3_q", [P, 2, NB, NQ], BF16)
            nsT = k.sb(c1, "l3_nsT", [P, N])
            with ExitStack() as c2:
                h = k.sb(c2, "l3_h", [P, NB, D])
                work = k.sb(c2, "l3_work", [P, NB, D])
                normed_and_turned(k, "l3_", w, h[:, :, :], hT, work[:, :, :])
                layer3_prepare(k, w, h, hT, work, dg, q2, nsT)
            gru(k, "l3e_", w, "L3_edge_", nsT, hT, dg)
            layer3_scores(k, q2, e2)
        rows = k.sb(ctx, "l3_rows", [P, N], BF16)
        sel = k.sb(ctx, "l3_sel", [P, H3 * P], BF16)
        big = k.sb(ctx, "l3_big", [P, P], BF16)
        layer3_maxima(k, e2, rows, sel, big)
        with ExitStack() as c1:
            es = k.sb(c1, "l3_es", [P, NB, D])
            layer3_attend(k, w, hT, e2, rows, sel, big, es)
            layer3_turn(k, es)
            gru(k, "l3n_", w, "L3_node_", es[:, :, :].rearrange("p b f -> p (b f)"), hT, dg)


def layer3_prepare(k, w, h, hT, work, dg, q2, nsT):
    with ExitStack() as ctx:
        wa = k.sb(ctx, "l3_wa", [D, 2 * H3])
        q = k.sb(ctx, "l3_qn", [P, NB, 2 * H3])
        qr = k.sb(ctx, "l3_qr", [P, NB, 2 * H3])
        s_dg, s_wap, s_wa, s_qp, s_ns, s_nsc = (k.sem("l3p_" + n) for n in ("diag_out", "wa_product", "wa", "q_product", "ns_product", "nsT"))
        with k.block() as block, ExitStack() as pctx:
            nsp = k.ps(pctx, "l3_nsp", [P, 4, CH])
            wap = k.ps(pctx, "l3_wap", [P, CH])
            qp = k.ps(pctx, "l3_qp", [P, CH])
            STEP = N + P
            head = k.adjT[:, 0:(NB - 1) * STEP].rearrange("p (b r) -> p b r", r=STEP)[:, :, 0:P]
            tail = k.adjT[:, (NB - 1) * STEP:]

            @block.vector
            def _(v):
                step = k.steps.on(v)
                step(v.tensor_tensor(work[:, 0:NB - 1, :], head, row(k.ident[:, :], NB - 1), ALU.mult))
                step(v.tensor_tensor(work[:, NB - 1, :], tail, k.ident[:, :], ALU.mult))
                step(v.tensor_reduce(dg[:, :], work[:, :, :], AX_X, ALU.add))
                step(v.tensor_tensor(head, head, work[:, 0:NB - 1, :], ALU.subtract))
                v.tensor_tensor(tail, tail, work[:, NB - 1, :], ALU.subtract).then_inc(s_dg, 1)
                v.wait_ge(s_wap, 1)
                v.tensor_copy(wa[:, :], wap[:, 0:2 * H3]).then_inc(s_wa, 1)
                v.wait_ge(s_qp, 1)
                step(v.tensor_copy(q[:, :, :], qp[:, 0:NB * 2 * H3].rearrange("p (b q) -> p b q", q=2 * H3)))
                parts = lambda s: [q2[:, s, :, :].rearrange("p b (s r h) -> p b s r h", s=2, r=3)[:, :, :, r, :] for r in range(3)]
                qv, rv = (t[:, :, :].rearrange("p b (s h) -> p b s h", s=2) for t in (q, qr))
                split_bf16(step, v, qv, parts(0), rv)
                n3 = NQ // 2
                step(v.tensor_copy(q2[:, 1, :, 0:n3], q2[:, 0, :, n3:]))
                step(v.tensor_copy(q2[:, 1, :, n3:], q2[:, 0, :, 0:n3]))

            @block.tensor
            def _(pe):
                for n in range(H3):
                    mm = pe.matmul(wap[:, 0:2 * H3].rearrange("p (a h) -> p h a", a=2)[:, n, :], w["L3_gat_WT"][:, n, :], w["L3_gat_a"][:, n, :], start=True, stop=True)
                mm.then_inc(s_wap, 1)
                pe.wait_ge(s_dg, 1)
                for c in range(NC):
                    for jb in range(NB):
                        mm = pe.matmul(nsp[:, c, :], h[:, jb, :], k.adj_rows(jb, c * CH, CH), start=jb == 0, stop=jb == NB - 1)
                    mm.then_inc(s_ns, 1)
                    if c == 0:
                        pe.wait_ge(s_wa, 1)
                        for b in range(NB):
                            mm = pe.matmul(qp[:, ds(b * 2 * H3, 2 * H3)], hT[:, ds(b * P, P)], wa[:, :], start=True, stop=True)
                        mm.then_inc(s_qp, 1)

            @block.scalar
            def _(act):
                for c in range(NC):
                    act.wait_ge(s_ns, c + 1)
                    act.activation(nsT[:, ds(c * CH, CH)], nsp[:, c, :], ACT.Copy).then_inc(s_nsc, 1)


def gru(k, tag, w, name, xT, hT, dg):
    wi, wh, bi, bh = (w[name + n] for n in ("WihT", "WhhT", "bih", "bhh"))
    with ExitStack() as ctx:
        r, z, m, o = (k.sb(ctx, tag + n, [P, CH]) for n in ("r", "z", "m", "o"))
        b2 = k.sb(ctx, tag + "b2", [P, 2])
        names = ("bias", "gates", "r", "z", "n_arg", "n", "freed", "out", "turned", "added")
        s_b, s_g, s_r, s_z, s_na, s_n, s_free, s_o, s_tr, s_add = (k.sem(tag + n) for n in names)
        with k.block() as block, ExitStack() as pctx:
            gp = k.ps(pctx, tag + "gp", [P, 4, CH])
            tp = k.ps(pctx, tag + "tp", [P, CH])

            @block.tensor
            def _(pe):
                with pe.Fori(0, NC) as c:
                    i = ds(c * CH, CH)
                    pe.wait_ge(s_free, c + 1)
                    for g in range(2):
                        pe.matmul(gp[:, g, :], wi[:, ds(g * D, D)], xT[:, i], start=True, stop=False)
                        pe.matmul(gp[:, g, :], wh[:, ds(g * D, D)], hT[:, i], start=False, stop=True).then_inc(s_g, 1)
                    pe.matmul(gp[:, 3, :], wh[:, ds(2 * D, D)], hT[:, i], start=True, stop=True).then_inc(s_g, 1)
                    pe.matmul(gp[:, 2, :], wi[:, ds(2 * D, D)], xT[:, i], start=True, stop=True).then_inc(s_g, 1)
                    pe.wait_ge(s_o, c + 1)
                    for b in range(4):
                        mm = pe.transpose(tp[:, ds(b * P, P)], o[:, ds(b * P, P)], k.ident[:, :])
                    mm.then_inc(s_tr, 1)

            @block.scalar
            def _(act):
                act.preload_act_table(ACT.Sigmoid)
                act.wait_ge(s_b, 1)
                with act.Fori(0, NC) as c:
                    act.wait_ge(s_g, c * 4 + 1)
                    act.activation(r[:, :], gp[:, 0, :], ACT.Sigmoid, bias=b2[:, 0:1]).then_inc(s_r, 1)
                    act.wait_ge(s_g, c * 4 + 2)
                    act.activation(z[:, :], gp[:, 1, :], ACT.Sigmoid, bias=b2[:, 1:2]).then_inc(s_z, 1)
                    act.wait_ge(s_na, c + 1)
                    act.activation(m[:, :], m[:, :], ACT.Tanh, bias=bi[:, 2:3]).then_inc(s_n, 1)

            @block.vector
            def _(v):
                step = k.steps.on(v)
                v.tensor_tensor(b2[:, :], bi[:, 0:2], bh[:, 0:2], ALU.add).then_inc(s_b, 1)
                v.sem_inc(s_free, 1)
                first, PER = step.n, 5
                with v.Fori(0, NC) as c:
                    step.begin(c, PER)
                    v.wait_ge(s_r, c + 1)
                    v.wait_ge(s_g, c * 4 + 3)
                    step(v.scalar_tensor_tensor(m[:, :], gp[:, 3, :], bh[:, 2:3], r[:, :], ALU.add, ALU.mult))
                    v.wait_ge(s_g, c * 4 + 4)
                    step(v.tensor_tensor(m[:, :], m[:, :], gp[:, 2, :], ALU.add))
                    v.sem_inc(s_na, 1)
                    v.wait_ge(s_n, c + 1)
                    v.wait_ge(s_z, c + 1)
                    step(v.tensor_tensor(o[:, :], hT[:, ds(c * CH, CH)], m[:, :], ALU.subtract))
                    step(v.tensor_tensor(o[:, :], o[:, :], z[:, :], ALU.mult))
                    step(v.tensor_tensor(o[:, :], o[:, :], m[:, :], ALU.add))
                    step.end(NC, first, PER)
                    v.sem_inc(s_o, 1)
                    v.sem_inc(s_free, 1)
                    v.wait_ge(s_tr, c + 1)
                    for b in range(4):
                        xb = k.x[:, :, :].rearrange("p b f -> p (b f)")[:, ds(c * CH + b * P, P)]
                        v.scalar_tensor_tensor(xb, tp[:, ds(b * P, P)], dg[:, ds(c * 4 + b, 1)], xb, ALU.mult, ALU.add).then_inc(s_add, 1)
                    v.wait_ge(s_add, c * 4 + 4)


def layer3_scores(k, q2, e2):
    with ExitStack() as ctx:
        mk = k.sb(ctx, "l3_mask", [P, 2, 2, N], BF16)
        eq = k.sb(ctx, "l3_eq", [P, NB, 2, 3, H3])
        s_m, s_p = (k.sem("l3s_" + n) for n in ("masks", "summed"))
        with k.block() as block, ExitStack() as pctx:
            ep = k.ps(pctx, "l3_ep", [P, CH])
            qf = q2[:, :, :, :].rearrange("p s b q -> p (s b q)")

            @block.vector
            def _(v):
                step = k.steps.on(v)
                v.sem_inc(s_p, 2)
                with v.Fori(0, NB // 2) as t:
                    for u in range(2):
                        v.wait_ge(s_p, t * 2 + u + 1)
                        v.tensor_scalar(mk[:, u, 0, :], k.adj_rows(t * 2 + u), 0.0, None, ALU.is_gt).then_inc(s_m, 1)
                        v.tensor_scalar(mk[:, u, 1, :], k.adj_rows(t * 2 + u), 0.0, None, ALU.is_lt).then_inc(s_m, 1)
                v.wait_ge(s_p, NB + 2)
                step(v.tensor_copy(eq[:, :, :, :, :].rearrange("p b s r h -> p (b s r h)"), ep[:, 0:NB * NQ]))
                step(v.tensor_tensor(e2[:, :, :, :], eq[:, :, :, 2, :], eq[:, :, :, 1, :], ALU.add))
                step(v.tensor_tensor(e2[:, :, :, :], e2[:, :, :, :], eq[:, :, :, 0, :], ALU.add))
                ef = e2[:, :, :, :].rearrange("p b s h -> p (b s h)")
                step(v.scalar_tensor_tensor(ef, ef, 0.2, ef, ALU.mult, ALU.max))

            @block.tensor
            def _(pe):
                pe.matmul(ep[:, 0:NB * NQ], k.zeros[:, 0:P], k.zeros[:, 0:NB * NQ], start=True, stop=False, skip_group_check=True)
                with pe.Fori(0, NB // 2) as t:
                    for u in range(2):
                        pe.wait_ge(s_m, t * 4 + 2 * u + 2)
                        for b in range(NB):
                            for sign in range(2):
                                mm = pe.matmul(ep[:, ds(b * NQ, NQ)], mk[:, u, sign, ds(b * P, P)], qf[:, ds(t * (2 * NQ) + u * NQ + sign * NB * NQ, NQ)],
                                               start=False, stop=False, skip_group_check=True)
                        mm.then_inc(s_p, 1)


def layer3_maxima(k, e2, rows, sel, big):
    with ExitStack() as ctx:
        R = k.sb(ctx, "l3_R", [P, H3, N], BF16)
        t = k.sb(ctx, "l3_t", [P, 2, H3, N], BF16)
        BT = k.sb(ctx, "l3_BT", [P, 2, N], BF16)
        mx = k.sb(ctx, "l3_mx", [P, H3, NB])
        rn = BT[:, 0, :].rearrange("p (b r) -> p b r", r=P)
        selr = k.sb(ctx, "l3_selr", [H3, H3 * P])
        s_sel, s_bt, s_t, s_m, s_tr, s_rows, s_rt = (k.sem("l3m_" + n) for n in ("sel", "masks", "logits", "maxed", "turned", "rows", "rows_turned"))
        ef = e2[:, :, :, :].rearrange("p b s h -> p (b s h)")
        with k.block() as block, ExitStack() as pctx:
            rt = k.ps(pctx, "l3_rt", [P, H3, N], BF16)
            ro = k.ps(pctx, "l3_ro", [P, N], BF16)

            @block.sync
            def _(sp):
                sp.dma_start(selr[:, :], k.io["sel_rows3"]).then_inc(s_sel, 16)
                sp.wait_ge(s_sel, 16)

            @block.scalar
            def _(act):
                with act.Fori(0, NB) as jb:
                    for h in range(H3):
                        act.wait_ge(s_bt, jb * 2 + 1)
                        act.wait_ge(s_m, jb * H3 + h + 1)
                        k.carry(act, k.act_waits)
                        act.activation(t[:, 0, h, :], BT[:, 0, :], ACT.Identity, bias=ef[:, ds(jb * (2 * H3) + h, 1)]).then_inc(s_t, 1)

            @block.vector
            def _(v):
                step = k.steps.on(v)
                step(v.memset(sel[:, :], 0.0))
                v.wait_ge(s_sel, 16)
                step(v.tensor_copy(sel[0:H3, :], selr[:, :]))
                step(v.tensor_scalar(big[:, :], k.ident[:, :], -BIG, None, ALU.mult))
                step(v.memset(R[:, :, :], -BIG))
                v.sem_inc(s_m, 3)
                first, PER = step.n, 2 * H3
                with v.Fori(0, NB) as jb:
                    step.begin(jb, PER)
                    v.tensor_scalar(BT[:, 0, :], k.adj_rows(jb), 0.0, -BIG, ALU.is_le, ALU.mult).then_inc(s_bt, 1)
                    v.tensor_scalar(BT[:, 1, :], k.adj_rows(jb), 0.0, -BIG, ALU.is_ge, ALU.mult).then_inc(s_bt, 1)
                    v.wait_ge(s_bt, jb * 2 + 2)
                    for h in range(H3):
                        step(v.tensor_scalar(t[:, 1, h, :], BT[:, 1, :], ef[:, ds(jb * (2 * H3) + H3 + h, 1)], None, ALU.add))
                    for h in range(H3):
                        step(v.tensor_tensor(R[:, h, :], R[:, h, :], t[:, 1, h, :], ALU.max))
                    for h in range(H3):
                        v.wait_ge(s_t, jb * H3 + h + 1)
                        v.tensor_tensor(R[:, h, :], R[:, h, :], t[:, 0, h, :], ALU.max).then_inc(s_m, 1)
                    v.wait_ge(s_m, jb * H3 + H3 + 3)
                    step.end(NB, first, PER)
                for h in range(H3):
                    v.wait_ge(s_tr, h + 1)
                    step(v.tensor_reduce(mx[:, h, :], rt[:, h, :].rearrange("p (b q) -> p b q", q=P), AX_X, ALU.max))
                step(v.memset(rn, 0.0))
                mf = mx[:, :, :].rearrange("p h b -> p (h b)")
                step(v.scalar_tensor_tensor(mf, mf, -0.5 * BIG, mf, ALU.is_gt, ALU.mult))
                step(v.tensor_scalar(rn[:, :, 0:H3].rearrange("p b h -> p h b"), mx[:, :, :], -1.0, None, ALU.mult))
                v.sem_inc(s_rows, 1)
                v.wait_ge(s_rt, NB)
                v.tensor_copy(rows[:, :], ro[:, :])

            @block.tensor
            def _(pe):
                pe.wait_ge(s_m, NB * H3 + 3)
                for h in range(H3):
                    for b in range(NB):
                        mm = pe.transpose(rt[:, h, ds(b * P, P)], R[:, h, ds(b * P, P)], k.ident_b[:, :])
                    mm.then_inc(s_tr, 1)
                pe.wait_ge(s_rows, 1)
                for b in range(NB):
                    pe.transpose(ro[:, ds(b * P, P)], rn[:, b, :], k.ident_b[:, :]).then_inc(s_rt, 1)


def layer3_attend(k, w, hT, e2, rows, sel, big, es):
    with ExitStack() as ctx:
        hW = k.sb(ctx, "l3_hW", [P, NB * D])
        mk = k.sb(ctx, "l3_mk", [P, 2, 2, N], BF16)
        U = k.sb(ctx, "l3_U", [P, 4, CH])
        W = k.sb(ctx, "l3_W", [P, 4, CH])
        rden = k.sb(ctx, "l3_rden", [P, NB])
        de = k.sb(ctx, "l3_de", [P, NB, H3])
        ones = k.sb(ctx, "l3_ones", [P, 1])
        part = W[:, :, :].rearrange("p c (r f) -> p (c r) f", f=D)
        ef = e2[:, :, :, :].rearrange("p b s h -> p (b s h)")
        df = de[:, :, :].rearrange("p b h -> p (b h)")
        names = ("init", "hW_product", "hW", "masks", "shift", "logits", "exp", "weighed", "summed", "head_summed", "head_out")
        s_i, s_hp, s_hw, s_mk, s_ps, s_u, s_e, s_w, s_pv, s_hs, s_ho = (k.sem("l3a_" + n) for n in names)
        with k.block() as block, ExitStack() as pctx:
            ps = k.ps(pctx, "l3_ps", [P, 2, CH])
            acc = k.ps(pctx, "l3_acc", [P, 6, CH])

            @block.gpsimd
            def _(pool):
                with pool.Fori(0, H3) as h:
                    for jb in range(NB):
                        pool.wait_ge(s_ps, h * UN3 + 4 * jb + 4)
                        pool.wait_ge(s_u, h * UN3 + 4 * jb + 4)
                        k.carry(pool, k.pool_waits)
                        pool.tensor_scalar(mk[:, jb % 2, 0, :], k.adj_rows(jb), 0.0, None, ALU.is_equal).then_inc(s_mk, 1)
                        pool.tensor_scalar(mk[:, jb % 2, 1, :], k.adj_rows(jb), 0.0, None, ALU.is_lt).then_inc(s_mk, 1)

            @block.tensor
            def _(pe):
                pe.sem_inc(s_ps, 8)
                pe.sem_inc(s_pv, 4)

                def shift(h, t, n):
                    pe.wait_ge(s_mk, h * (2 * NB) + t * 4 + n // 4 * 2 + 2)
                    pe.wait_ge(s_u, h * UN3 + t * 8 + n + 7)
                    i = ds(n % 4 * CH, CH)
                    pe.matmul(ps[:, n % 2, :], sel[:, ds(h * P, P)], rows[:, i], start=True, stop=False)
                    pe.matmul(ps[:, n % 2, :], big[:, :], mk[:, n // 4 % 2, 0, i], start=False, stop=True).then_inc(s_ps, 1)

                def weigh(h, t, n):
                    pe.wait_ge(s_e, h * UN3 + t * 8 + n + 1)
                    for b in range(4):
                        ib = n % 4 * 4 + b
                        pe.matmul(acc[:, ib // ROWB, ds(ib % ROWB * (D + 1) + D, 1)], U[:, n % 4, ds(b * P, P)], ones[:, :], start=False, stop=False, skip_group_check=True)
                    pe.wait_ge(s_w, h * UN3 + t * 8 + n + 1)
                    for b in range(4):
                        ib = n % 4 * 4 + b
                        mm = pe.matmul(acc[:, ib // ROWB, ds(ib % ROWB * (D + 1), D)], W[:, n % 4, ds(b * P, P)], hW[:, ds(t * (2 * D) + n // 4 * D, D)],
                                       start=False, stop=False, skip_group_check=True)
                    mm.then_inc(s_pv, 1)

                pe.wait_ge(s_i, 2)
                with pe.Fori(0, H3) as h:
                    wk = w["L3_gat_W"][:, :, :].rearrange("p h f -> p (h f)")[:, ds(h * D, D)]
                    for c in range(4):
                        pe.wait_ge(s_hw, h * 4 + c + 1)
                        pe.wait_ge(s_u, h * UN3 + 8)
                        for b in range(4):
                            mm = pe.matmul(ps[:, c % 2, ds(b * P, P)], hT[:, ds((4 * c + b) * P, P)], wk, start=True, stop=True)
                        mm.then_inc(s_hp, 1)
                    pe.wait_ge(s_hw, h * 4 + 4 + 2)
                    pe.wait_ge(s_ho, h + 1)
                    for b in range(6):
                        pe.matmul(acc[:, b, 0:ROWB * (D + 1)], k.zeros[:, 0:P], k.zeros[:, 0:ROWB * (D + 1)], start=True, stop=False, skip_group_check=True)
                    shift(h, 0, 0)
                    with pe.Fori(0, UN3 // 8 - 1) as t:
                        for n in range(8):
                            if n < 7:
                                shift(h, t, n + 1)
                            else:
                                shift(h, t + 1, 0)
                            weigh(h, t, n)
                    last = UN3 // 8 - 1
                    for n in range(8):
                        if n < 7:
                            shift(h, last, n + 1)
                        weigh(h, last, n)
                    pe.sem_inc(s_hs, 1)

            @block.scalar
            def _(act):
                act.preload_act_table(ACT.Exp)
                act.sem_inc(s_hw, 2)
                with act.Fori(0, H3) as h:
                    for c in range(4):
                        act.wait_ge(s_hp, h * 4 + c + 1)
                        act.wait_ge(s_pv, h * UN3 + 4)
                        act.activation(hW[:, ds(c * CH, CH)], ps[:, c % 2, :], ACT.Copy).then_inc(s_hw, 1)
                    with act.Fori(0, UN3 // 8) as t:
                        for n in range(8):
                            act.wait_ge(s_u, h * UN3 + t * 8 + n + 9)
                            k.carry(act, k.act_waits)
                            act.activation(U[:, n % 4, :], U[:, n % 4, :], ACT.Exp, bias=ef[:, ds(t * (4 * H3) + n // 4 * (2 * H3) + h, 1)]).then_inc(s_e, 1)

            @block.vector
            def _(v):
                step = k.steps.on(v)
                step(v.memset(es[:, :, :], 0.0))
                v.memset(ones[:, :], 1.0).then_inc(s_i, 1)
                step(v.tensor_tensor(de[:, :, :], e2[:, :, 1, :], e2[:, :, 0, :], ALU.subtract))
                v.sem_inc(s_i, 1)
                v.sem_inc(s_u, 8)
                v.sem_inc(s_ho, 1)

                def logits(h, t, n):
                    v.wait_ge(s_pv, h * UN3 + t * 8 + n + 1)
                    v.wait_ge(s_ps, h * UN3 + t * 8 + n + 9)
                    v.scalar_tensor_tensor(U[:, n % 4, :], mk[:, n // 4, 1, ds(n % 4 * CH, CH)], df[:, ds(t * (2 * H3) + n // 4 * H3 + h, 1)],
                                           ps[:, n % 2, :], ALU.mult, ALU.add).then_inc(s_u, 1)

                def weighed(h, t, n):
                    v.wait_ge(s_e, h * UN3 + t * 8 + n + 1)
                    v.tensor_tensor(W[:, n % 4, :], U[:, n % 4, :], k.adjT[:, ds(t * (2 * N) + n * CH, CH)], ALU.mult).then_inc(s_w, 1)

                first, PER = step.n, 6
                with v.Fori(0, H3) as h:
                    step.begin(h, PER)
                    logits(h, 0, 0)
                    with v.Fori(0, UN3 // 8 - 1) as t:
                        for n in range(8):
                            if n < 7:
                                logits(h, t, n + 1)
                            else:
                                logits(h, t + 1, 0)
                            weighed(h, t, n)
                    last = UN3 // 8 - 1
                    for n in range(8):
                        if n < 7:
                            logits(h, last, n + 1)
                        weighed(h, last, n)
                    v.wait_ge(s_pv, h * UN3 + UN3 + 4)
                    av = acc[:, :, 0:ROWB * (D + 1)].rearrange("p b (r f) -> p b r f", f=D + 1)
                    rv = rden[:, 0:15].rearrange("p (b r) -> p b r", r=ROWB)
                    step(v.tensor_scalar(rv, av[:, 0:5, :, D], TINY, None, ALU.max))
                    step(v.tensor_scalar(rden[:, 15:16], av[:, 5, 0:1, D], TINY, None, ALU.max))
                    step(v.reciprocal(rden[:, :], rden[:, :]))
                    step(v.tensor_tensor(part[:, 0:15, :].rearrange("p (b r) f -> p b r f", r=ROWB), av[:, 0:5, :, 0:D], rv.unsqueeze(3).broadcast_to([P, 5, ROWB, D]), ALU.mult))
                    step(v.tensor_scalar(part[:, 15, :], av[:, 5, 0, 0:D], rden[:, 15:16], None, ALU.mult))
                    v.sem_inc(s_ho, 1)
                    step(v.scalar_tensor_tensor(es[:, :, :], part[:, :, :], 1.0 / H3, es[:, :, :], ALU.mult, ALU.add))
                    step.end(H3, first, PER)


def layer3_turn(k, es):
    s_tr, s_c = k.sem("l3t_turned"), k.sem("l3t_copied")
    with k.block() as block, ExitStack() as pctx:
        tr = k.ps(pctx, "l3t_tr", [P, 4, CH])

        @block.tensor
        def _(pe):
            for b in range(NB):
                pe.transpose(tr[:, b // 4, ds(b % 4 * P, P)], es[:, b, :], k.ident[:, :]).then_inc(s_tr, 1)

        @block.scalar
        def _(act):
            for c in range(NC):
                act.wait_ge(s_tr, 4 * c + 4)
                act.activation(es[:, 4 * c:4 * c + 4, :], tr[:, c, :].rearrange("p (b f) -> p b f", f=D), ACT.Copy).then_inc(s_c, 1)


def stage_store(k):
    s_out = k.sem("out_stored")
    with k.block() as block:

        @block.sync
        def _(sp):
            sp.dma_start(k.io["out"].rearrange("(b p) f -> p b f", p=P), k.x[:, :, :]).then_inc(s_out, 16)
            sp.wait_ge(s_out, 16)


def build(nc, io):
    with ExitStack() as ctx:
        k = Core(nc, io, ctx)
        stage_start(k)
        if 0 in LAYERS:
            layer0(k)
        if 1 in LAYERS:
            layer1(k)
        if 2 in LAYERS:
            layer2(k)
        if 3 in LAYERS:
            layer3(k)
        stage_store(k)


def selectors():
    s = np.zeros((4, H2, 2, H2, P), np.float32)
    for h in range(H2):
        s[0, h, 0, h, :] = 1.0
        s[1:, h, 1, h, :] = 1.0
    return s.reshape(NR, 2, H2 * P)


def _laid_out(inp):
    f = lambda n: np.asarray(inp[n])
    c = np.ascontiguousarray
    halves = lambda a: c(np.moveaxis(a.reshape(CB, P, *a.shape[1:]), 0, 1))
    return {
        "x": c(f("x")), "adjT": c(f("adj").T),
        "ident": np.eye(P, dtype=np.float32),
        "L2_WT": c(f("L2_gnn_W").T), "L2_src": f("L2_gnn_attn_src").reshape(D, 1), "L2_dst": f("L2_gnn_attn_dst").reshape(D, 1),
        "head_mask": np.repeat(np.eye(H2, dtype=np.float32), HD, axis=0), "sel_rows": selectors(),
        "L2_eW": f("L2_gnn_edge_W").reshape(H2), "L2_eb": f("L2_gnn_edge_b"), "L2_fuse_WT": c(f("L2_gnn_fuse_W").T),
        "L2_fuse_b": f("L2_gnn_fuse_b"), "L2_ln_g": f("L2_gnn_ln_g"), "L2_ln_b": f("L2_gnn_ln_b"),
        "L3_gat_W": c(f("L3_gnn_gat_W").transpose(1, 0, 2)), "L3_gat_WT": c(f("L3_gnn_gat_W").transpose(2, 0, 1)),
        "L3_gat_a": c(f("L3_gnn_gat_a").reshape(H3, 2, D).transpose(2, 0, 1)),
        "sel_rows3": np.repeat(np.eye(H3, dtype=np.float32), P, axis=1),
        **{"L3_%s_W%sT" % (a, b): c(f("L3_gnn_%s_W%s" % (a, b)).T) for a in ("edge", "node") for b in ("ih", "hh")},
        **{"L3_%s_b%s" % (a, b): c(f("L3_gnn_%s_b%s" % (a, b)).reshape(3, D).T) for a in ("edge", "node") for b in ("ih", "hh")},
        "L1_gcn_w": c(f("L1_gnn_gcn_w")), "L1_gcn_b": c(f("L1_gnn_gcn_b")), "L1_w_in": c(f("L1_gnn_w_in")),
        "L1_w_xp": halves(f("L1_gnn_w_xp")), "L1_w_dt": c(f("L1_gnn_w_dt")), "L1_w_out": halves(f("L1_gnn_w_out")),
        "L1_A_log": halves(f("L1_gnn_A_log")).reshape(P, CB * DS), "L1_conv_w": halves(f("L1_gnn_conv_w")),
        "L1_conv_b": halves(f("L1_gnn_conv_b")), "L1_b_dt": halves(f("L1_gnn_b_dt")), "L1_D": halves(f("L1_gnn_D_skip")),
        "L1_ln_g": f("L1_gnn_ln_g").reshape(D, 1), "L1_ln_b": f("L1_gnn_ln_b").reshape(D, 1),
        "L0_WT": c(f("L0_gnn_W").T), "L0_bias": c(f("L0_gnn_bias")), "L0_b": c(f("L0_gnn_b")),
    }


def kernel(**inputs):
    import concourse.bacc as bacc
    from concourse.bass_utils import run_bass_kernel_spmd as run

    arrays = _laid_out(inputs)
    nc = bacc.Bacc("TRN2", target_bir_lowering=False, num_devices=1)
    io = {n: nc.dram_tensor("in_" + n, a.shape, mybir.dt.from_np(a.dtype), kind="ExternalInput").ap() for n, a in arrays.items()}
    io["out"] = nc.dram_tensor("out_x", (N, D), F32, kind="ExternalOutput").ap()
    build(nc, io)
    r = run(nc, [{"in_" + n: a for n, a in arrays.items()}], core_ids=[0])
    return r.results[0]["out_x"]
```

```python
from contextlib import ExitStack

import numpy as np

import concourse.bass as bass
from concourse import mybir

ALU = mybir.AluOpType
ACT = mybir.ActivationFunctionType
F32 = mybir.dt.float32
BF16 = mybir.dt.bfloat16
AX_X = mybir.AxisListType.X
ds = bass.ds

P = 128
N = 2048
D = 128
NB = N // P
CH = 512
NC = N // CH
EPS = 1e-5
DI = 256
CB = DI // P
DS = 16
DTR = 8
KC = 4
XP = DTR + 2 * DS
H2 = 8
HD = D // H2
H3 = 3
BIG = 1e30
ROWB = 3
A2 = (2, 1, 1)
LAYERS = (0, 1, 2, 3)


class Steps:

    def __init__(self, eng, sem):
        self.eng, self.sem, self.n, self.turn = eng, sem, 0, 0

    def __call__(self, ins):
        ins.then_inc(self.sem, 1)
        self.n += 1
        self.eng.wait_ge(self.sem, self.turn + self.n)

    def begin(self, turn_index, per_turn):
        self.turn = turn_index * per_turn

    def on(self, eng):
        self.eng = eng
        return self

    def end(self, turns, start, per_turn):
        assert self.n - start == per_turn, (self.n, start, per_turn)
        self.n = start + turns * per_turn
        self.turn = 0


class Core:

    def __init__(self, nc, io, ctx):
        self.nc, self.io, self.ctx = nc, io, ctx
        self.adjT = self.sb(ctx, "adjT", [P, NB * N])
        self.x = self.sb(ctx, "x_nat", [P, NB, D])
        self.ident = self.sb(ctx, "ident", [P, P])
        self.ident_b = self.sb(ctx, "ident_b", [P, P], BF16)
        self.zeros = self.sb(ctx, "zeros", [P, CH], BF16)
        self.eps = self.sb(ctx, "eps", [P, 1])
        self.x_kept = nc.dram_tensor("x_kept", (P, NB, D), F32, kind="Internal").ap()
        self.s_x_kept = self.sem("x_kept")
        self.adj_even = self.sem("adj_even")
        self.adj_odd = self.sem("adj_odd")
        self.steps = Steps(None, self.sem("dve_steps"))
        self.act_waits = self.sem("act_waits_carried")
        self.pool_waits = self.sem("pool_waits_carried")

    def sb(self, ctx, name, shape, dt=F32):
        return ctx.enter_context(self.nc.sbuf_tensor(name, shape, dt))

    def ps(self, ctx, name, shape, dt=F32):
        return ctx.enter_context(self.nc.psum_tensor(name, shape, dt))

    def sem(self, name):
        return self.ctx.enter_context(self.nc.semaphore(name))

    def block(self):
        return self.nc.Block(no_gpsimd_drain=True)

    def carry(self, eng, sem):
        eng.sem_inc(sem, 1)

    def adj_rows(self, jb, i0=0, n=N):
        return self.adjT[:, ds(jb * N + i0, n)]


def run_ahead(eng, ahead, h, turns, per, first, second):
    for n in range(ahead):
        first(h, 0, n)

    def turn(t, more):
        for n in range(per):
            if n + ahead < per:
                first(h, t, n + ahead)
            elif more:
                first(h, t + 1, n + ahead - per)
            second(h, t, n)

    with eng.Fori(0, turns - 1) as t:
        turn(t, True)
    turn(turns - 1, False)


def per_block(t, n=D):
    return t.unsqueeze(2).broadcast_to([t.shape[0], t.shape[1], n])


def row(t, nb=NB):
    return t.unsqueeze(1).broadcast_to([t.shape[0], nb, t.shape[1]])


def center_and_sum(v, step, src, cen, sq, mean, var):
    step(v.tensor_reduce(mean, src, AX_X, ALU.add))
    step(v.tensor_scalar(mean, mean, 1.0 / D, None, ALU.mult))
    step(v.tensor_tensor(cen, src, per_block(mean), ALU.subtract))
    step(v.tensor_tensor(sq, cen, cen, ALU.mult))
    step(v.tensor_reduce(var, sq, AX_X, ALU.add))


def stage_start(k):
    io = k.io
    s_load, s_const = k.sem("start_loaded"), k.sem("start_const")
    with k.block() as block:

        @block.sync
        def _(sp):
            sp.dma_start(k.x[:, :, :], io["x"].rearrange("(b p) f -> p b f", p=P)).then_inc(s_load, 16)
            sp.dma_start(k.ident[:, :], io["ident"]).then_inc(s_load, 16)
            sp.wait_ge(s_load, 32)
            if 0 not in LAYERS:
                load_adjacency(k, sp)

        @block.vector
        def _(v):
            v.memset(k.zeros[:, :], 0.0)
            v.memset(k.eps[:, :], EPS)
            v.wait_ge(s_load, 32)
            v.tensor_copy(k.ident_b[:, :], k.ident[:, :]).then_inc(s_const, 1)


def load_adjacency(k, sp, first=0):
    adj = k.io["adjT"].rearrange("(b p) i -> p b i", p=P)
    for jb in range(first, NB):
        s, n = (k.adj_even, k.adj_odd)[jb % 2], jb // 2
        if n:
            sp.wait_ge(s, 16 * n)
        sp.dma_start(k.adj_rows(jb), adj[:, jb, :]).then_inc(s, 16)


def layer0(k):
    nc, io = k.nc, k.io
    with ExitStack() as ctx:
        gT = k.sb(ctx, "l0_gT", [P, N])
        V = k.sb(ctx, "l0_V", [P, NB, D + 1])
        wT = k.sb(ctx, "l0_wT", [D, D])
        bias = k.sb(ctx, "l0_bias", [P, D])
        b8 = k.sb(ctx, "l0_b8", [P, 1])
        T = k.sb(ctx, "l0_T", [P, 2, N])
        Pm = k.sb(ctx, "l0_P", [P, 2, N])
        stat = k.sb(ctx, "l0_stat", [P, 2, P])
        mean = k.sb(ctx, "l0_mean", [P, NB])
        var = k.sb(ctx, "l0_var", [P, NB])
        norm = k.sb(ctx, "l0_norm", [P, NB])
        rn = k.sb(ctx, "l0_rn", [P, NB])
        h = T[:, 0, :].rearrange("p (b f) -> p b f", f=D)
        sq = T[:, 1, :].rearrange("p (b f) -> p b f", f=D)
        g = Pm[:, 0, :].rearrange("p (b f) -> p b f", f=D)

        s_w, s_var, s_std, s_ss, s_nrm = (k.sem("l0_" + n) for n in ("w_loaded", "var", "std", "sumsq", "norm"))
        s_g, s_gp, s_gt, s_vp = (k.sem("l0_" + n) for n in ("g_ready", "g_turned", "gT_ready", "V_product"))
        with k.block() as block, ExitStack() as pctx:
            tr = k.ps(pctx, "l0_tr", [P, 4, CH])
            vp = k.ps(pctx, "l0_vp", [P, 4, CH])

            @block.sync
            def _(sp):
                sp.dma_start(wT[:, :], io["L0_WT"]).then_inc(s_w, 16)
                sp.dma_start(bias[:, :], io["L0_bias"].partition_broadcast(P)).then_inc(s_w, 16)
                sp.dma_start(b8[:, :], io["L0_b"].partition_broadcast(P)).then_inc(s_w, 16)
                load_adjacency(k, sp)
                sp.wait_ge(s_w, 48)

            @block.vector
            def _(v):
                step = k.steps.on(v)
                center_and_sum(v, step, k.x[:, :, :], h, sq, mean[:, :], var[:, :])
                v.sem_inc(s_var, 1)
                v.wait_ge(s_std, 1)
                step(v.reciprocal(rn[:, :], norm[:, :]))
                step(v.scalar_tensor_tensor(h, h, 0.0, per_block(rn[:, :]), ALU.max, ALU.mult))
                step(v.tensor_tensor(sq, h, h, ALU.mult))
                step(v.tensor_reduce(var[:, :], sq, AX_X, ALU.add))
                v.sem_inc(s_ss, 1)
                v.wait_ge(s_nrm, 1)
                step(v.reciprocal(rn[:, :], norm[:, :]))
                v.tensor_tensor(g, h, per_block(rn[:, :]), ALU.mult).then_inc(s_g, 1)
                v.memset(V[:, :, D:D + 1], 1.0)
                v.wait_ge(s_w, 48)
                v.tensor_scalar(b8[:, :], b8[:, :], 0.125, None, ALU.mult)
                for c in range(4):
                    v.wait_ge(s_vp, 4 * c + 4)
                    v.tensor_tensor(V[:, 4 * c:4 * c + 4, 0:D], vp[:, c, :].rearrange("p (b f) -> p b f", f=D),
                                    per_block(norm[:, 4 * c:4 * c + 4]), ALU.mult)

            @block.scalar
            def _(act):
                act.wait_ge(s_var, 1)
                act.activation(norm[:, :], var[:, :], ACT.Sqrt, bias=k.eps[:, :], scale=1.0 / D).then_inc(s_std, 1)
                act.wait_ge(s_ss, 1)
                act.activation(norm[:, :], var[:, :], ACT.Sqrt).then_inc(s_nrm, 1)
                for c in range(4):
                    act.wait_ge(s_gp, 4 * c + 4)
                    act.activation(gT[:, ds(c * CH, CH)], tr[:, c, :], ACT.Copy).then_inc(s_gt, 1)

            @block.tensor
            def _(pe):
                pe.wait_ge(s_g, 1)
                for b in range(NB):
                    pe.transpose(tr[:, b // 4, ds(b % 4 * P, P)], g[:, b, :], k.ident[:, :]).then_inc(s_gp, 1)
                pe.wait_ge(s_w, 48)
                for b in range(NB):
                    pe.wait_ge(s_gt, b // 4 + 1)
                    pe.matmul(vp[:, b // 4, ds(b % 4 * P, P)], gT[:, ds(b * P, P)], wT[:, :], start=True, stop=True).then_inc(s_vp, 1)

        s_stat, s_score, s_tanh, s_exp, s_p, s_pv = (k.sem("l0_" + n) for n in ("stationary", "score", "tanh", "exp", "probs", "pv"))
        with k.block() as block, ExitStack() as pctx:
            S = k.ps(pctx, "l0_S", [P, 2, CH])
            acc = k.ps(pctx, "l0_acc", [P, 6, CH])

            @block.gpsimd
            def _(pool):
                with pool.Fori(0, NB // 2) as t:
                    for u in range(2):
                        if u == 0:
                            pool.wait_ge(s_score, t * 8 + 4)
                        else:
                            pool.wait_ge(s_score, t * 8 + 8)
                        pool.tensor_copy(stat[:, u, :], gT[:, ds(t * (2 * P) + u * P, P)]).then_inc(s_stat, 1)

            @block.tensor
            def _(pe):
                pe.sem_inc(s_score, 8)
                pe.sem_inc(s_pv, 2)
                for b in range(6):
                    pe.matmul(acc[:, b, 0:ROWB * (D + 1)], k.zeros[:, 0:P], k.zeros[:, 0:ROWB * (D + 1)],
                              start=True, stop=False, skip_group_check=True)

                def scores(t, u):
                    pe.wait_ge(s_stat, t * 2 + u + 1)
                    for c in range(NC):
                        pe.wait_ge(s_tanh, t * 8 + 4 * u + c + 1)
                        pe.matmul(S[:, c % 2, :], stat[:, u % 2, :], gT[:, ds(c * CH, CH)], start=True, stop=True).then_inc(s_score, 1)

                def weigh(t, u):
                    pe.wait_ge(s_p, t * 2 + u + 3)
                    for b in range(NB):
                        mm = pe.matmul(acc[:, b // ROWB, ds(b % ROWB * (D + 1), D + 1)], Pm[:, u, ds(b * P, P)],
                                       V[:, :, :].rearrange("p b f -> p (b f)")[:, ds(t * (2 * (D + 1)) + u * (D + 1), D + 1)],
                                       start=False, stop=False, skip_group_check=True)
                    mm.then_inc(s_pv, 1)

                scores(0, 0)
                with pe.Fori(0, NB // 2 - 1) as t:
                    scores(t, 1)
                    weigh(t, 0)
                    scores(t + 1, 0)
                    weigh(t, 1)
                last = NB // 2 - 1
                scores(last, 1)
                weigh(last, 0)
                weigh(last, 1)

            @block.scalar
            def _(act):
                act.sem_inc(s_tanh, 2)
                act.preload_act_table(ACT.Exp)
                with act.Fori(0, NB // 2) as t:
                    for u in range(2):
                        act.wait_ge(s_p, t * 2 + u + 1)
                        for c in range(NC):
                            act.wait_ge(s_score, t * 8 + 4 * u + c + 9)
                            act.activation(T[:, u, ds(c * CH, CH)], S[:, c % 2, :], ACT.Tanh, scale=b8[:, 0:1]).then_inc(s_tanh, 1)
                        act.wait_ge(s_tanh, t * 8 + 4 * u + NC + 2)
                        act.activation(T[:, u, :], T[:, u, :], ACT.Exp, scale=8.0).then_inc(s_exp, 1)

            @block.vector
            def _(v):
                step = k.steps.on(v)
                v.sem_inc(s_p, 2)
                with v.Fori(0, NB // 2) as t:
                    for u in range(2):
                        v.wait_ge((k.adj_even, k.adj_odd)[u], t * 16 + 16)
                        v.wait_ge(s_exp, t * 2 + u + 1)
                        v.wait_ge(s_pv, t * 2 + u + 1)
                        v.tensor_tensor(Pm[:, u, :], T[:, u, :], k.adj_rows(t * 2 + u), ALU.mult).then_inc(s_p, 1)
                v.wait_ge(s_pv, NB + 2)
                accv = acc[:, :, 0:ROWB * (D + 1)].rearrange("p b (r f) -> p b r f", f=D + 1)
                rv = rn[:, 0:15].rearrange("p (b r) -> p b r", r=ROWB)
                ov = T[:, 0, 0:15 * D].rearrange("p (b r f) -> p b r f", r=ROWB, f=D)
                step(v.reciprocal(rv, accv[:, 0:5, :, D]))
                step(v.reciprocal(rn[:, 15:16], accv[:, 5, 0:1, D]))
                step(v.tensor_tensor(ov, accv[:, 0:5, :, 0:D], rv.unsqueeze(3).broadcast_to([P, 5, ROWB, D]), ALU.mult))
                step(v.tensor_scalar(T[:, 0, 15 * D:16 * D], accv[:, 5, 0, 0:D], rn[:, 15:16], None, ALU.mult))
                step(v.tensor_tensor(k.x[:, :, :], k.x[:, :, :], h, ALU.add))
                step(v.tensor_tensor(k.x[:, :, :], k.x[:, :, :], row(bias[:, :]), ALU.add))


def layer1_gcn(k, hT, wts):
    io = k.io
    with ExitStack() as ctx:
        h1 = k.sb(ctx, "l1_h1", [P, NB, D])
        cen = k.sb(ctx, "l1_cen", [P, NB, D])
        sq = k.sb(ctx, "l1_sq", [P, NB, D])
        axT = k.sb(ctx, "l1_axT", [P, N])
        gw = k.sb(ctx, "l1_gcn_w", [D, D])
        gb = k.sb(ctx, "l1_gcn_b", [P, D])
        mean = k.sb(ctx, "l1_mean", [P, NB])
        var = k.sb(ctx, "l1_var", [P, NB])
        std = k.sb(ctx, "l1_std", [P, NB])
        s_wl = k.sem("l1_all_weights_loaded")
        s_w, s_var, s_std, s_h, s_ax, s_axT, s_aw, s_n, s_tr, s_hT = (
            k.sem("l1_" + n) for n in ("w_loaded", "var", "std", "h1_ready", "ax_product", "axT_ready", "axw_product", "normed", "turned", "hT_ready"))
        with k.block() as block, ExitStack() as pctx:
            ax = k.ps(pctx, "l1_ax", [P, 4, CH])
            aw = k.ps(pctx, "l1_aw", [P, 4, CH])

            @block.sync
            def _(sp):
                sp.dma_start(gw[:, :], io["L1_gcn_w"]).then_inc(s_w, 16)
                sp.dma_start(gb[:, :], io["L1_gcn_b"].partition_broadcast(P)).then_inc(s_w, 16)
                for t, n in wts:
                    sp.dma_start(t, io[n]).then_inc(s_wl, 16)
                sp.wait_ge(s_w, 32)
                sp.wait_ge(s_wl, 16 * len(wts))

            @block.vector
            def _(v):
                step = k.steps.on(v)
                center_and_sum(v, step, k.x[:, :, :], cen[:, :, :], sq[:, :, :], mean[:, :], var[:, :])
                v.sem_inc(s_var, 1)
                v.wait_ge(s_std, 1)
                step(v.reciprocal(var[:, :], std[:, :]))
                v.scalar_tensor_tensor(h1[:, :, :], cen[:, :, :], 0.0, per_block(var[:, :]), ALU.max, ALU.mult).then_inc(s_h, 1)
                v.wait_ge(s_h, 1)
                v.wait_ge(s_w, 32)
                for c in range(4):
                    v.wait_ge(s_aw, 4 * c + 4)
                    v.tensor_tensor(sq[:, 4 * c:4 * c + 4, :], aw[:, c, :].rearrange("p (b f) -> p b f", f=D), row(gb[:, :], 4), ALU.add).then_inc(s_h, 1)
                v.wait_ge(s_h, 5)
                step(v.tensor_scalar(sq[:, :, :], sq[:, :, :], 0.0, None, ALU.max))
                center_and_sum(v, step, sq[:, :, :], cen[:, :, :], h1[:, :, :], mean[:, :], var[:, :])
                v.sem_inc(s_var, 1)
                v.wait_ge(s_std, 2)
                step(v.reciprocal(var[:, :], std[:, :]))
                v.tensor_tensor(cen[:, :, :], cen[:, :, :], per_block(var[:, :]), ALU.mult).then_inc(s_n, 1)

            @block.scalar
            def _(act):
                for r in range(2):
                    act.wait_ge(s_var, r + 1)
                    act.activation(std[:, :], var[:, :], ACT.Sqrt, bias=k.eps[:, :], scale=1.0 / D).then_inc(s_std, 1)
                    if r == 0:
                        for c in range(NC):
                            act.wait_ge(s_ax, c + 1)
                            act.activation(axT[:, ds(c * CH, CH)], ax[:, c, :], ACT.Copy).then_inc(s_axT, 1)
                act.wait_ge(s_wl, 16 * len(wts))
                for c in range(4):
                    act.wait_ge(s_tr, 4 * c + 4)
                    act.activation(hT[:, ds(c * CH, CH)], ax[:, c, :], ACT.Identity, bias=k.l1["ln_b"][:, :], scale=k.l1["ln_g"][:, :]).then_inc(s_hT, 1)

            @block.tensor
            def _(pe):
                pe.wait_ge(s_h, 1)
                for r in range(NB // 2):
                    pe.wait_ge(k.adj_even, 16 * (r + 1))
                    pe.wait_ge(k.adj_odd, 16 * (r + 1))
                for c in range(NC):
                    for jb in range(NB):
                        mm = pe.matmul(ax[:, c, :], h1[:, jb, :], k.adj_rows(jb, c * CH, CH), start=jb == 0, stop=jb == NB - 1)
                    mm.then_inc(s_ax, 1)
                pe.wait_ge(s_w, 32)
                for b in range(NB):
                    pe.wait_ge(s_axT, b // 4 + 1)
                    pe.matmul(aw[:, b // 4, ds(b % 4 * P, P)], axT[:, ds(b * P, P)], gw[:, :], start=True, stop=True).then_inc(s_aw, 1)
                pe.wait_ge(s_n, 1)
                for b in range(NB):
                    pe.transpose(ax[:, b // 4, ds(b % 4 * P, P)], cen[:, b, :], k.ident[:, :]).then_inc(s_tr, 1)


def layer1_ssm(k, hT):
    io, w = k.io, k.l1
    with ExitStack() as ctx:
        t2 = lambda n, dt=F32: k.sb(ctx, "l1_" + n, [P, CB, CH], dt)
        RING = 4
        xin = k.sb(ctx, "l1_xin", [P, CB, CH + KC - 1])
        u, sz, dt, du = t2("u"), t2("sz"), t2("dt"), t2("du")
        hs, hC = t2("hs"), t2("hC")
        dA = k.sb(ctx, "l1_dA", [P, 2, CB, CH])
        dBu = t2("dBu")
        dbc = dA[0:XP, 0, 0, :]
        bc = k.sb(ctx, "l1_bc", [P, RING, 2, CH])
        state = k.sb(ctx, "l1_state", [P, CB * DS])
        negA = k.sb(ctx, "l1_negA", [P, CB * DS])
        bc_dram = k.nc.dram_tensor("l1_bc_rows", (2 * DS, N), F32, kind="Internal").ap()
        bc_src = bc_dram.rearrange("(a n) t -> a (n t)", a=2)

        names = ("init", "xz_product", "xin_ready", "sz_ready", "conv", "u_ready", "dbc_product", "dbc_ready", "dt_product",
                 "softplus_in", "softplus_e", "softplus_l", "dt_ready", "bc_stored", "dA_ready", "dBu_ready",
                 "scanned", "hC_ready", "y_summed", "yT_ready", "out_product", "out_added", "negA_exp", "du_free")
        (s_init, s_xz, s_xin, s_sz, s_conv, s_u, s_dbcp, s_dbc, s_dtp, s_spin, s_spe, s_spl, s_dt, s_bcst, s_dA, s_dBu,
         s_scan, s_hC, s_y, s_yT, s_op, s_oa, s_nA, s_duf) = (k.sem("l1_" + n) for n in names)
        s_bc = [k.sem("l1_bc%d" % n) for n in range(RING)]
        TURNS = DS // RING
        with k.block() as block, ExitStack() as pctx:
            xp = k.ps(pctx, "l1_xp", [P, CB, CH])
            zp = k.ps(pctx, "l1_zp", [P, CB, CH])
            yp = k.ps(pctx, "l1_yp", [P, CB, CH])
            dp = k.ps(pctx, "l1_dp", [P, CH])
            op = k.ps(pctx, "l1_op", [P, CH])

            @block.sync
            def _(sp):
                sp.sem_inc(s_hC, 2 * RING)
                with sp.Fori(0, NC) as q:
                    sp.wait_ge(s_dbc, q + 1)
                    sp.dma_start(bc_dram[:, ds(q * CH, CH)], dA[DTR:XP, 0, 0, :]).then_inc(s_bcst, 16)
                    with sp.Fori(0, TURNS) as r:
                        for e in range(RING):
                            if e == 0:
                                sp.wait_ge(s_bcst, q * 16 + 16)
                            sp.wait_ge(s_hC, q * (2 * DS) + r * (2 * RING) + 2 * e + 2)
                            sp.dma_start(bc[:, e, :, :], bc_src[:, ds((r * RING + e) * N + q * CH, CH)].partition_broadcast(P)).then_inc(s_bc[e], 16)

            @block.gpsimd
            def _(pool):
                pool.memset(state[:, :], 0.0)
                pool.memset(xin[:, :, 0:KC - 1], 0.0).then_inc(s_init, 1)
                with pool.Fori(0, NC) as q:
                    with pool.Fori(0, TURNS) as r:
                        for e in range(RING):
                            pool.wait_ge(s_dt, q + 1)
                            pool.wait_ge(s_bc[e], q * (16 * TURNS) + r * 16 + 16)
                            for cb in range(CB):
                                pool.wait_ge(s_scan, q * (2 * DS) + r * (2 * RING) + 2 * e + cb + 3)
                                pool.tensor_tensor(dBu[:, cb, :], du[:, cb, :], bc[:, e, 0, :], ALU.mult).then_inc(s_dBu, 1)

            @block.tensor
            def _(pe):
                pe.sem_inc(s_y, 2)
                with pe.Fori(0, NC) as q:
                    pe.wait_ge(s_duf, q + 1)
                    for cb in range(CB):
                        pe.matmul(xp[:, cb, :], w["w_in"][:, ds(cb * P, P)], hT[:, ds(q * CH, CH)], start=True, stop=True).then_inc(s_xz, 1)
                    for cb in range(CB):
                        pe.matmul(zp[:, cb, :], w["w_in"][:, ds(DI + cb * P, P)], hT[:, ds(q * CH, CH)], start=True, stop=True).then_inc(s_xz, 1)
                        pe.matmul(yp[:, cb, :], k.zeros[:, 0:P], k.zeros[:, :], start=True, stop=False, skip_group_check=True)
                    pe.wait_ge(s_u, q * 2 + 2)
                    for cb in range(CB):
                        mm = pe.matmul(dp[0:XP, :], w["w_xp"][:, cb, :], u[:, cb, :], start=cb == 0, stop=cb == 1)
                    mm.then_inc(s_dbcp, 1)
                    pe.wait_ge(s_dbc, q + 1)
                    for cb in range(CB):
                        pe.matmul(xp[:, cb, :], w["w_dt"][:, ds(cb * P, P)], dA[0:DTR, 0, 0, :], start=True, stop=True).then_inc(s_dtp, 1)
                    with pe.Fori(0, DS) as n:
                        for cb in range(CB):
                            pe.wait_ge(s_hC, q * (2 * DS) + n * 2 + cb + 2 * RING + 1)
                            pe.matmul(yp[:, cb, :], k.ident[:, :], hC[:, cb, :], start=False, stop=False, skip_group_check=True).then_inc(s_y, 1)
                    pe.wait_ge(s_yT, q * 2 + 2)
                    for b in range(CH // P):
                        for cb in range(CB):
                            mm = pe.matmul(op[:, ds(b * P, P)], hC[:, cb, ds(b * P, P)], w["w_out"][:, cb, :], start=cb == 0, stop=cb == 1)
                    mm.then_inc(s_op, 1)

            @block.scalar
            def _(act):
                act.activation(negA[:, :], w["A_log"][:, :], ACT.Exp).then_inc(s_nA, 1)
                with act.Fori(0, NC) as q:
                    for cb in range(CB):
                        act.wait_ge(s_xz, q * 4 + cb + 1)
                        act.activation(xin[:, cb, KC - 1:], xp[:, cb, :], ACT.Copy).then_inc(s_xin, 1)
                    for cb in range(CB):
                        act.wait_ge(s_conv, q * 2 + cb + 1)
                        act.activation(u[:, cb, :], hs[:, cb, :], ACT.Silu, bias=w["conv_b"][:, cb:cb + 1]).then_inc(s_u, 1)
                    for cb in range(CB):
                        act.wait_ge(s_xz, q * 4 + cb + 3)
                        act.activation(sz[:, cb, :], zp[:, cb, :], ACT.Silu).then_inc(s_sz, 1)
                    act.wait_ge(s_dbcp, q + 1)
                    act.activation(dbc, dp[0:XP, :], ACT.Copy).then_inc(s_dbc, 1)
                    act.wait_ge(s_spin, q * 2 + 2)
                    for cb in range(CB):
                        act.activation(hC[:, cb, :], dBu[:, cb, :], ACT.Exp).then_inc(s_spe, 1)
                    act.wait_ge(s_spe, q * 2 + 2)
                    for cb in range(CB):
                        act.activation(du[:, cb, :], hC[:, cb, :], ACT.Ln, bias=1.0).then_inc(s_spl, 1)
                    act.wait_ge(s_dt, q + 1)
                    act.wait_ge(s_bcst, q * 16 + 16)
                    k.carry(act, k.act_waits)
                    act.preload_act_table(ACT.Exp)
                    with act.Fori(0, DS // 2) as r:
                        for e in range(2):
                            for cb in range(CB):
                                act.wait_ge(s_scan, q * (2 * DS) + r * 4 + 2 * e + cb + 1)
                                act.activation(dA[:, e, cb, :], dt[:, cb, :], ACT.Exp, scale=negA[:, ds(r * 2 + e + cb * DS, 1)]).then_inc(s_dA, 1)

            @block.vector
            def _(v):
                step = k.steps.on(v)
                v.wait_ge(s_nA, 1)
                step(v.tensor_scalar(negA[:, :], negA[:, :], -1.0, None, ALU.mult))
                v.sem_inc(s_duf, 1)
                v.sem_inc(s_scan, 4)
                v.wait_ge(s_init, 1)
                first, PER = step.n, 22
                with v.Fori(0, NC) as q:
                    step.begin(q, PER)
                    cv = hs
                    for kk in range(KC):
                        for cb in range(CB):
                            if kk == 0:
                                v.wait_ge(s_xin, q * 2 + cb + 1)
                                ins = v.tensor_scalar(cv[:, cb, :], xin[:, cb, 0:CH], w["conv_w"][:, cb, 0:1], None, ALU.mult)
                            else:
                                ins = v.scalar_tensor_tensor(cv[:, cb, :], xin[:, cb, kk:kk + CH], w["conv_w"][:, cb, kk:kk + 1], cv[:, cb, :], ALU.mult, ALU.add)
                            step(ins)
                            if kk == KC - 1:
                                v.sem_inc(s_conv, 1)
                    for cb in range(CB):
                        step(v.tensor_copy(xin[:, cb, 0:KC - 1], xin[:, cb, CH:CH + KC - 1]))
                    for cb in range(CB):
                        v.wait_ge(s_dtp, q * 2 + cb + 1)
                        step(v.tensor_scalar(dt[:, cb, :], xp[:, cb, :], w["b_dt"][:, cb:cb + 1], None, ALU.add))
                        v.scalar_tensor_tensor(dBu[:, cb, :], dt[:, cb, :], -1.0, dt[:, cb, :], ALU.mult, ALU.min).then_inc(s_spin, 1)
                    for cb in range(CB):
                        v.wait_ge(s_spe, q * 2 + cb + 1)
                        step(v.tensor_scalar(hs[:, cb, :], hC[:, cb, :], 1.0, None, ALU.add))
                        step(v.scalar_tensor_tensor(hs[:, cb, :], hs[:, cb, :], -1.0, hC[:, cb, :], ALU.add, ALU.subtract))
                        v.wait_ge(s_spl, q * 2 + cb + 1)
                        step(v.scalar_tensor_tensor(dt[:, cb, :], dt[:, cb, :], 0.0, du[:, cb, :], ALU.max, ALU.add))
                        step(v.tensor_tensor(dt[:, cb, :], dt[:, cb, :], hs[:, cb, :], ALU.subtract))
                        if cb == 0:
                            step(v.tensor_tensor(du[:, cb, :], dt[:, cb, :], u[:, cb, :], ALU.mult))
                        else:
                            step(v.tensor_tensor(du[:, cb, :], dt[:, cb, :], u[:, cb, :], ALU.mult))
                    step.end(NC, first, PER)
                    v.sem_inc(s_dt, 1)
                    with v.Fori(0, TURNS) as r:
                        for e in range(RING):
                            base = q * (2 * DS) + r * (2 * RING) + 2 * e
                            for cb in range(CB):
                                at = state[:, ds(r * RING + e + cb * DS, 1)]
                                v.wait_ge(s_dA, base + cb + 1)
                                v.wait_ge(s_dBu, base + cb + 1)
                                v.tensor_tensor_scan(hs[:, cb, :], dA[:, e % 2, cb, :], dBu[:, cb, :], at, ALU.mult, ALU.add).then_inc(s_scan, 1)
                            v.wait_ge(s_bc[e], q * (16 * TURNS) + r * 16 + 16)
                            for cb in range(CB):
                                at = state[:, ds(r * RING + e + cb * DS, 1)]
                                v.wait_ge(s_scan, base + cb + 5)
                                v.wait_ge(s_y, base + cb + 1)
                                v.tensor_tensor(hC[:, cb, :], hs[:, cb, :], bc[:, e, 1, :], ALU.mult).then_inc(s_hC, 1)
                                v.tensor_copy(at, hs[:, cb, CH - 1:CH]).then_inc(s_oa, 1)
                            v.wait_ge(s_oa, base + 2)
                            v.wait_ge(s_hC, base + 2 + 2 * RING)
                    for cb in range(CB):
                        v.wait_ge(s_y, q * (2 * DS) + 2 * DS + 2)
                        v.scalar_tensor_tensor(hs[:, cb, :], u[:, cb, :], w["D"][:, cb:cb + 1], yp[:, cb, :], ALU.mult, ALU.add).then_inc(s_init, 1)
                        v.wait_ge(s_init, q * 2 + cb + 2)
                        v.wait_ge(s_sz, q * 2 + cb + 1)
                        v.tensor_tensor(hC[:, cb, :], hs[:, cb, :], sz[:, cb, :], ALU.mult).then_inc(s_yT, 1)
                    v.wait_ge(s_op, q + 1)
                    xq = k.x[:, :, :].rearrange("p b f -> p (b f)")[:, ds(q * CH, CH)]
                    v.tensor_tensor(xq, xq, op[:, :], ALU.add).then_inc(s_duf, 1)


def layer1(k):
    with ExitStack() as ctx:
        w = k.l1 = {}
        for n, shape in (("w_in", [D, 2 * DI]), ("w_xp", [P, CB, XP]), ("w_dt", [DTR, DI]), ("w_out", [P, CB, D]), ("A_log", [P, CB * DS]),
                         ("conv_w", [P, CB, KC]), ("conv_b", [P, CB]), ("b_dt", [P, CB]), ("D", [P, CB]), ("ln_g", [P, 1]), ("ln_b", [P, 1])):
            w[n] = k.sb(ctx, "l1w_" + n, shape)
        hT = k.sb(ctx, "l1_hT", [P, N])
        layer1_gcn(k, hT, [(w[n][tuple(slice(None) for _ in w[n].shape)], "L1_" + n) for n in w])
        layer1_ssm(k, hT)


def load_weights(k, ctx, sp_list):
    w = {}
    for n, shape in sp_list:
        w[n] = k.sb(ctx, "w_" + n, shape)
    return w


def normed_and_turned(k, tag, w, h, hT, work):
    with ExitStack() as ctx:
        mean, var, std = (k.sb(ctx, tag + n, [P, NB]) for n in ("mean", "var", "std"))
        s_w, s_var, s_std, s_h, s_tr, s_hT = (k.sem(tag + n) for n in ("weights", "var", "std", "h", "turned", "hT"))
        with k.block() as block, ExitStack() as pctx:
            tr = k.ps(pctx, tag + "tr", [P, 4, CH])

            @block.sync
            def _(sp):
                for n in w:
                    t = w[n]
                    sp.dma_start(t[tuple(slice(None) for _ in t.shape)], k.io[n] if len(k.io[n].shape) > 1 else k.io[n].partition_broadcast(P)).then_inc(s_w, 16)
                sp.wait_ge(s_w, 16 * len(w))

            @block.vector
            def _(v):
                step = k.steps.on(v)
                center_and_sum(v, step, k.x[:, :, :], h, work, mean[:, :], var[:, :])
                v.sem_inc(s_var, 1)
                v.wait_ge(s_std, 1)
                step(v.reciprocal(var[:, :], std[:, :]))
                v.scalar_tensor_tensor(h, h, 0.0, per_block(var[:, :]), ALU.max, ALU.mult).then_inc(s_h, 1)

            @block.scalar
            def _(act):
                act.wait_ge(s_var, 1)
                act.activation(std[:, :], var[:, :], ACT.Sqrt, bias=k.eps[:, :], scale=1.0 / D).then_inc(s_std, 1)
                for c in range(NC):
                    act.wait_ge(s_tr, 4 * c + 4)
                    act.activation(hT[:, ds(c * CH, CH)], tr[:, c, :], ACT.Copy).then_inc(s_hT, 1)

            @block.tensor
            def _(pe):
                pe.wait_ge(s_h, 1)
                for b in range(NB):
                    pe.transpose(tr[:, b // 4, ds(b % 4 * P, P)], h[:, b, :], k.ident[:, :]).then_inc(s_tr, 1)


def split_bf16(step, v, src, parts, rest):
    step(v.tensor_copy(parts[0], src))
    step(v.tensor_tensor(rest, src, parts[0], ALU.subtract))
    step(v.tensor_copy(parts[1], rest))
    step(v.tensor_tensor(rest, rest, parts[1], ALU.subtract))
    step(v.tensor_copy(parts[2], rest))


HALF = N // 2
UNITS = 2 * NB
VW = HD + 1
NR = 4 * H2


def layer2(k):
    with ExitStack() as ctx:
        w = load_weights(k, ctx, [("L2_WT", [D, D]), ("L2_src", [D, 1]), ("L2_dst", [D, 1]), ("head_mask", [D, H2]), ("L2_eW", [P, H2]), ("L2_eb", [P, H2]),
                                  ("L2_fuse_WT", [D, D]), ("L2_fuse_b", [P, D]), ("L2_ln_g", [P, D]), ("L2_ln_b", [P, D])])
        V = k.sb(ctx, "l2_V", [P, NB, H2, VW])
        ad = k.sb(ctx, "l2_ad", [P, NB, H2])
        srcn = k.sb(ctx, "l2_as", [P, NB, H2])
        rows = k.sb(ctx, "l2_rows", [P, N], BF16)
        big = k.sb(ctx, "l2_big", [P, P], BF16)
        layer2_project(k, w, V, ad, srcn)
        layer2_maxima(k, w, ad, srcn, rows, big)
        hout = k.sb(ctx, "l2_hout", [P, NB, D])
        layer2_attend(k, w, V, ad, rows, big, hout)
        layer2_fuse(k, w, hout)


def layer2_project(k, w, V, ad, srcn):
    with ExitStack() as ctx:
        h = k.sb(ctx, "l2_h", [P, NB, D])
        hT = k.sb(ctx, "l2_hT", [P, N])
        h2T = k.sb(ctx, "l2_h2T", [P, N])
        att = k.sb(ctx, "l2_att", [D, 2 * H2])
        normed_and_turned(k, "l2_", w, h[:, :, :], hT, h2T[:, :].rearrange("p (b f) -> p b f", f=D))
        s_att, s_h2T, s_h2Tc, s_v, s_vc, s_a, s_a2 = (k.sem("l2p_" + n) for n in ("att", "h2T_product", "h2T", "V_product", "V", "logit_terms", "ones"))
        with k.block() as block, ExitStack() as pctx:
            @block.sync
            def _(sp):
                sp.dma_start(k.x_kept, k.x[:, :, :]).then_inc(k.s_x_kept, 16)
                sp.wait_ge(k.s_x_kept, 16)

            tp = k.ps(pctx, "l2_tp", [P, 4, CH])
            vp = k.ps(pctx, "l2_vp", [P, 3, CH])
            ap = k.ps(pctx, "l2_ap", [P, NB, 2 * H2])

            @block.tensor
            def _(pe):
                for c in range(NC):
                    pe.matmul(tp[:, c, :], w["L2_WT"][:, :], hT[:, ds(c * CH, CH)], start=True, stop=True).then_inc(s_h2T, 1)
                for b in range(NB):
                    if b >= 12 and b % 4 == 0:
                        pe.wait_ge(s_vc, b // 4 - 2)
                    pe.matmul(vp[:, b // 4 % 3, ds(b % 4 * P, P)], hT[:, ds(b * P, P)], w["L2_WT"][:, :], start=True, stop=True).then_inc(s_v, 1)
                pe.wait_ge(s_att, 2)
                for b in range(NB):
                    pe.wait_ge(s_h2Tc, b // 4 + 1)
                    pe.matmul(ap[:, b, :], h2T[:, ds(b * P, P)], att[:, :], start=True, stop=True).then_inc(s_a, 1)

            @block.scalar
            def _(act):
                for c in range(NC):
                    act.wait_ge(s_h2T, c + 1)
                    act.activation(h2T[:, ds(c * CH, CH)], tp[:, c, :], ACT.Copy).then_inc(s_h2Tc, 1)

            @block.vector
            def _(v):
                for n, name in enumerate(("L2_src", "L2_dst")):
                    v.tensor_scalar(att[:, ds(n * H2, H2)], w["head_mask"][:, :], w[name][:, 0:1], None, ALU.mult).then_inc(s_att, 1)
                v.memset(V[:, :, :, HD:VW], 1.0)
                for c in range(4):
                    v.wait_ge(s_v, 4 * c + 4)
                    v.tensor_copy(V[:, 4 * c:4 * c + 4, :, 0:HD], vp[:, c % 3, :].rearrange("p (b h d) -> p b h d", h=H2, d=HD)).then_inc(s_vc, 1)
                v.wait_ge(s_a, NB)
                v.tensor_copy(srcn[:, :, :], ap[:, :, 0:H2])
                v.tensor_copy(ad[:, :, :], ap[:, :, H2:])


def layer2_maxima(k, w, ad, srcn, rows, big):
    with ExitStack() as ctx:
        R = k.sb(ctx, "l2_R", [P, H2, N], BF16)
        t = k.sb(ctx, "l2_t", [P, 4, N], BF16)
        ab0 = k.sb(ctx, "l2_ab", [P, N], BF16)
        spare = k.x[:, :, :].rearrange("p b f -> p (b f)").bitcast(BF16).rearrange("p (a i) -> p a i", a=2)
        BT, ab = (rows[:, :], spare[:, 0, :]), (ab0[:, :], spare[:, 1, :])
        eI = k.sb(ctx, "l2_eI", [P, H2 - 2, P], BF16)
        mx = t[:, 1, 0:2 * NB * H2].bitcast(F32).rearrange("p (h b) -> p h b", b=NB)
        rn = ab0[:, :].rearrange("p (b r) -> p b r", r=P)
        rest = t[:, 0, 0:2 * NB * H2].bitcast(F32).rearrange("p (b h) -> p b h", h=H2)
        s_t, s_bt, s_m, s_r, s_sp = (k.sem("l2m_" + n) for n in ("logits", "mask", "masked", "maxed", "masked_sum"))
        s_tr, s_red, s_rows, s_rt = (k.sem("l2m_" + n) for n in ("turned", "reduced", "rows", "rows_turned"))
        PE0 = 2
        ACTH = H2 - 1
        with k.block() as block, ExitStack() as pctx:
            masked = k.ps(pctx, "l2_masked", [P, 2, 4, CH])

            @block.tensor
            def _(pe):
                with pe.Fori(0, NB // 2) as tt:
                    for u, h in ((u, h) for u in range(2) for h in range(PE0, H2)):
                        jb = tt * 2 + u
                        pe.wait_ge(s_bt, jb * 2 + 2)
                        pe.wait_ge(s_t, jb * ACTH + (h + 4 if h < PE0 + 2 else h + 5))
                        for c in range(NC):
                            pe.matmul(masked[:, h % 2, c, :], eI[:, h - PE0, :], ab[u][:, ds(c * CH, CH)], start=True, stop=False)
                            mm = pe.matmul(masked[:, h % 2, c, :], k.ident_b[:, :], BT[u][:, ds(c * CH, CH)], start=False, stop=True)
                        mm.then_inc(s_sp, 1)

            @block.scalar
            def _(act):
                act.sem_inc(s_t, ACTH)
                with act.Fori(0, NB) as jb:
                    for h in range(1, H2):
                        act.wait_ge(s_r, jb * H2 + h + 1)
                        bias = ad[:, :, :].rearrange("p b h -> p (b h)")[:, ds(jb * H2 + h, 1)]
                        if h < PE0:
                            act.activation(t[:, h % 4, :], k.adj_rows(jb), ACT.Identity, scale=w["L2_eW"][:, h:h + 1], bias=bias).then_inc(s_t, 1)
                        else:
                            act.wait_ge(s_sp, jb * (H2 - PE0) + h - PE0 + 1)
                            k.carry(act, k.act_waits)
                            act.activation(t[:, h % 4, :], masked[:, h % 2, :, :].rearrange("p c i -> p (c i)"), ACT.Identity, bias=bias).then_inc(s_t, 1)

            @block.vector
            def _(v):
                step = k.steps.on(v)
                step(v.memset(R[:, :, :], -BIG))
                v.tensor_scalar(big[:, :], k.ident[:, :], -BIG, None, ALU.mult)
                for h in range(PE0, H2):
                    step(v.tensor_scalar(eI[:, h - PE0, :], k.ident[:, :], w["L2_eW"][:, h:h + 1], None, ALU.mult))
                v.sem_inc(s_r, 4)

                def tiles(jb, u):
                    v.tensor_scalar(BT[u], k.adj_rows(jb), 0.0, -BIG, ALU.is_le, ALU.mult).then_inc(s_bt, 1)
                    v.tensor_copy(ab[u], k.adj_rows(jb)).then_inc(s_bt, 1)

                def compare(jb, u, more):
                    v.wait_ge(s_bt, jb * 2 + 2)
                    v.tensor_scalar(t[:, 0, :], ab[u], w["L2_eW"][:, 0:1], ad[:, :, :].rearrange("p b h -> p (b h)")[:, ds(jb * H2, 1)], ALU.mult, ALU.add).then_inc(s_m, 1)
                    v.wait_ge(s_m, jb * 3 + 1)
                    v.tensor_tensor(t[:, 0, :], t[:, 0, :], BT[u], ALU.add).then_inc(s_m, 1)
                    v.wait_ge(s_t, jb * ACTH + 1 + ACTH)
                    v.tensor_tensor(t[:, 1, :], t[:, 1, :], BT[u], ALU.add).then_inc(s_m, 1)
                    for h in range(2):
                        v.wait_ge(s_m, jb * 3 + h + 2)
                        v.tensor_tensor(R[:, h, :], R[:, h, :], t[:, h, :], ALU.max).then_inc(s_r, 1)
                    for h in range(PE0, H2):
                        if h == 4 and more:
                            tiles(jb + 1, 1 - u)
                        v.wait_ge(s_t, jb * ACTH + h + ACTH)
                        v.tensor_tensor(R[:, h, :], R[:, h, :], t[:, h % 4, :], ALU.max).then_inc(s_r, 1)
                    v.wait_ge(s_r, jb * H2 + H2 + 4)

                tiles(0, 0)
                with v.Fori(0, NB // 2 - 1) as tt:
                    compare(tt * 2, 0, True)
                    compare(tt * 2 + 1, 1, True)
                compare(NB - 2, 0, True)
                compare(NB - 1, 1, False)

        with k.block() as block, ExitStack() as pctx:
            rt = k.ps(pctx, "l2_rt", [P, 2, N], BF16)
            ro = k.ps(pctx, "l2_ro", [P, N], BF16)

            @block.vector
            def _(v):
                step = k.steps.on(v)
                for h in range(H2):
                    v.wait_ge(s_tr, h + 1)
                    step(v.tensor_reduce(mx[:, h, :], rt[:, h % 2, :].rearrange("p (b q) -> p b q", q=P), AX_X, ALU.max))
                    v.sem_inc(s_red, 1)
                mxv = mx[:, :, :].rearrange("p h b -> p b h")
                step(v.tensor_tensor(rest[:, :, :], srcn[:, :, :], mxv, ALU.add))
                step(v.tensor_tensor(rest[:, :, :], rest[:, :, :], row(w["L2_eb"][:, :]), ALU.add))
                step(v.memset(rn, 0.0))
                step(v.scalar_tensor_tensor(rest[:, :, :], rest[:, :, :], 0.2, rest[:, :, :], ALU.mult, ALU.max))
                step(v.tensor_scalar(rn[:, :, 0:H2], rest[:, :, :], -1.0, None, ALU.mult))
                split_bf16(step, v, srcn[:, :, :], [rn[:, :, ds(H2 * (n + 1), H2)] for n in range(3)], rest[:, :, :])
                v.sem_inc(s_rows, 1)
                step(v.tensor_tensor(ad[:, :, :], ad[:, :, :], row(w["L2_eb"][:, :]), ALU.add))
                v.wait_ge(s_rt, NB)
                v.tensor_copy(rows[:, :], ro[:, :])

            @block.tensor
            def _(pe):
                for h in range(H2):
                    if h >= 2:
                        pe.wait_ge(s_red, h - 1)
                    for b in range(NB):
                        mm = pe.transpose(rt[:, h % 2, ds(b * P, P)], R[:, h, ds(b * P, P)], k.ident_b[:, :])
                    mm.then_inc(s_tr, 1)
                pe.wait_ge(s_rows, 1)
                for b in range(NB):
                    pe.transpose(ro[:, ds(b * P, P)], rn[:, b, :], k.ident_b[:, :]).then_inc(s_rt, 1)


def layer2_attend(k, w, V, ad, rows, big, hout):
    with ExitStack() as ctx:
        AS = k.sb(ctx, "l2_AS", [P, N])
        nm = k.sb(ctx, "l2_nm", [P, 2, N], BF16)
        U = k.sb(ctx, "l2_U", [P, 4, HALF])
        Rl = k.sb(ctx, "l2_relu", [P, 2, HALF])
        ad8 = k.sb(ctx, "l2_ad8", [P, NB * H2])
        rden = k.sb(ctx, "l2_rden", [P, NB])
        sel = k.sb(ctx, "l2_sel", [P, 2, H2 * P], BF16)
        selr = U[0:NR, 0:2, :].rearrange("p a i -> p (a i)")
        s_sum = k.sem("l2a_leaky_sum")
        s_sel, s_selc = k.sem("l2a_sel_loaded"), k.sem("l2a_sel_ready")
        Vf = V[:, :, :, :].rearrange("p b h d -> p (b h d)")
        adf = ad[:, :, :].rearrange("p b h -> p (b h)")
        names = ("as_product", "as_ready", "logits", "leaky", "shifted", "exp", "pv", "shift", "mask", "head_summed", "rden", "head_out")
        s_asp, s_as, s_u, s_pre, s_add, s_e, s_pv, s_ps, s_nm, s_hs, s_rd, s_ho = (k.sem("l2a_" + n) for n in names)
        with k.block() as block, ExitStack() as pctx:
            ps = k.ps(pctx, "l2_ps", [P, 2, 2, CH])
            acc = k.ps(pctx, "l2_acc", [P, CH])
            asp = k.ps(pctx, "l2_asp", [P, 2, CH])

            @block.sync
            def _(sp):
                sp.dma_start(selr, k.io["sel_rows"].rearrange("r a n -> r (a n)")).then_inc(s_sel, 16)
                sp.dma_start(k.x[:, :, :], k.x_kept).then_inc(k.s_x_kept, 16)
                sp.wait_ge(k.s_x_kept, 32)
                sp.wait_ge(s_sel, 16)

            @block.gpsimd
            def _(pool):
                with pool.Fori(0, H2) as h:
                    for jb in range(NB):
                        pool.wait_ge(s_ps, h * UNITS + 2 * jb + 2)
                        k.carry(pool, k.pool_waits)
                        pool.tensor_scalar(nm[:, jb % 2, :], k.adj_rows(jb), 0.0, None, ALU.is_le).then_inc(s_nm, 1)

            @block.tensor
            def _(pe):
                pe.wait_ge(s_selc, 4)
                pe.sem_inc(s_ps, 4)
                pe.sem_inc(s_pv, 4)

                def shift(h, t, u):
                    pe.wait_ge(s_nm, h * NB + t * 2 + u // 2 + 1)
                    joined = u % 2 == 0
                    pe.wait_ge(s_add, h * UNITS + t * 4 + u + 1)
                    for q in range(2):
                        i0 = u % 2 * HALF + q * CH
                        pe.matmul(ps[:, u % 2, q, :], sel[:, 0, ds(h * P, P)], rows[:, ds(i0, CH)], start=True, stop=False)
                        mm = pe.matmul(ps[:, u % 2, q, :], big[:, :], nm[:, u // 2 % 2, ds(i0, CH)], start=False, stop=not joined)
                    if joined:
                        pe.wait_ge(s_pre, h * UNITS + t * 4 + u + 1)
                        for q in range(2):
                            mm = pe.matmul(ps[:, u % 2, q, :], k.ident[:, :], Rl[:, u % 2, ds(q * CH, CH)], start=False, stop=True)
                    mm.then_inc(s_ps, 1)

                def weigh(h, t, u):
                    pe.wait_ge(s_e, h * UNITS + t * 4 + u + 1)
                    for b in range(NB // 2):
                        ib = u % 2 * (NB // 2) + b
                        mm = pe.matmul(acc[:, ds(ib * VW, VW)], U[:, u % 4, ds(b * P, P)],
                                       Vf[:, ds(t * (2 * H2 * VW) + u // 2 * (H2 * VW) + h * VW, VW)], start=False, stop=False, skip_group_check=True)
                    mm.then_inc(s_pv, 1)

                with pe.Fori(0, H2) as h:
                    for c in range(NC):
                        pe.wait_ge(s_as, h * NC + c + 1)
                        pe.matmul(asp[:, c % 2, :], sel[:, 1, ds(h * P, P)], rows[:, ds(c * CH, CH)], start=True, stop=True).then_inc(s_asp, 1)
                    pe.wait_ge(s_ho, h + 1)
                    pe.matmul(acc[:, 0:NB * VW], k.zeros[:, 0:P], k.zeros[:, 0:NB * VW], start=True, stop=False, skip_group_check=True)
                    run_ahead(pe, A2[0], h, UNITS // 4, 4, shift, weigh)
                    pe.sem_inc(s_hs, 1)

            @block.scalar
            def _(act):
                act.preload_act_table(ACT.Exp)
                act.sem_inc(s_as, 2)

                def leaky(h, t, u):
                    act.wait_ge(s_u, h * UNITS + t * 4 + u + 2)
                    act.wait_ge(s_add, h * UNITS + t * 4 + u + 1)
                    k.carry(act, k.act_waits)
                    act.activation(Rl[:, u % 2, :], U[:, u % 4, :], ACT.Relu, scale=0.8, bias=ad8[:, ds(t * (2 * H2) + u // 2 * H2 + h, 1)]).then_inc(s_pre, 1)

                def exps(h, t, u):
                    act.wait_ge(s_add, h * UNITS + t * 4 + u + 3)
                    k.carry(act, k.act_waits)
                    act.activation(U[:, u, :], U[:, u, :], ACT.Exp, bias=adf[:, ds(t * (2 * H2) + u // 2 * H2 + h, 1)]).then_inc(s_e, 1)

                with act.Fori(0, H2) as h:
                    act.wait_ge(s_u, h * UNITS + 1)
                    for c in range(NC):
                        act.wait_ge(s_asp, h * NC + c + 1)
                        act.activation(AS[:, ds(c * CH, CH)], asp[:, c % 2, :], ACT.Copy).then_inc(s_as, 1)
                    run_ahead(act, A2[1], h, UNITS // 4, 4, leaky, exps)

            @block.vector
            def _(v):
                v.memset(sel[:, :, :], 0.0).then_inc(s_selc, 1)
                v.wait_ge(s_selc, 1)
                v.wait_ge(s_sel, 16)
                v.tensor_copy(sel[0:NR, :, :].rearrange("r a n -> r (a n)"), selr).then_inc(s_selc, 1)
                v.tensor_scalar(ad8[:, :], adf, 0.8, None, ALU.mult).then_inc(s_selc, 1)
                v.wait_ge(s_selc, 3)
                v.tensor_scalar(adf, adf, 0.2, None, ALU.mult).then_inc(s_selc, 1)
                v.wait_ge(s_selc, 4)
                v.sem_inc(s_u, 1)
                v.sem_inc(s_add, 2)
                v.sem_inc(s_ho, 1)

                def logits(h, t, u):
                    v.wait_ge(s_pv, h * UNITS + t * 4 + u + 1)
                    v.scalar_tensor_tensor(U[:, u % 4, :], k.adjT[:, ds(t * (2 * N) + u // 2 * N + u % 2 * HALF, HALF)],
                                           w["L2_eW"][:, ds(h, 1)], AS[:, ds(u % 2 * HALF, HALF)], ALU.mult, ALU.add).then_inc(s_u, 1)

                def shifted(h, t, u):
                    v.wait_ge(s_pre, h * UNITS + t * 4 + u + 1)
                    shift = ps[:, u % 2, :, :].rearrange("p a c -> p (a c)")
                    if u % 2 == 0:
                        v.wait_ge(s_ps, h * UNITS + t * 4 + u + 5)
                        v.scalar_tensor_tensor(U[:, u, :], U[:, u, :], 0.2, shift, ALU.mult, ALU.add).then_inc(s_add, 1)
                    else:
                        v.scalar_tensor_tensor(U[:, u, :], U[:, u, :], 0.2, Rl[:, u % 2, :], ALU.mult, ALU.add).then_inc(s_sum, 1)
                        v.wait_ge(s_ps, h * UNITS + t * 4 + u + 5)
                        v.wait_ge(s_sum, h * (UNITS // 2) + t * 2 + u // 2 + 1)
                        v.tensor_tensor(U[:, u, :], U[:, u, :], shift, ALU.add).then_inc(s_add, 1)

                with v.Fori(0, H2) as h:
                    v.wait_ge(s_as, h * NC + NC + 2)
                    run_ahead(v, A2[2], h, UNITS // 4, 4, logits, shifted)
                    v.wait_ge(s_pv, h * UNITS + UNITS + 4)
                    av = acc[:, 0:NB * VW].rearrange("p (b d) -> p b d", d=VW)
                    v.reciprocal(rden[:, :], av[:, :, HD]).then_inc(s_rd, 1)
                    v.wait_ge(s_rd, h + 1)
                    v.tensor_tensor(hout[:, :, ds(h * HD, HD)], av[:, :, 0:HD], per_block(rden[:, :], HD), ALU.mult).then_inc(s_ho, 1)


def layer2_fuse(k, w, hout):
    with ExitStack() as ctx:
        hoT = k.sb(ctx, "l2_hoT", [P, N])
        y = k.sb(ctx, "l2_y", [P, NB, D])
        cen = k.sb(ctx, "l2_cen", [P, NB, D])
        mean, var, std = (k.sb(ctx, "l2f_" + n, [P, NB]) for n in ("mean", "var", "std"))
        s_tr, s_hoT, s_y, s_yb, s_var, s_std = (k.sem("l2f_" + n) for n in ("turned", "hoT", "product", "biased", "var", "std"))
        with k.block() as block, ExitStack() as pctx:
            tr = k.ps(pctx, "l2f_tr", [P, 4, CH])
            yp = k.ps(pctx, "l2f_yp", [P, 4, CH])

            @block.tensor
            def _(pe):
                for b in range(NB):
                    pe.transpose(tr[:, b // 4, ds(b % 4 * P, P)], hout[:, b, :], k.ident[:, :]).then_inc(s_tr, 1)
                for b in range(NB):
                    pe.wait_ge(s_hoT, b // 4 + 1)
                    pe.matmul(yp[:, b // 4, ds(b % 4 * P, P)], hoT[:, ds(b * P, P)], w["L2_fuse_WT"][:, :], start=True, stop=True).then_inc(s_y, 1)

            @block.scalar
            def _(act):
                for c in range(NC):
                    act.wait_ge(s_tr, 4 * c + 4)
                    act.activation(hoT[:, ds(c * CH, CH)], tr[:, c, :], ACT.Copy).then_inc(s_hoT, 1)
                act.wait_ge(s_var, 1)
                act.activation(std[:, :], var[:, :], ACT.Sqrt, bias=k.eps[:, :], scale=1.0 / D).then_inc(s_std, 1)

            @block.vector
            def _(v):
                step = k.steps.on(v)
                for c in range(4):
                    v.wait_ge(s_y, 4 * c + 4)
                    step(v.tensor_tensor(y[:, 4 * c:4 * c + 4, :], yp[:, c, :].rearrange("p (b f) -> p b f", f=D), row(w["L2_fuse_b"][:, :], 4), ALU.add))
                center_and_sum(v, step, y[:, :, :], cen[:, :, :], y[:, :, :], mean[:, :], var[:, :])
                v.sem_inc(s_var, 1)
                v.wait_ge(s_std, 1)
                step(v.reciprocal(var[:, :], std[:, :]))
                step(v.tensor_tensor(cen[:, :, :], cen[:, :, :], per_block(var[:, :]), ALU.mult))
                step(v.tensor_tensor(cen[:, :, :], cen[:, :, :], row(w["L2_ln_g"][:, :]), ALU.mult))
                step(v.tensor_tensor(cen[:, :, :], cen[:, :, :], row(w["L2_ln_b"][:, :]), ALU.add))
                step(v.scalar_tensor_tensor(k.x[:, :, :], cen[:, :, :], 0.0, k.x[:, :, :], ALU.max, ALU.add))


NQ = 2 * 3 * H3
UN3 = NB * NC
TINY = 1e-37


def layer3(k):
    with ExitStack() as ctx:
        gru_w = lambda a: [("L3_%s_%s" % (a, n), s) for n, s in (("WihT", [D, 3 * D]), ("WhhT", [D, 3 * D]), ("bih", [D, 3]), ("bhh", [D, 3]))]
        w = load_weights(k, ctx, [("L3_gat_W", [D, H3, D])] + gru_w("node"))
        hT = k.sb(ctx, "l3_hT", [P, N])
        dg = k.sb(ctx, "l3_diag", [P, NB])
        gru_sems = [k.sem("gru_" + n) for n in ("bias", "gates", "r", "z", "n_arg", "n", "freed", "out", "turned", "added")]
        e2 = k.sb(ctx, "l3_e", [P, NB, 2, H3])
        with ExitStack() as c1:
            w.update(load_weights(k, c1, [("L3_gat_WT", [D, H3, D]), ("L3_gat_a", [D, H3, 2])] + gru_w("edge")))
            q2 = k.sb(c1, "l3_q", [P, 2, NB, NQ], BF16)
            nsT = k.sb(c1, "l3_nsT", [P, N])
            with ExitStack() as c2:
                h = k.sb(c2, "l3_h", [P, NB, D])
                work = k.sb(c2, "l3_work", [P, NB, D])
                normed_and_turned(k, "l3_", w, h[:, :, :], hT, work[:, :, :])
                layer3_prepare(k, w, h, hT, work, dg, q2, nsT)
            gru(k, "l3e_", w, "L3_edge_", nsT, hT, dg, gru_sems, 0)
            layer3_scores(k, q2, e2)
        rows = k.sb(ctx, "l3_rows", [P, N], BF16)
        sel = k.sb(ctx, "l3_sel", [P, H3 * P], BF16)
        big = k.sb(ctx, "l3_big", [P, P], BF16)
        layer3_maxima(k, e2, rows, sel, big)
        with ExitStack() as c1:
            es = k.sb(c1, "l3_es", [P, NB, D])
            layer3_attend(k, w, hT, e2, rows, sel, big, es)
            layer3_turn(k, es)
            gru(k, "l3n_", w, "L3_node_", es[:, :, :].rearrange("p b f -> p (b f)"), hT, dg, gru_sems, NC)


def layer3_prepare(k, w, h, hT, work, dg, q2, nsT):
    with ExitStack() as ctx:
        wa = k.sb(ctx, "l3_wa", [D, 2 * H3])
        q = k.sb(ctx, "l3_qn", [P, NB, 2 * H3])
        qr = k.sb(ctx, "l3_qr", [P, NB, 2 * H3])
        s_dg, s_wap, s_wa, s_qp, s_ns, s_nsc = (k.sem("l3p_" + n) for n in ("diag_out", "wa_product", "wa", "q_product", "ns_product", "nsT"))
        with k.block() as block, ExitStack() as pctx:
            nsp = k.ps(pctx, "l3_nsp", [P, 4, CH])
            wap = k.ps(pctx, "l3_wap", [P, CH])
            qp = k.ps(pctx, "l3_qp", [P, CH])
            STEP = N + P
            head = k.adjT[:, 0:(NB - 1) * STEP].rearrange("p (b r) -> p b r", r=STEP)[:, :, 0:P]
            tail = k.adjT[:, (NB - 1) * STEP:]

            @block.vector
            def _(v):
                step = k.steps.on(v)
                step(v.tensor_tensor(work[:, 0:NB - 1, :], head, row(k.ident[:, :], NB - 1), ALU.mult))
                step(v.tensor_tensor(work[:, NB - 1, :], tail, k.ident[:, :], ALU.mult))
                step(v.tensor_reduce(dg[:, :], work[:, :, :], AX_X, ALU.add))
                step(v.tensor_tensor(head, head, work[:, 0:NB - 1, :], ALU.subtract))
                v.tensor_tensor(tail, tail, work[:, NB - 1, :], ALU.subtract).then_inc(s_dg, 1)
                v.wait_ge(s_wap, 1)
                v.tensor_copy(wa[:, :], wap[:, 0:2 * H3]).then_inc(s_wa, 1)
                v.wait_ge(s_qp, 1)
                step(v.tensor_copy(q[:, :, :], qp[:, 0:NB * 2 * H3].rearrange("p (b q) -> p b q", q=2 * H3)))
                parts = lambda s: [q2[:, s, :, :].rearrange("p b (s r h) -> p b s r h", s=2, r=3)[:, :, :, r, :] for r in range(3)]
                qv, rv = (t[:, :, :].rearrange("p b (s h) -> p b s h", s=2) for t in (q, qr))
                split_bf16(step, v, qv, parts(0), rv)
                n3 = NQ // 2
                step(v.tensor_copy(q2[:, 1, :, 0:n3], q2[:, 0, :, n3:]))
                step(v.tensor_copy(q2[:, 1, :, n3:], q2[:, 0, :, 0:n3]))

            @block.tensor
            def _(pe):
                for n in range(H3):
                    mm = pe.matmul(wap[:, 0:2 * H3].rearrange("p (a h) -> p h a", a=2)[:, n, :], w["L3_gat_WT"][:, n, :], w["L3_gat_a"][:, n, :], start=True, stop=True)
                mm.then_inc(s_wap, 1)
                pe.wait_ge(s_dg, 1)
                for c in range(NC):
                    for jb in range(NB):
                        mm = pe.matmul(nsp[:, c, :], h[:, jb, :], k.adj_rows(jb, c * CH, CH), start=jb == 0, stop=jb == NB - 1)
                    mm.then_inc(s_ns, 1)
                    if c == 0:
                        pe.wait_ge(s_wa, 1)
                        for b in range(NB):
                            mm = pe.matmul(qp[:, ds(b * 2 * H3, 2 * H3)], hT[:, ds(b * P, P)], wa[:, :], start=True, stop=True)
                        mm.then_inc(s_qp, 1)

            @block.scalar
            def _(act):
                for c in range(NC):
                    act.wait_ge(s_ns, c + 1)
                    act.activation(nsT[:, ds(c * CH, CH)], nsp[:, c, :], ACT.Copy).then_inc(s_nsc, 1)


def gru(k, tag, w, name, xT, hT, dg, sems, done):
    wi, wh, bi, bh = (w[name + n] for n in ("WihT", "WhhT", "bih", "bhh"))
    with ExitStack() as ctx:
        r, z, m, o = (k.sb(ctx, tag + n, [P, CH]) for n in ("r", "z", "m", "o"))
        b2 = k.sb(ctx, tag + "b2", [P, 2])
        s_b, s_g, s_r, s_z, s_na, s_n, s_free, s_o, s_tr, s_add = sems
        with k.block() as block, ExitStack() as pctx:
            gp = k.ps(pctx, tag + "gp", [P, 4, CH])
            tp = k.ps(pctx, tag + "tp", [P, CH])

            @block.tensor
            def _(pe):
                with pe.Fori(0, NC) as c:
                    i = ds(c * CH, CH)
                    pe.wait_ge(s_free, c + done + 1)
                    for g in range(2):
                        pe.matmul(gp[:, g, :], wi[:, ds(g * D, D)], xT[:, i], start=True, stop=False)
                        pe.matmul(gp[:, g, :], wh[:, ds(g * D, D)], hT[:, i], start=False, stop=True).then_inc(s_g, 1)
                    pe.matmul(gp[:, 3, :], wh[:, ds(2 * D, D)], hT[:, i], start=True, stop=True).then_inc(s_g, 1)
                    pe.matmul(gp[:, 2, :], wi[:, ds(2 * D, D)], xT[:, i], start=True, stop=True).then_inc(s_g, 1)
                    pe.wait_ge(s_o, c + done + 1)
                    for b in range(4):
                        mm = pe.transpose(tp[:, ds(b * P, P)], o[:, ds(b * P, P)], k.ident[:, :])
                    mm.then_inc(s_tr, 1)

            @block.scalar
            def _(act):
                act.preload_act_table(ACT.Sigmoid)
                act.wait_ge(s_b, done // NC + 1)
                with act.Fori(0, NC) as c:
                    act.wait_ge(s_g, (c + done) * 4 + 1)
                    act.activation(r[:, :], gp[:, 0, :], ACT.Sigmoid, bias=b2[:, 0:1]).then_inc(s_r, 1)
                    act.wait_ge(s_g, (c + done) * 4 + 2)
                    act.activation(z[:, :], gp[:, 1, :], ACT.Sigmoid, bias=b2[:, 1:2]).then_inc(s_z, 1)
                    act.wait_ge(s_na, c + done + 1)
                    act.activation(m[:, :], m[:, :], ACT.Tanh, bias=bi[:, 2:3]).then_inc(s_n, 1)

            @block.vector
            def _(v):
                step = k.steps.on(v)
                v.tensor_tensor(b2[:, :], bi[:, 0:2], bh[:, 0:2], ALU.add).then_inc(s_b, 1)
                if not done:
                    v.sem_inc(s_free, 1)
                first, PER = step.n, 5
                with v.Fori(0, NC) as c:
                    step.begin(c, PER)
                    v.wait_ge(s_r, c + done + 1)
                    v.wait_ge(s_g, (c + done) * 4 + 3)
                    step(v.scalar_tensor_tensor(m[:, :], gp[:, 3, :], bh[:, 2:3], r[:, :], ALU.add, ALU.mult))
                    v.wait_ge(s_g, (c + done) * 4 + 4)
                    step(v.tensor_tensor(m[:, :], m[:, :], gp[:, 2, :], ALU.add))
                    v.sem_inc(s_na, 1)
                    v.wait_ge(s_n, c + done + 1)
                    v.wait_ge(s_z, c + done + 1)
                    step(v.tensor_tensor(o[:, :], hT[:, ds(c * CH, CH)], m[:, :], ALU.subtract))
                    step(v.tensor_tensor(o[:, :], o[:, :], z[:, :], ALU.mult))
                    step(v.tensor_tensor(o[:, :], o[:, :], m[:, :], ALU.add))
                    step.end(NC, first, PER)
                    v.sem_inc(s_o, 1)
                    v.sem_inc(s_free, 1)
                    v.wait_ge(s_tr, c + done + 1)
                    for b in range(4):
                        xb = k.x[:, :, :].rearrange("p b f -> p (b f)")[:, ds(c * CH + b * P, P)]
                        v.scalar_tensor_tensor(xb, tp[:, ds(b * P, P)], dg[:, ds(c * 4 + b, 1)], xb, ALU.mult, ALU.add).then_inc(s_add, 1)
                    v.wait_ge(s_add, (c + done) * 4 + 4)


def layer3_scores(k, q2, e2):
    with ExitStack() as ctx:
        mk = k.sb(ctx, "l3_mask", [P, 2, 2, N], BF16)
        eq = k.sb(ctx, "l3_eq", [P, NB, 2, 3, H3])
        s_m, s_p = (k.sem("l3s_" + n) for n in ("masks", "summed"))
        with k.block() as block, ExitStack() as pctx:
            ep = k.ps(pctx, "l3_ep", [P, CH])
            qf = q2[:, :, :, :].rearrange("p s b q -> p (s b q)")

            @block.vector
            def _(v):
                step = k.steps.on(v)
                v.sem_inc(s_p, 2)
                with v.Fori(0, NB // 2) as t:
                    for u in range(2):
                        v.wait_ge(s_p, t * 2 + u + 1)
                        v.tensor_scalar(mk[:, u, 0, :], k.adj_rows(t * 2 + u), 0.0, None, ALU.is_gt).then_inc(s_m, 1)
                        v.tensor_scalar(mk[:, u, 1, :], k.adj_rows(t * 2 + u), 0.0, None, ALU.is_lt).then_inc(s_m, 1)
                v.wait_ge(s_p, NB + 2)
                step(v.tensor_copy(eq[:, :, :, :, :].rearrange("p b s r h -> p (b s r h)"), ep[:, 0:NB * NQ]))
                step(v.tensor_tensor(e2[:, :, :, :], eq[:, :, :, 2, :], eq[:, :, :, 1, :], ALU.add))
                step(v.tensor_tensor(e2[:, :, :, :], e2[:, :, :, :], eq[:, :, :, 0, :], ALU.add))
                ef = e2[:, :, :, :].rearrange("p b s h -> p (b s h)")
                step(v.scalar_tensor_tensor(ef, ef, 0.2, ef, ALU.mult, ALU.max))

            @block.tensor
            def _(pe):
                pe.matmul(ep[:, 0:NB * NQ], k.zeros[:, 0:P], k.zeros[:, 0:NB * NQ], start=True, stop=False, skip_group_check=True)
                with pe.Fori(0, NB // 2) as t:
                    for u in range(2):
                        pe.wait_ge(s_m, t * 4 + 2 * u + 2)
                        for b in range(NB):
                            for sign in range(2):
                                mm = pe.matmul(ep[:, ds(b * NQ, NQ)], mk[:, u, sign, ds(b * P, P)], qf[:, ds(t * (2 * NQ) + u * NQ + sign * NB * NQ, NQ)],
                                               start=False, stop=False, skip_group_check=True)
                        mm.then_inc(s_p, 1)


def layer3_maxima(k, e2, rows, sel, big):
    with ExitStack() as ctx:
        R = k.sb(ctx, "l3_R", [P, H3, N], BF16)
        t = k.sb(ctx, "l3_t", [P, 2, H3, N], BF16)
        BT = k.sb(ctx, "l3_BT", [P, 2, N], BF16)
        mx = k.sb(ctx, "l3_mx", [P, H3, NB])
        rn = BT[:, 0, :].rearrange("p (b r) -> p b r", r=P)
        selr = k.sb(ctx, "l3_selr", [H3, H3 * P])
        s_sel, s_bt, s_t, s_m, s_tr, s_rows, s_rt = (k.sem("l3m_" + n) for n in ("sel", "masks", "logits", "maxed", "turned", "rows", "rows_turned"))
        ef = e2[:, :, :, :].rearrange("p b s h -> p (b s h)")
        with k.block() as block, ExitStack() as pctx:
            rt = k.ps(pctx, "l3_rt", [P, H3, N], BF16)
            ro = k.ps(pctx, "l3_ro", [P, N], BF16)

            @block.sync
            def _(sp):
                sp.dma_start(selr[:, :], k.io["sel_rows3"]).then_inc(s_sel, 16)
                sp.wait_ge(s_sel, 16)

            @block.scalar
            def _(act):
                with act.Fori(0, NB) as jb:
                    for h in range(H3):
                        act.wait_ge(s_bt, jb * 2 + 1)
                        act.wait_ge(s_m, jb * H3 + h + 1)
                        k.carry(act, k.act_waits)
                        act.activation(t[:, 0, h, :], BT[:, 0, :], ACT.Identity, bias=ef[:, ds(jb * (2 * H3) + h, 1)]).then_inc(s_t, 1)

            @block.vector
            def _(v):
                step = k.steps.on(v)
                step(v.memset(sel[:, :], 0.0))
                v.wait_ge(s_sel, 16)
                step(v.tensor_copy(sel[0:H3, :], selr[:, :]))
                step(v.tensor_scalar(big[:, :], k.ident[:, :], -BIG, None, ALU.mult))
                step(v.memset(R[:, :, :], -BIG))
                v.sem_inc(s_m, 3)
                first, PER = step.n, 2 * H3
                with v.Fori(0, NB) as jb:
                    step.begin(jb, PER)
                    v.tensor_scalar(BT[:, 0, :], k.adj_rows(jb), 0.0, -BIG, ALU.is_le, ALU.mult).then_inc(s_bt, 1)
                    v.tensor_scalar(BT[:, 1, :], k.adj_rows(jb), 0.0, -BIG, ALU.is_ge, ALU.mult).then_inc(s_bt, 1)
                    v.wait_ge(s_bt, jb * 2 + 2)
                    for h in range(H3):
                        step(v.tensor_scalar(t[:, 1, h, :], BT[:, 1, :], ef[:, ds(jb * (2 * H3) + H3 + h, 1)], None, ALU.add))
                    for h in range(H3):
                        step(v.tensor_tensor(R[:, h, :], R[:, h, :], t[:, 1, h, :], ALU.max))
                    for h in range(H3):
                        v.wait_ge(s_t, jb * H3 + h + 1)
                        v.tensor_tensor(R[:, h, :], R[:, h, :], t[:, 0, h, :], ALU.max).then_inc(s_m, 1)
                    v.wait_ge(s_m, jb * H3 + H3 + 3)
                    step.end(NB, first, PER)
                for h in range(H3):
                    v.wait_ge(s_tr, h + 1)
                    step(v.tensor_reduce(mx[:, h, :], rt[:, h, :].rearrange("p (b q) -> p b q", q=P), AX_X, ALU.max))
                step(v.memset(rn, 0.0))
                mf = mx[:, :, :].rearrange("p h b -> p (h b)")
                step(v.scalar_tensor_tensor(mf, mf, -0.5 * BIG, mf, ALU.is_gt, ALU.mult))
                step(v.tensor_scalar(rn[:, :, 0:H3].rearrange("p b h -> p h b"), mx[:, :, :], -1.0, None, ALU.mult))
                v.sem_inc(s_rows, 1)
                v.wait_ge(s_rt, NB)
                v.tensor_copy(rows[:, :], ro[:, :])

            @block.tensor
            def _(pe):
                pe.wait_ge(s_m, NB * H3 + 3)
                for h in range(H3):
                    for b in range(NB):
                        mm = pe.transpose(rt[:, h, ds(b * P, P)], R[:, h, ds(b * P, P)], k.ident_b[:, :])
                    mm.then_inc(s_tr, 1)
                pe.wait_ge(s_rows, 1)
                for b in range(NB):
                    pe.transpose(ro[:, ds(b * P, P)], rn[:, b, :], k.ident_b[:, :]).then_inc(s_rt, 1)


def layer3_attend(k, w, hT, e2, rows, sel, big, es):
    with ExitStack() as ctx:
        hW = k.sb(ctx, "l3_hW", [P, NB * D])
        mk = k.sb(ctx, "l3_mk", [P, 2, 2, N], BF16)
        U = k.sb(ctx, "l3_U", [P, 4, CH])
        W = k.sb(ctx, "l3_W", [P, 4, CH])
        rden = k.sb(ctx, "l3_rden", [P, NB])
        de = k.sb(ctx, "l3_de", [P, NB, H3])
        ones = k.sb(ctx, "l3_ones", [P, 1])
        part = W[:, :, :].rearrange("p c (r f) -> p (c r) f", f=D)
        ef = e2[:, :, :, :].rearrange("p b s h -> p (b s h)")
        df = de[:, :, :].rearrange("p b h -> p (b h)")
        names = ("init", "hW_product", "hW", "mask", "negative", "shift", "logits", "exp", "weighed", "summed", "head_summed", "head_out")
        s_i, s_hp, s_hw, s_mk, s_mn, s_ps, s_u, s_e, s_w, s_pv, s_hs, s_ho = (k.sem("l3a_" + n) for n in names)
        with k.block() as block, ExitStack() as pctx:
            ps = k.ps(pctx, "l3_ps", [P, 2, CH])
            acc = k.ps(pctx, "l3_acc", [P, 6, CH])

            @block.gpsimd
            def _(pool):
                with pool.Fori(0, H3) as h:
                    for jb in range(NB):
                        pool.wait_ge(s_ps, h * UN3 + 4 * jb + 4)
                        k.carry(pool, k.pool_waits)
                        pool.tensor_scalar(mk[:, jb % 2, 0, :], k.adj_rows(jb), 0.0, None, ALU.is_equal).then_inc(s_mk, 1)

            @block.tensor
            def _(pe):
                pe.sem_inc(s_ps, 8)
                pe.sem_inc(s_pv, 4)

                def shift(h, t, n):
                    pe.wait_ge(s_mk, h * NB + t * 2 + n // 4 + 1)
                    pe.wait_ge(s_u, h * UN3 + t * 8 + n + 7)
                    i = ds(n % 4 * CH, CH)
                    pe.matmul(ps[:, n % 2, :], sel[:, ds(h * P, P)], rows[:, i], start=True, stop=False)
                    pe.matmul(ps[:, n % 2, :], big[:, :], mk[:, n // 4 % 2, 0, i], start=False, stop=True).then_inc(s_ps, 1)

                def weigh(h, t, n):
                    pe.wait_ge(s_e, h * UN3 + t * 8 + n + 1)
                    for b in range(4):
                        ib = n % 4 * 4 + b
                        pe.matmul(acc[:, ib // ROWB, ds(ib % ROWB * (D + 1) + D, 1)], U[:, n % 4, ds(b * P, P)], ones[:, :], start=False, stop=False, skip_group_check=True)
                    pe.wait_ge(s_w, h * UN3 + t * 8 + n + 1)
                    for b in range(4):
                        ib = n % 4 * 4 + b
                        mm = pe.matmul(acc[:, ib // ROWB, ds(ib % ROWB * (D + 1), D)], W[:, n % 4, ds(b * P, P)], hW[:, ds(t * (2 * D) + n // 4 * D, D)],
                                       start=False, stop=False, skip_group_check=True)
                    mm.then_inc(s_pv, 1)

                pe.wait_ge(s_i, 2)
                with pe.Fori(0, H3) as h:
                    wk = w["L3_gat_W"][:, :, :].rearrange("p h f -> p (h f)")[:, ds(h * D, D)]
                    for c in range(4):
                        pe.wait_ge(s_hw, h * 4 + c + 1)
                        pe.wait_ge(s_u, h * UN3 + 8)
                        for b in range(4):
                            mm = pe.matmul(ps[:, c % 2, ds(b * P, P)], hT[:, ds((4 * c + b) * P, P)], wk, start=True, stop=True)
                        mm.then_inc(s_hp, 1)
                    pe.wait_ge(s_hw, h * 4 + 4 + 2)
                    pe.wait_ge(s_ho, h + 1)
                    for b in range(6):
                        pe.matmul(acc[:, b, 0:ROWB * (D + 1)], k.zeros[:, 0:P], k.zeros[:, 0:ROWB * (D + 1)], start=True, stop=False, skip_group_check=True)
                    run_ahead(pe, 2, h, UN3 // 8, 8, shift, weigh)
                    pe.sem_inc(s_hs, 1)

            @block.scalar
            def _(act):
                act.preload_act_table(ACT.Exp)
                act.sem_inc(s_hw, 2)
                with act.Fori(0, H3) as h:
                    for c in range(4):
                        act.wait_ge(s_hp, h * 4 + c + 1)
                        act.wait_ge(s_pv, h * UN3 + 4)
                        act.activation(hW[:, ds(c * CH, CH)], ps[:, c % 2, :], ACT.Copy).then_inc(s_hw, 1)
                    with act.Fori(0, UN3 // 8) as t:
                        for n in range(8):
                            act.wait_ge(s_u, h * UN3 + t * 8 + n + 9)
                            k.carry(act, k.act_waits)
                            act.activation(U[:, n % 4, :], U[:, n % 4, :], ACT.Exp, bias=ef[:, ds(t * (4 * H3) + n // 4 * (2 * H3) + h, 1)]).then_inc(s_e, 1)

            @block.vector
            def _(v):
                step = k.steps.on(v)
                step(v.memset(es[:, :, :], 0.0))
                v.memset(ones[:, :], 1.0).then_inc(s_i, 1)
                step(v.tensor_tensor(de[:, :, :], e2[:, :, 1, :], e2[:, :, 0, :], ALU.subtract))
                v.sem_inc(s_i, 1)
                v.sem_inc(s_u, 8)
                v.sem_inc(s_ho, 1)

                def logits(h, t, n):
                    if n % 4 == 0:
                        v.tensor_scalar(mk[:, n // 4, 1, :], k.adj_rows(t * 2 + n // 4), 0.0, None, ALU.is_lt).then_inc(s_mn, 1)
                        v.wait_ge(s_mn, h * NB + t * 2 + n // 4 + 1)
                    v.wait_ge(s_pv, h * UN3 + t * 8 + n + 1)
                    v.wait_ge(s_ps, h * UN3 + t * 8 + n + 9)
                    v.scalar_tensor_tensor(U[:, n % 4, :], mk[:, n // 4, 1, ds(n % 4 * CH, CH)], df[:, ds(t * (2 * H3) + n // 4 * H3 + h, 1)],
                                           ps[:, n % 2, :], ALU.mult, ALU.add).then_inc(s_u, 1)

                def weighed(h, t, n):
                    v.wait_ge(s_e, h * UN3 + t * 8 + n + 1)
                    v.tensor_tensor(W[:, n % 4, :], U[:, n % 4, :], k.adjT[:, ds(t * (2 * N) + n * CH, CH)], ALU.mult).then_inc(s_w, 1)

                first, PER = step.n, 6
                with v.Fori(0, H3) as h:
                    step.begin(h, PER)
                    run_ahead(v, 1, h, UN3 // 8, 8, logits, weighed)
                    v.wait_ge(s_pv, h * UN3 + UN3 + 4)
                    av = acc[:, :, 0:ROWB * (D + 1)].rearrange("p b (r f) -> p b r f", f=D + 1)
                    rv = rden[:, 0:15].rearrange("p (b r) -> p b r", r=ROWB)
                    step(v.tensor_scalar(rv, av[:, 0:5, :, D], TINY, None, ALU.max))
                    step(v.tensor_scalar(rden[:, 15:16], av[:, 5, 0:1, D], TINY, None, ALU.max))
                    step(v.reciprocal(rden[:, :], rden[:, :]))
                    step(v.tensor_tensor(part[:, 0:15, :].rearrange("p (b r) f -> p b r f", r=ROWB), av[:, 0:5, :, 0:D], rv.unsqueeze(3).broadcast_to([P, 5, ROWB, D]), ALU.mult))
                    step(v.tensor_scalar(part[:, 15, :], av[:, 5, 0, 0:D], rden[:, 15:16], None, ALU.mult))
                    v.sem_inc(s_ho, 1)
                    step(v.scalar_tensor_tensor(es[:, :, :], part[:, :, :], 1.0 / H3, es[:, :, :], ALU.mult, ALU.add))
                    step.end(H3, first, PER)


def layer3_turn(k, es):
    s_tr, s_c = k.sem("l3t_turned"), k.sem("l3t_copied")
    with k.block() as block, ExitStack() as pctx:
        tr = k.ps(pctx, "l3t_tr", [P, 4, CH])

        @block.tensor
        def _(pe):
            for b in range(NB):
                pe.transpose(tr[:, b // 4, ds(b % 4 * P, P)], es[:, b, :], k.ident[:, :]).then_inc(s_tr, 1)

        @block.scalar
        def _(act):
            for c in range(NC):
                act.wait_ge(s_tr, 4 * c + 4)
                act.activation(es[:, 4 * c:4 * c + 4, :], tr[:, c, :].rearrange("p (b f) -> p b f", f=D), ACT.Copy).then_inc(s_c, 1)


def stage_store(k):
    s_out = k.sem("out_stored")
    with k.block() as block:

        @block.sync
        def _(sp):
            sp.dma_start(k.io["out"].rearrange("(b p) f -> p b f", p=P), k.x[:, :, :]).then_inc(s_out, 16)
            sp.wait_ge(s_out, 16)


def build(nc, io):
    with ExitStack() as ctx:
        k = Core(nc, io, ctx)
        stage_start(k)
        if 0 in LAYERS:
            layer0(k)
        if 1 in LAYERS:
            layer1(k)
        if 2 in LAYERS:
            layer2(k)
        if 3 in LAYERS:
            layer3(k)
        stage_store(k)


def selectors():
    s = np.zeros((4, H2, 2, H2, P), np.float32)
    for h in range(H2):
        s[0, h, 0, h, :] = 1.0
        s[1:, h, 1, h, :] = 1.0
    return s.reshape(NR, 2, H2 * P)


def _laid_out(inp):
    f = lambda n: np.asarray(inp[n])
    c = np.ascontiguousarray
    halves = lambda a: c(np.moveaxis(a.reshape(CB, P, *a.shape[1:]), 0, 1))
    return {
        "x": c(f("x")), "adjT": c(f("adj").T),
        "ident": np.eye(P, dtype=np.float32),
        "L2_WT": c(f("L2_gnn_W").T), "L2_src": f("L2_gnn_attn_src").reshape(D, 1), "L2_dst": f("L2_gnn_attn_dst").reshape(D, 1),
        "head_mask": np.repeat(np.eye(H2, dtype=np.float32), HD, axis=0), "sel_rows": selectors(),
        "L2_eW": f("L2_gnn_edge_W").reshape(H2), "L2_eb": f("L2_gnn_edge_b"), "L2_fuse_WT": c(f("L2_gnn_fuse_W").T),
        "L2_fuse_b": f("L2_gnn_fuse_b"), "L2_ln_g": f("L2_gnn_ln_g"), "L2_ln_b": f("L2_gnn_ln_b"),
        "L3_gat_W": c(f("L3_gnn_gat_W").transpose(1, 0, 2)), "L3_gat_WT": c(f("L3_gnn_gat_W").transpose(2, 0, 1)),
        "L3_gat_a": c(f("L3_gnn_gat_a").reshape(H3, 2, D).transpose(2, 0, 1)),
        "sel_rows3": np.repeat(np.eye(H3, dtype=np.float32), P, axis=1),
        **{"L3_%s_W%sT" % (a, b): c(f("L3_gnn_%s_W%s" % (a, b)).T) for a in ("edge", "node") for b in ("ih", "hh")},
        **{"L3_%s_b%s" % (a, b): c(f("L3_gnn_%s_b%s" % (a, b)).reshape(3, D).T) for a in ("edge", "node") for b in ("ih", "hh")},
        "L1_gcn_w": c(f("L1_gnn_gcn_w")), "L1_gcn_b": c(f("L1_gnn_gcn_b")), "L1_w_in": c(f("L1_gnn_w_in")),
        "L1_w_xp": halves(f("L1_gnn_w_xp")), "L1_w_dt": c(f("L1_gnn_w_dt")), "L1_w_out": halves(f("L1_gnn_w_out")),
        "L1_A_log": halves(f("L1_gnn_A_log")).reshape(P, CB * DS), "L1_conv_w": halves(f("L1_gnn_conv_w")),
        "L1_conv_b": halves(f("L1_gnn_conv_b")), "L1_b_dt": halves(f("L1_gnn_b_dt")), "L1_D": halves(f("L1_gnn_D_skip")),
        "L1_ln_g": f("L1_gnn_ln_g").reshape(D, 1), "L1_ln_b": f("L1_gnn_ln_b").reshape(D, 1),
        "L0_WT": c(f("L0_gnn_W").T), "L0_bias": c(f("L0_gnn_bias")), "L0_b": c(f("L0_gnn_b")),
    }


def kernel(**inputs):
    import concourse.bacc as bacc
    from concourse.bass_utils import run_bass_kernel_spmd as run

    arrays = _laid_out(inputs)
    nc = bacc.Bacc("TRN2", target_bir_lowering=False, num_devices=1)
    io = {n: nc.dram_tensor("in_" + n, a.shape, mybir.dt.from_np(a.dtype), kind="ExternalInput").ap() for n, a in arrays.items()}
    io["out"] = nc.dram_tensor("out_x", (N, D), F32, kind="ExternalOutput").ap()
    build(nc, io)
    r = run(nc, [{"in_" + n: a for n, a in arrays.items()}], core_ids=[0])
    return r.results[0]["out_x"]
```

```python
from contextlib import ExitStack

import numpy as np

import concourse.bass as bass
from concourse import mybir

ALU = mybir.AluOpType
ACT = mybir.ActivationFunctionType
F32 = mybir.dt.float32
BF16 = mybir.dt.bfloat16
AX_X = mybir.AxisListType.X
ds = bass.ds

P = 128
N = 2048
D = 128
NB = N // P
CH = 512
NC = N // CH
EPS = 1e-5
DI = 256
CB = DI // P
DS = 16
DTR = 8
KC = 4
XP = DTR + 2 * DS
H2 = 8
HD = D // H2
H3 = 3
BIG = 1e30
ROWB = 3


class Steps:

    def __init__(self, eng, sem):
        self.eng, self.sem, self.n, self.turn = eng, sem, 0, 0

    def __call__(self, ins):
        ins.then_inc(self.sem, 1)
        self.n += 1
        self.eng.wait_ge(self.sem, self.turn + self.n)

    def begin(self, turn_index, per_turn):
        self.turn = turn_index * per_turn

    def on(self, eng):
        self.eng = eng
        return self

    def end(self, turns, start, per_turn):
        assert self.n - start == per_turn, (self.n, start, per_turn)
        self.n = start + turns * per_turn
        self.turn = 0


class Core:

    def __init__(self, nc, io, ctx):
        self.nc, self.io, self.ctx = nc, io, ctx
        self.adjT = self.sb(ctx, "adjT", [P, NB * N])
        self.x = self.sb(ctx, "x_nat", [P, NB, D])
        self.ident = self.sb(ctx, "ident", [P, P])
        self.ident_b = self.sb(ctx, "ident_b", [P, P], BF16)
        self.zeros = self.sb(ctx, "zeros", [P, CH], BF16)
        self.eps = self.sb(ctx, "eps", [P, 1])
        self.x_kept = nc.dram_tensor("x_kept", (P, NB, D), F32, kind="Internal").ap()
        self.s_x_kept, self.s_x_stored = self.sem("x_kept"), self.sem("x_kept_again")
        self.adj_even = self.sem("adj_even")
        self.adj_odd = self.sem("adj_odd")
        self.steps = Steps(None, self.sem("dve_steps"))
        self.norm_sems, self.normed = [self.sem("norm_" + n) for n in ("var", "std", "h", "turned", "hT")], 0
        self.act_waits = self.sem("act_waits_carried")
        self.pool_waits = self.sem("pool_waits_carried")

    def sb(self, ctx, name, shape, dt=F32):
        return ctx.enter_context(self.nc.sbuf_tensor(name, shape, dt))

    def ps(self, ctx, name, shape, dt=F32):
        return ctx.enter_context(self.nc.psum_tensor(name, shape, dt))

    def sem(self, name):
        return self.ctx.enter_context(self.nc.semaphore(name))

    def block(self):
        return self.nc.Block(no_gpsimd_drain=True)

    def carry(self, eng, sem):
        eng.sem_inc(sem, 1)

    def adj_rows(self, jb, i0=0, n=N):
        return self.adjT[:, ds(jb * N + i0, n)]


def run_ahead(eng, ahead, h, turns, per, first, second, start=True, follow=None, before=None, midway=None, peeled=()):
    if start:
        for n in range(ahead):
            first(h, 0, n)

    def turn(t, more):
        if before is not None:
            before(t)
        for n in range(per):
            if n + ahead < per:
                first(h, t, n + ahead)
            elif more:
                first(h, t + 1, n + ahead - per)
            elif follow is not None:
                first(follow, 0, n + ahead - per)
            second(h, t, n)
            if n == 1 and midway is not None:
                midway(t)

    for t, then in enumerate(peeled):
        turn(t, True)
        then()
    with eng.Fori(0, turns - 1 - len(peeled)) as t:
        turn(t + len(peeled), True)
    turn(turns - 1, False)


def each_head(eng, body):
    body((0, 0), (1, 1))
    with eng.Fori(0, H2 // 2 - 1) as hh:
        body((hh * 2 + 1, 1), (hh * 2 + 2, 0))
        body((hh * 2 + 2, 0), (hh * 2 + 3, 1))
    body((H2 - 1, 1), None)


def per_block(t, n=D):
    return t.unsqueeze(2).broadcast_to([t.shape[0], t.shape[1], n])


def row(t, nb=NB):
    return t.unsqueeze(1).broadcast_to([t.shape[0], nb, t.shape[1]])


def center_and_sum(v, step, src, cen, sq, mean, var):
    step(v.tensor_reduce(mean, src, AX_X, ALU.add))
    step(v.tensor_scalar(mean, mean, 1.0 / D, None, ALU.mult))
    step(v.tensor_tensor(cen, src, per_block(mean), ALU.subtract))
    step(v.tensor_tensor(sq, cen, cen, ALU.mult))
    step(v.tensor_reduce(var, sq, AX_X, ALU.add))


def stage_start(k):
    io = k.io
    s_load, s_const = k.sem("start_loaded"), k.sem("start_const")
    with k.block() as block:

        @block.sync
        def _(sp):
            sp.dma_start(k.x[:, :, :], io["x"].rearrange("(b p) f -> p b f", p=P)).then_inc(s_load, 16)
            sp.dma_start(k.ident[:, :], io["ident"]).then_inc(s_load, 16)
            sp.wait_ge(s_load, 32)

        @block.vector
        def _(v):
            v.memset(k.zeros[:, :], 0.0)
            v.memset(k.eps[:, :], EPS)
            v.wait_ge(s_load, 32)
            v.tensor_copy(k.ident_b[:, :], k.ident[:, :]).then_inc(s_const, 1)


def load_adjacency(k, sp, first=0, end=NB):
    adj = k.io["adjT"].rearrange("(b p) i -> p b i", p=P)
    for jb in range(first, end):
        s, n = (k.adj_even, k.adj_odd)[jb % 2], jb // 2
        if n:
            sp.wait_ge(s, 16 * n)
        sp.dma_start(k.adj_rows(jb), adj[:, jb, :]).then_inc(s, 16)


def layer0(k):
    nc, io = k.nc, k.io
    with ExitStack() as ctx:
        gT = k.sb(ctx, "l0_gT", [P, N])
        V = k.sb(ctx, "l0_V", [P, NB, D + 1])
        wT = k.sb(ctx, "l0_wT", [D, D])
        bias = k.sb(ctx, "l0_bias", [P, D])
        b8 = k.sb(ctx, "l0_b8", [P, 1])
        T = k.sb(ctx, "l0_T", [P, 2, N])
        Pm = k.sb(ctx, "l0_P", [P, 2, N])
        stat = k.sb(ctx, "l0_stat", [P, 2, P])
        mean = k.sb(ctx, "l0_mean", [P, NB])
        var = k.sb(ctx, "l0_var", [P, NB])
        norm = k.sb(ctx, "l0_norm", [P, NB])
        rn = k.sb(ctx, "l0_rn", [P, NB])
        h = T[:, 0, :].rearrange("p (b f) -> p b f", f=D)
        sq = T[:, 1, :].rearrange("p (b f) -> p b f", f=D)
        g = Pm[:, 0, :].rearrange("p (b f) -> p b f", f=D)

        s_w, s_var, s_std, s_ss, s_nrm = (k.sem("l0_" + n) for n in ("w_loaded", "var", "std", "sumsq", "norm"))
        s_g, s_gp, s_gt, s_vp = (k.sem("l0_" + n) for n in ("g_ready", "g_turned", "gT_ready", "V_product"))
        with k.block() as block, ExitStack() as pctx:
            tr = k.ps(pctx, "l0_tr", [P, 4, CH])
            vp = k.ps(pctx, "l0_vp", [P, 4, CH])

            @block.sync
            def _(sp):
                sp.dma_start(wT[:, :], io["L0_WT"]).then_inc(s_w, 16)
                sp.dma_start(bias[:, :], io["L0_bias"].partition_broadcast(P)).then_inc(s_w, 16)
                sp.dma_start(b8[:, :], io["L0_b"].partition_broadcast(P)).then_inc(s_w, 16)
                load_adjacency(k, sp, 0, 8)
                sp.wait_ge(s_w, 48)

            @block.vector
            def _(v):
                step = k.steps.on(v)
                center_and_sum(v, step, k.x[:, :, :], h, sq, mean[:, :], var[:, :])
                v.sem_inc(s_var, 1)
                v.wait_ge(s_std, 1)
                step(v.reciprocal(rn[:, :], norm[:, :]))
                step(v.scalar_tensor_tensor(h, h, 0.0, per_block(rn[:, :]), ALU.max, ALU.mult))
                step(v.tensor_tensor(sq, h, h, ALU.mult))
                step(v.tensor_reduce(var[:, :], sq, AX_X, ALU.add))
                v.sem_inc(s_ss, 1)
                v.wait_ge(s_nrm, 1)
                step(v.reciprocal(rn[:, :], norm[:, :]))
                v.tensor_tensor(g, h, per_block(rn[:, :]), ALU.mult).then_inc(s_g, 1)
                v.memset(V[:, :, D:D + 1], 1.0)
                v.wait_ge(s_w, 48)
                v.tensor_scalar(b8[:, :], b8[:, :], 0.125, None, ALU.mult)
                for c in range(4):
                    v.wait_ge(s_vp, 4 * c + 4)
                    v.tensor_tensor(V[:, 4 * c:4 * c + 4, 0:D], vp[:, c, :].rearrange("p (b f) -> p b f", f=D),
                                    per_block(norm[:, 4 * c:4 * c + 4]), ALU.mult)

            @block.scalar
            def _(act):
                act.wait_ge(s_var, 1)
                act.activation(norm[:, :], var[:, :], ACT.Sqrt, bias=k.eps[:, :], scale=1.0 / D).then_inc(s_std, 1)
                act.wait_ge(s_ss, 1)
                act.activation(norm[:, :], var[:, :], ACT.Sqrt).then_inc(s_nrm, 1)
                for c in range(4):
                    act.wait_ge(s_gp, 4 * c + 4)
                    act.activation(gT[:, ds(c * CH, CH)], tr[:, c, :], ACT.Copy).then_inc(s_gt, 1)

            @block.tensor
            def _(pe):
                pe.wait_ge(s_g, 1)
                for b in range(NB):
                    pe.transpose(tr[:, b // 4, ds(b % 4 * P, P)], g[:, b, :], k.ident[:, :]).then_inc(s_gp, 1)
                pe.wait_ge(s_w, 48)
                for b in range(NB):
                    pe.wait_ge(s_gt, b // 4 + 1)
                    pe.matmul(vp[:, b // 4, ds(b % 4 * P, P)], gT[:, ds(b * P, P)], wT[:, :], start=True, stop=True).then_inc(s_vp, 1)

        s_stat, s_score, s_tanh, s_exp, s_p, s_pv = (k.sem("l0_" + n) for n in ("stationary", "score", "tanh", "exp", "probs", "pv"))
        with k.block() as block, ExitStack() as pctx:
            S = k.ps(pctx, "l0_S", [P, 2, CH])
            acc = k.ps(pctx, "l0_acc", [P, 6, CH])

            @block.sync
            def _(sp):
                load_adjacency(k, sp, 8)

            @block.gpsimd
            def _(pool):
                with pool.Fori(0, NB // 2) as t:
                    for u in range(2):
                        if u == 0:
                            pool.wait_ge(s_score, t * 8 + 4)
                        else:
                            pool.wait_ge(s_score, t * 8 + 8)
                        pool.tensor_copy(stat[:, u, :], gT[:, ds(t * (2 * P) + u * P, P)]).then_inc(s_stat, 1)

            @block.tensor
            def _(pe):
                pe.sem_inc(s_score, 8)
                pe.sem_inc(s_pv, 2)
                for b in range(6):
                    pe.matmul(acc[:, b, 0:ROWB * (D + 1)], k.zeros[:, 0:P], k.zeros[:, 0:ROWB * (D + 1)],
                              start=True, stop=False, skip_group_check=True)

                def scores(t, u):
                    pe.wait_ge(s_stat, t * 2 + u + 1)
                    for c in range(NC):
                        pe.wait_ge(s_tanh, t * 8 + 4 * u + c + 1)
                        pe.matmul(S[:, c % 2, :], stat[:, u % 2, :], gT[:, ds(c * CH, CH)], start=True, stop=True).then_inc(s_score, 1)

                def weigh(t, u):
                    pe.wait_ge(s_p, t * 2 + u + 3)
                    for b in range(NB):
                        mm = pe.matmul(acc[:, b // ROWB, ds(b % ROWB * (D + 1), D + 1)], Pm[:, u, ds(b * P, P)],
                                       V[:, :, :].rearrange("p b f -> p (b f)")[:, ds(t * (2 * (D + 1)) + u * (D + 1), D + 1)],
                                       start=False, stop=False, skip_group_check=True)
                    mm.then_inc(s_pv, 1)

                scores(0, 0)
                with pe.Fori(0, NB // 2 - 1) as t:
                    scores(t, 1)
                    weigh(t, 0)
                    scores(t + 1, 0)
                    weigh(t, 1)
                last = NB // 2 - 1
                scores(last, 1)
                weigh(last, 0)
                weigh(last, 1)

            @block.scalar
            def _(act):
                act.sem_inc(s_tanh, 2)
                act.preload_act_table(ACT.Exp)
                with act.Fori(0, NB // 2) as t:
                    for u in range(2):
                        act.wait_ge(s_p, t * 2 + u + 1)
                        for c in range(NC):
                            act.wait_ge(s_score, t * 8 + 4 * u + c + 9)
                            act.activation(T[:, u, ds(c * CH, CH)], S[:, c % 2, :], ACT.Tanh, scale=b8[:, 0:1]).then_inc(s_tanh, 1)
                        act.wait_ge(s_tanh, t * 8 + 4 * u + NC + 2)
                        act.activation(T[:, u, :], T[:, u, :], ACT.Exp, scale=8.0).then_inc(s_exp, 1)

            @block.vector
            def _(v):
                step = k.steps.on(v)
                v.sem_inc(s_p, 2)
                with v.Fori(0, NB // 2) as t:
                    for u in range(2):
                        v.wait_ge((k.adj_even, k.adj_odd)[u], t * 16 + 16)
                        v.wait_ge(s_exp, t * 2 + u + 1)
                        v.wait_ge(s_pv, t * 2 + u + 1)
                        v.tensor_tensor(Pm[:, u, :], T[:, u, :], k.adj_rows(t * 2 + u), ALU.mult).then_inc(s_p, 1)
                v.wait_ge(s_pv, NB + 2)
                accv = acc[:, :, 0:ROWB * (D + 1)].rearrange("p b (r f) -> p b r f", f=D + 1)
                rv = rn[:, 0:15].rearrange("p (b r) -> p b r", r=ROWB)
                ov = T[:, 0, 0:15 * D].rearrange("p (b r f) -> p b r f", r=ROWB, f=D)
                step(v.reciprocal(rv, accv[:, 0:5, :, D]))
                step(v.reciprocal(rn[:, 15:16], accv[:, 5, 0:1, D]))
                step(v.tensor_tensor(ov, accv[:, 0:5, :, 0:D], rv.unsqueeze(3).broadcast_to([P, 5, ROWB, D]), ALU.mult))
                step(v.tensor_scalar(T[:, 0, 15 * D:16 * D], accv[:, 5, 0, 0:D], rn[:, 15:16], None, ALU.mult))
                step(v.tensor_tensor(k.x[:, :, :], k.x[:, :, :], h, ALU.add))
                step(v.tensor_tensor(k.x[:, :, :], k.x[:, :, :], row(bias[:, :]), ALU.add))


def layer1_gcn(k, hT, wts):
    io = k.io
    with ExitStack() as ctx:
        h1 = k.sb(ctx, "l1_h1", [P, NB, D])
        cen = k.sb(ctx, "l1_cen", [P, NB, D])
        sq = k.sb(ctx, "l1_sq", [P, NB, D])
        axT = k.sb(ctx, "l1_axT", [P, N])
        gw = k.sb(ctx, "l1_gcn_w", [D, D])
        gb = k.sb(ctx, "l1_gcn_b", [P, D])
        mean = k.sb(ctx, "l1_mean", [P, NB])
        var = k.sb(ctx, "l1_var", [P, NB])
        std = k.sb(ctx, "l1_std", [P, NB])
        s_wl = k.sem("l1_all_weights_loaded")
        s_w, s_var, s_std, s_h, s_ax, s_axT, s_aw, s_n, s_tr, s_hT = (
            k.sem("l1_" + n) for n in ("w_loaded", "var", "std", "h1_ready", "ax_product", "axT_ready", "axw_product", "normed", "turned", "hT_ready"))
        with k.block() as block, ExitStack() as pctx:
            ax = k.ps(pctx, "l1_ax", [P, 4, CH])
            aw = k.ps(pctx, "l1_aw", [P, 4, CH])

            @block.sync
            def _(sp):
                sp.dma_start(gw[:, :], io["L1_gcn_w"]).then_inc(s_w, 16)
                sp.dma_start(gb[:, :], io["L1_gcn_b"].partition_broadcast(P)).then_inc(s_w, 16)
                for t, n in wts:
                    sp.dma_start(t, io[n]).then_inc(s_wl, 16)
                sp.wait_ge(s_w, 32)
                sp.wait_ge(s_wl, 16 * len(wts))

            @block.vector
            def _(v):
                step = k.steps.on(v)
                center_and_sum(v, step, k.x[:, :, :], cen[:, :, :], sq[:, :, :], mean[:, :], var[:, :])
                v.sem_inc(s_var, 1)
                v.wait_ge(s_std, 1)
                step(v.reciprocal(var[:, :], std[:, :]))
                v.scalar_tensor_tensor(h1[:, :, :], cen[:, :, :], 0.0, per_block(var[:, :]), ALU.max, ALU.mult).then_inc(s_h, 1)
                v.wait_ge(s_h, 1)
                v.wait_ge(s_w, 32)
                for c in range(NC):
                    b = slice(4 * c, 4 * c + 4)
                    v.wait_ge(s_aw, 4 * c + 4)
                    step(v.tensor_tensor(sq[:, b, :], aw[:, c, :].rearrange("p (b f) -> p b f", f=D), row(gb[:, :], 4), ALU.add))
                    step(v.tensor_scalar(sq[:, b, :], sq[:, b, :], 0.0, None, ALU.max))
                    center_and_sum(v, step, sq[:, b, :], cen[:, b, :], sq[:, b, :], mean[:, b], var[:, b])
                    v.sem_inc(s_var, 1)
                    v.wait_ge(s_std, c + 2)
                    step(v.reciprocal(var[:, b], std[:, b]))
                    v.tensor_tensor(cen[:, b, :], cen[:, b, :], per_block(var[:, b]), ALU.mult).then_inc(s_n, 1)

            @block.scalar
            def _(act):
                act.wait_ge(s_var, 1)
                act.activation(std[:, :], var[:, :], ACT.Sqrt, bias=k.eps[:, :], scale=1.0 / D).then_inc(s_std, 1)
                act.wait_ge(s_wl, 16 * len(wts))
                for c in range(NC + 2):
                    if c < NC:
                        act.wait_ge(s_ax, c + 1)
                        act.activation(axT[:, ds(c * CH, CH)], ax[:, c, :], ACT.Copy).then_inc(s_axT, 1)
                    if 1 <= c <= NC:
                        act.wait_ge(s_var, c + 1)
                        act.activation(std[:, 4 * c - 4:4 * c], var[:, 4 * c - 4:4 * c], ACT.Sqrt, bias=k.eps[:, :], scale=1.0 / D).then_inc(s_std, 1)
                    if c >= 2:
                        act.wait_ge(s_tr, 4 * (c - 1))
                        act.activation(hT[:, ds((c - 2) * CH, CH)], ax[:, c - 2, :], ACT.Identity, bias=k.l1["ln_b"][:, :], scale=k.l1["ln_g"][:, :]).then_inc(s_hT, 1)

            @block.tensor
            def _(pe):
                pe.wait_ge(s_h, 1)
                for r in range(NB // 2):
                    pe.wait_ge(k.adj_even, 16 * (r + 1))
                    pe.wait_ge(k.adj_odd, 16 * (r + 1))
                for c in range(NC + 2):
                    if c < NC:
                        for jb in range(NB):
                            mm = pe.matmul(ax[:, c, :], h1[:, jb, :], k.adj_rows(jb, c * CH, CH), start=jb == 0, stop=jb == NB - 1)
                        mm.then_inc(s_ax, 1)
                    if c == 0:
                        pe.wait_ge(s_w, 32)
                    if 1 <= c <= NC:
                        pe.wait_ge(s_axT, c)
                        for b in range(4 * c - 4, 4 * c):
                            pe.matmul(aw[:, b // 4, ds(b % 4 * P, P)], axT[:, ds(b * P, P)], gw[:, :], start=True, stop=True).then_inc(s_aw, 1)
                    if c >= 2:
                        pe.wait_ge(s_n, c - 1)
                        for b in range(4 * c - 8, 4 * c - 4):
                            pe.transpose(ax[:, b // 4, ds(b % 4 * P, P)], cen[:, b, :], k.ident[:, :]).then_inc(s_tr, 1)


def layer1_ssm(k, hT):
    io, w = k.io, k.l1
    with ExitStack() as ctx:
        t2 = lambda n, dt=F32: k.sb(ctx, "l1_" + n, [P, CB, CH], dt)
        RING = 4
        xin = k.sb(ctx, "l1_xin", [P, CB, CH + KC - 1])
        u, sz, dt, du = t2("u"), t2("sz"), t2("dt"), t2("du")
        hs, hC = t2("hs"), t2("hC")
        dA = k.sb(ctx, "l1_dA", [P, 2, CB, CH])
        dBu = t2("dBu")
        dbc = dA[0:XP, 0, 0, :]
        bc = k.sb(ctx, "l1_bc", [P, RING, 2, CH])
        state = k.sb(ctx, "l1_state", [P, CB * DS])
        negA = k.sb(ctx, "l1_negA", [P, CB * DS])
        bc_dram = k.nc.dram_tensor("l1_bc_rows", (2 * DS, N), F32, kind="Internal").ap()
        bc_src = bc_dram.rearrange("(a n) t -> a (n t)", a=2)

        names = ("init", "xz_product", "xin_ready", "sz_ready", "conv", "u_ready", "dbc_product", "dbc_ready", "dt_product",
                 "softplus_in", "softplus_e", "softplus_l", "dt_ready", "bc_stored", "dA_ready", "dBu_ready",
                 "scanned", "hC_ready", "y_summed", "yT_ready", "out_product", "out_added", "negA_exp", "du_free")
        (s_init, s_xz, s_xin, s_sz, s_conv, s_u, s_dbcp, s_dbc, s_dtp, s_spin, s_spe, s_spl, s_dt, s_bcst, s_dA, s_dBu,
         s_scan, s_hC, s_y, s_yT, s_op, s_oa, s_nA, s_duf) = (k.sem("l1_" + n) for n in names)
        s_bc = [k.sem("l1_bc%d" % n) for n in range(RING)]
        TURNS = DS // RING
        with k.block() as block, ExitStack() as pctx:
            xp = k.ps(pctx, "l1_xp", [P, CB, CH])
            zp = k.ps(pctx, "l1_zp", [P, CB, CH])
            yp = k.ps(pctx, "l1_yp", [P, CB, CH])
            dp = k.ps(pctx, "l1_dp", [P, CH])
            op = k.ps(pctx, "l1_op", [P, CH])

            @block.sync
            def _(sp):
                sp.sem_inc(s_hC, 2 * RING)
                with sp.Fori(0, NC) as q:
                    sp.wait_ge(s_dbc, q + 1)
                    sp.dma_start(bc_dram[:, ds(q * CH, CH)], dA[DTR:XP, 0, 0, :]).then_inc(s_bcst, 16)
                    with sp.Fori(0, TURNS) as r:
                        for e in range(RING):
                            if e == 0:
                                sp.wait_ge(s_bcst, q * 16 + 16)
                            sp.wait_ge(s_hC, q * (2 * DS) + r * (2 * RING) + 2 * e + 2)
                            sp.dma_start(bc[:, e, :, :], bc_src[:, ds((r * RING + e) * N + q * CH, CH)].partition_broadcast(P)).then_inc(s_bc[e], 16)

            @block.gpsimd
            def _(pool):
                pool.memset(state[:, :], 0.0)
                pool.memset(xin[:, :, 0:KC - 1], 0.0).then_inc(s_init, 1)
                with pool.Fori(0, NC) as q:
                    with pool.Fori(0, TURNS) as r:
                        for e in range(RING):
                            pool.wait_ge(s_dt, q + 1)
                            pool.wait_ge(s_bc[e], q * (16 * TURNS) + r * 16 + 16)
                            for cb in range(CB):
                                pool.wait_ge(s_scan, q * (2 * DS) + r * (2 * RING) + 2 * e + cb + 3)
                                pool.tensor_tensor(dBu[:, cb, :], du[:, cb, :], bc[:, e, 0, :], ALU.mult).then_inc(s_dBu, 1)

            @block.tensor
            def _(pe):
                pe.sem_inc(s_y, 2)
                with pe.Fori(0, NC) as q:
                    pe.wait_ge(s_duf, q + 1)
                    for cb in range(CB):
                        pe.matmul(xp[:, cb, :], w["w_in"][:, ds(cb * P, P)], hT[:, ds(q * CH, CH)], start=True, stop=True).then_inc(s_xz, 1)
                    for cb in range(CB):
                        pe.matmul(zp[:, cb, :], w["w_in"][:, ds(DI + cb * P, P)], hT[:, ds(q * CH, CH)], start=True, stop=True).then_inc(s_xz, 1)
                        pe.matmul(yp[:, cb, :], k.zeros[:, 0:P], k.zeros[:, :], start=True, stop=False, skip_group_check=True)
                    pe.wait_ge(s_u, q * 2 + 2)
                    for cb in range(CB):
                        mm = pe.matmul(dp[0:XP, :], w["w_xp"][:, cb, :], u[:, cb, :], start=cb == 0, stop=cb == 1)
                    mm.then_inc(s_dbcp, 1)
                    pe.wait_ge(s_dbc, q + 1)
                    for cb in range(CB):
                        pe.matmul(xp[:, cb, :], w["w_dt"][:, ds(cb * P, P)], dA[0:DTR, 0, 0, :], start=True, stop=True).then_inc(s_dtp, 1)
                    with pe.Fori(0, DS) as n:
                        for cb in range(CB):
                            pe.wait_ge(s_hC, q * (2 * DS) + n * 2 + cb + 2 * RING + 1)
                            pe.matmul(yp[:, cb, :], k.ident[:, :], hC[:, cb, :], start=False, stop=False, skip_group_check=True).then_inc(s_y, 1)
                    pe.wait_ge(s_yT, q * 2 + 2)
                    for b in range(CH // P):
                        for cb in range(CB):
                            mm = pe.matmul(op[:, ds(b * P, P)], hC[:, cb, ds(b * P, P)], w["w_out"][:, cb, :], start=cb == 0, stop=cb == 1)
                    mm.then_inc(s_op, 1)

            @block.scalar
            def _(act):
                act.activation(negA[:, :], w["A_log"][:, :], ACT.Exp).then_inc(s_nA, 1)
                with act.Fori(0, NC) as q:
                    for cb in range(CB):
                        act.wait_ge(s_xz, q * 4 + cb + 1)
                        act.activation(xin[:, cb, KC - 1:], xp[:, cb, :], ACT.Copy).then_inc(s_xin, 1)
                    for cb in range(CB):
                        act.wait_ge(s_conv, q * 2 + cb + 1)
                        act.activation(u[:, cb, :], hs[:, cb, :], ACT.Silu, bias=w["conv_b"][:, cb:cb + 1]).then_inc(s_u, 1)
                    for cb in range(CB):
                        act.wait_ge(s_xz, q * 4 + cb + 3)
                        act.activation(sz[:, cb, :], zp[:, cb, :], ACT.Silu).then_inc(s_sz, 1)
                    act.wait_ge(s_dbcp, q + 1)
                    act.activation(dbc, dp[0:XP, :], ACT.Copy).then_inc(s_dbc, 1)
                    act.wait_ge(s_spin, q * 2 + 2)
                    for cb in range(CB):
                        act.activation(hC[:, cb, :], dBu[:, cb, :], ACT.Exp).then_inc(s_spe, 1)
                    act.wait_ge(s_spe, q * 2 + 2)
                    for cb in range(CB):
                        act.activation(du[:, cb, :], hC[:, cb, :], ACT.Ln, bias=1.0).then_inc(s_spl, 1)
                    act.wait_ge(s_dt, q + 1)
                    act.wait_ge(s_bcst, q * 16 + 16)
                    k.carry(act, k.act_waits)
                    act.preload_act_table(ACT.Exp)
                    with act.Fori(0, DS // 2) as r:
                        for e in range(2):
                            for cb in range(CB):
                                act.wait_ge(s_scan, q * (2 * DS) + r * 4 + 2 * e + cb + 1)
                                act.activation(dA[:, e, cb, :], dt[:, cb, :], ACT.Exp, scale=negA[:, ds(r * 2 + e + cb * DS, 1)]).then_inc(s_dA, 1)

            @block.vector
            def _(v):
                step = k.steps.on(v)
                v.wait_ge(s_nA, 1)
                step(v.tensor_scalar(negA[:, :], negA[:, :], -1.0, None, ALU.mult))
                v.sem_inc(s_duf, 1)
                v.sem_inc(s_scan, 4)
                v.sem_inc(s_oa, 2)
                v.wait_ge(s_init, 1)
                first, PER = step.n, 22
                with v.Fori(0, NC) as q:
                    step.begin(q, PER)
                    cv = hs
                    for kk in range(KC):
                        for cb in range(CB):
                            if kk == 0:
                                v.wait_ge(s_xin, q * 2 + cb + 1)
                                ins = v.tensor_scalar(cv[:, cb, :], xin[:, cb, 0:CH], w["conv_w"][:, cb, 0:1], None, ALU.mult)
                            else:
                                ins = v.scalar_tensor_tensor(cv[:, cb, :], xin[:, cb, kk:kk + CH], w["conv_w"][:, cb, kk:kk + 1], cv[:, cb, :], ALU.mult, ALU.add)
                            step(ins)
                            if kk == KC - 1:
                                v.sem_inc(s_conv, 1)
                    for cb in range(CB):
                        step(v.tensor_copy(xin[:, cb, 0:KC - 1], xin[:, cb, CH:CH + KC - 1]))
                    for cb in range(CB):
                        v.wait_ge(s_dtp, q * 2 + cb + 1)
                        step(v.tensor_scalar(dt[:, cb, :], xp[:, cb, :], w["b_dt"][:, cb:cb + 1], None, ALU.add))
                        v.scalar_tensor_tensor(dBu[:, cb, :], dt[:, cb, :], -1.0, dt[:, cb, :], ALU.mult, ALU.min).then_inc(s_spin, 1)
                    for cb in range(CB):
                        v.wait_ge(s_spe, q * 2 + cb + 1)
                        step(v.tensor_scalar(hs[:, cb, :], hC[:, cb, :], 1.0, None, ALU.add))
                        step(v.scalar_tensor_tensor(hs[:, cb, :], hs[:, cb, :], -1.0, hC[:, cb, :], ALU.add, ALU.subtract))
                        v.wait_ge(s_spl, q * 2 + cb + 1)
                        step(v.scalar_tensor_tensor(dt[:, cb, :], dt[:, cb, :], 0.0, du[:, cb, :], ALU.max, ALU.add))
                        step(v.tensor_tensor(dt[:, cb, :], dt[:, cb, :], hs[:, cb, :], ALU.subtract))
                        if cb == 0:
                            step(v.tensor_tensor(du[:, cb, :], dt[:, cb, :], u[:, cb, :], ALU.mult))
                        else:
                            step(v.tensor_tensor(du[:, cb, :], dt[:, cb, :], u[:, cb, :], ALU.mult))
                    step.end(NC, first, PER)
                    v.sem_inc(s_dt, 1)
                    with v.Fori(0, TURNS) as r:
                        for e in range(RING):
                            base = q * (2 * DS) + r * (2 * RING) + 2 * e
                            for cb in range(CB):
                                at = state[:, ds(r * RING + e + cb * DS, 1)]
                                v.wait_ge(s_dA, base + cb + 1)
                                v.wait_ge(s_dBu, base + cb + 1)
                                v.wait_ge(s_hC, base + cb + 2 * RING - 1)
                                v.wait_ge(s_oa, base + cb + 1)
                                v.tensor_tensor_scan(hs[:, cb, :], dA[:, e % 2, cb, :], dBu[:, cb, :], at, ALU.mult, ALU.add).then_inc(s_scan, 1)
                            v.wait_ge(s_bc[e], q * (16 * TURNS) + r * 16 + 16)
                            for cb in range(CB):
                                at = state[:, ds(r * RING + e + cb * DS, 1)]
                                v.wait_ge(s_scan, base + cb + 5)
                                v.wait_ge(s_y, base + cb + 1)
                                v.tensor_tensor(hC[:, cb, :], hs[:, cb, :], bc[:, e, 1, :], ALU.mult).then_inc(s_hC, 1)
                                v.tensor_copy(at, hs[:, cb, CH - 1:CH]).then_inc(s_oa, 1)
                    v.wait_ge(s_oa, q * (2 * DS) + 2 * DS + 2)
                    for cb in range(CB):
                        v.wait_ge(s_y, q * (2 * DS) + 2 * DS + 2)
                        v.scalar_tensor_tensor(hs[:, cb, :], u[:, cb, :], w["D"][:, cb:cb + 1], yp[:, cb, :], ALU.mult, ALU.add).then_inc(s_init, 1)
                        v.wait_ge(s_init, q * 2 + cb + 2)
                        v.wait_ge(s_sz, q * 2 + cb + 1)
                        v.tensor_tensor(hC[:, cb, :], hs[:, cb, :], sz[:, cb, :], ALU.mult).then_inc(s_yT, 1)
                    v.wait_ge(s_op, q + 1)
                    xq = k.x[:, :, :].rearrange("p b f -> p (b f)")[:, ds(q * CH, CH)]
                    v.tensor_tensor(xq, xq, op[:, :], ALU.add).then_inc(s_duf, 1)


def layer1(k):
    with ExitStack() as ctx:
        w = k.l1 = {}
        for n, shape in (("w_in", [D, 2 * DI]), ("w_xp", [P, CB, XP]), ("w_dt", [DTR, DI]), ("w_out", [P, CB, D]), ("A_log", [P, CB * DS]),
                         ("conv_w", [P, CB, KC]), ("conv_b", [P, CB]), ("b_dt", [P, CB]), ("D", [P, CB]), ("ln_g", [P, 1]), ("ln_b", [P, 1])):
            w[n] = k.sb(ctx, "l1w_" + n, shape)
        hT = k.sb(ctx, "l1_hT", [P, N])
        layer1_gcn(k, hT, [(w[n][tuple(slice(None) for _ in w[n].shape)], "L1_" + n) for n in w])
        layer1_ssm(k, hT)


def load_weights(k, ctx, sp_list):
    w = {}
    for n, shape in sp_list:
        w[n] = k.sb(ctx, "w_" + n, shape)
    return w


def normed_and_turned(k, tag, w, h, hT, work):
    with ExitStack() as ctx:
        mean, var, std = (k.sb(ctx, tag + n, [P, NB]) for n in ("mean", "var", "std"))
        s_w = k.sem(tag + "weights")
        s_var, s_std, s_h, s_tr, s_hT = k.norm_sems
        done = k.normed
        k.normed += 1
        with k.block() as block, ExitStack() as pctx:
            tr = k.ps(pctx, tag + "tr", [P, 4, CH])

            @block.sync
            def _(sp):
                for n in w:
                    t = w[n]
                    sp.dma_start(t[tuple(slice(None) for _ in t.shape)], k.io[n] if len(k.io[n].shape) > 1 else k.io[n].partition_broadcast(P)).then_inc(s_w, 16)
                sp.wait_ge(s_w, 16 * len(w))

            @block.vector
            def _(v):
                step = k.steps.on(v)
                center_and_sum(v, step, k.x[:, :, :], h, work, mean[:, :], var[:, :])
                v.sem_inc(s_var, 1)
                v.wait_ge(s_std, done + 1)
                step(v.reciprocal(var[:, :], std[:, :]))
                v.scalar_tensor_tensor(h, h, 0.0, per_block(var[:, :]), ALU.max, ALU.mult).then_inc(s_h, 1)

            @block.scalar
            def _(act):
                act.wait_ge(s_var, done + 1)
                act.activation(std[:, :], var[:, :], ACT.Sqrt, bias=k.eps[:, :], scale=1.0 / D).then_inc(s_std, 1)
                for c in range(NC):
                    act.wait_ge(s_tr, done * NB + 4 * c + 4)
                    act.activation(hT[:, ds(c * CH, CH)], tr[:, c, :], ACT.Copy).then_inc(s_hT, 1)

            @block.tensor
            def _(pe):
                pe.wait_ge(s_h, done + 1)
                for b in range(NB):
                    pe.transpose(tr[:, b // 4, ds(b % 4 * P, P)], h[:, b, :], k.ident[:, :]).then_inc(s_tr, 1)


def split_bf16(step, v, src, parts, rest):
    step(v.tensor_copy(parts[0], src))
    step(v.tensor_tensor(rest, src, parts[0], ALU.subtract))
    step(v.tensor_copy(parts[1], rest))
    step(v.tensor_tensor(rest, rest, parts[1], ALU.subtract))
    step(v.tensor_copy(parts[2], rest))


HALF = N // 2
UNITS = 2 * NB
VW = HD + 1
NR = 4 * H2


def layer2(k):
    with ExitStack() as ctx:
        w = load_weights(k, ctx, [("L2_eW", [P, H2]), ("L2_eb", [P, H2])])
        V = k.sb(ctx, "l2_V", [P, NB, H2, VW])
        ad = k.sb(ctx, "l2_ad", [P, NB, H2])
        srcn = k.sb(ctx, "l2_as", [P, NB, H2])
        rows = k.sb(ctx, "l2_rows", [P, N], BF16)
        big = k.sb(ctx, "l2_big", [P, P], BF16)
        layer2_project(k, w, V, ad, srcn)
        layer2_maxima(k, w, ad, srcn, rows, big)
        hout = k.sb(ctx, "l2_hout", [P, NB, D])
        layer2_attend(k, w, V, ad, srcn, rows, big, hout)
        layer2_fuse(k, hout)


def layer2_project(k, w, V, ad, srcn):
    with ExitStack() as ctx:
        h = k.sb(ctx, "l2_h", [P, NB, D])
        hT = k.sb(ctx, "l2_hT", [P, N])
        h2T = k.sb(ctx, "l2_h2T", [P, N])
        att = k.sb(ctx, "l2_att", [D, 2 * H2])
        w = {**w, **load_weights(k, ctx, [("L2_WT", [D, D]), ("L2_src", [D, 1]), ("L2_dst", [D, 1]), ("head_mask", [D, H2])])}
        normed_and_turned(k, "l2_", w, h[:, :, :], hT, h2T[:, :].rearrange("p (b f) -> p b f", f=D))
        s_att, s_h2T, s_h2Tc, s_v, s_vc, s_a, s_a2 = (k.sem("l2p_" + n) for n in ("att", "h2T_product", "h2T", "V_product", "V", "logit_terms", "ones"))
        with k.block() as block, ExitStack() as pctx:
            @block.sync
            def _(sp):
                sp.dma_start(k.x_kept, k.x[:, :, :]).then_inc(k.s_x_kept, 16)
                sp.wait_ge(k.s_x_kept, 16)

            tp = k.ps(pctx, "l2_tp", [P, 4, CH])
            vp = k.ps(pctx, "l2_vp", [P, 3, CH])
            ap = k.ps(pctx, "l2_ap", [P, NB, 2 * H2])

            @block.tensor
            def _(pe):
                for c in range(NC):
                    pe.matmul(tp[:, c, :], w["L2_WT"][:, :], hT[:, ds(c * CH, CH)], start=True, stop=True).then_inc(s_h2T, 1)
                for b in range(NB):
                    if b >= 12 and b % 4 == 0:
                        pe.wait_ge(s_vc, b // 4 - 2)
                    pe.matmul(vp[:, b // 4 % 3, ds(b % 4 * P, P)], hT[:, ds(b * P, P)], w["L2_WT"][:, :], start=True, stop=True).then_inc(s_v, 1)
                pe.wait_ge(s_att, 2)
                for b in range(NB):
                    pe.wait_ge(s_h2Tc, b // 4 + 1)
                    pe.matmul(ap[:, b, :], h2T[:, ds(b * P, P)], att[:, :], start=True, stop=True).then_inc(s_a, 1)

            @block.scalar
            def _(act):
                for c in range(NC):
                    act.wait_ge(s_h2T, c + 1)
                    act.activation(h2T[:, ds(c * CH, CH)], tp[:, c, :], ACT.Copy).then_inc(s_h2Tc, 1)

            @block.vector
            def _(v):
                for n, name in enumerate(("L2_src", "L2_dst")):
                    v.tensor_scalar(att[:, ds(n * H2, H2)], w["head_mask"][:, :], w[name][:, 0:1], None, ALU.mult).then_inc(s_att, 1)
                v.memset(V[:, :, :, HD:VW], 1.0)
                for c in range(4):
                    v.wait_ge(s_v, 4 * c + 4)
                    v.tensor_copy(V[:, 4 * c:4 * c + 4, :, 0:HD], vp[:, c % 3, :].rearrange("p (b h d) -> p b h d", h=H2, d=HD)).then_inc(s_vc, 1)
                v.wait_ge(s_a, NB)
                v.tensor_copy(srcn[:, :, :], ap[:, :, 0:H2])
                v.tensor_copy(ad[:, :, :], ap[:, :, H2:])


def layer2_maxima(k, w, ad, srcn, rows, big):
    with ExitStack() as ctx:
        R = k.sb(ctx, "l2_R", [P, H2, N], BF16)
        t = k.sb(ctx, "l2_t", [P, 4, N], BF16)
        ab0 = k.sb(ctx, "l2_ab", [P, N], BF16)
        spare = k.x[:, :, :].rearrange("p b f -> p (b f)").bitcast(BF16).rearrange("p (a i) -> p a i", a=2)
        BT, ab = (rows[:, :], spare[:, 0, :]), (ab0[:, :], spare[:, 1, :])
        eI = k.sb(ctx, "l2_eI", [P, H2 - 2, P], BF16)
        mx = t[:, 1, 0:2 * NB * H2].bitcast(F32).rearrange("p (h b) -> p h b", b=NB)
        rn = ab0[:, :].rearrange("p (b r) -> p b r", r=P)
        rest = t[:, 0, 0:2 * NB * H2].bitcast(F32).rearrange("p (b h) -> p b h", h=H2)
        s_t, s_bt, s_m, s_r, s_sp = (k.sem("l2m_" + n) for n in ("logits", "mask", "masked", "maxed", "masked_sum"))
        s_tr, s_red, s_rows, s_rt = (k.sem("l2m_" + n) for n in ("turned", "reduced", "rows", "rows_turned"))
        PE0 = 2
        ACTH = H2 - 1
        with k.block() as block, ExitStack() as pctx:
            masked = k.ps(pctx, "l2_masked", [P, 2, 4, CH])

            @block.tensor
            def _(pe):
                with pe.Fori(0, NB // 2) as tt:
                    for u, h in ((u, h) for u in range(2) for h in range(PE0, H2)):
                        jb = tt * 2 + u
                        pe.wait_ge(s_bt, jb * 2 + 2)
                        pe.wait_ge(s_t, jb * ACTH + (h + 4 if h < PE0 + 2 else h + 5))
                        for c in range(NC):
                            pe.matmul(masked[:, h % 2, c, :], eI[:, h - PE0, :], ab[u][:, ds(c * CH, CH)], start=True, stop=False)
                            mm = pe.matmul(masked[:, h % 2, c, :], k.ident_b[:, :], BT[u][:, ds(c * CH, CH)], start=False, stop=True)
                        mm.then_inc(s_sp, 1)

            @block.scalar
            def _(act):
                act.sem_inc(s_t, ACTH)
                with act.Fori(0, NB) as jb:
                    for h in range(1, H2):
                        act.wait_ge(s_r, jb * H2 + h + 1)
                        bias = ad[:, :, :].rearrange("p b h -> p (b h)")[:, ds(jb * H2 + h, 1)]
                        if h < PE0:
                            act.activation(t[:, h % 4, :], k.adj_rows(jb), ACT.Identity, scale=w["L2_eW"][:, h:h + 1], bias=bias).then_inc(s_t, 1)
                        else:
                            act.wait_ge(s_sp, jb * (H2 - PE0) + h - PE0 + 1)
                            k.carry(act, k.act_waits)
                            act.activation(t[:, h % 4, :], masked[:, h % 2, :, :].rearrange("p c i -> p (c i)"), ACT.Identity, bias=bias).then_inc(s_t, 1)

            @block.vector
            def _(v):
                step = k.steps.on(v)
                step(v.memset(R[:, :, :], -BIG))
                v.tensor_scalar(big[:, :], k.ident[:, :], -BIG, None, ALU.mult)
                for h in range(PE0, H2):
                    step(v.tensor_scalar(eI[:, h - PE0, :], k.ident[:, :], w["L2_eW"][:, h:h + 1], None, ALU.mult))
                v.sem_inc(s_r, 4)

                def tiles(jb, u):
                    v.tensor_scalar(BT[u], k.adj_rows(jb), 0.0, -BIG, ALU.is_le, ALU.mult).then_inc(s_bt, 1)
                    v.tensor_copy(ab[u], k.adj_rows(jb)).then_inc(s_bt, 1)

                def compare(jb, u, more):
                    v.wait_ge(s_bt, jb * 2 + 2)
                    v.tensor_scalar(t[:, 0, :], ab[u], w["L2_eW"][:, 0:1], ad[:, :, :].rearrange("p b h -> p (b h)")[:, ds(jb * H2, 1)], ALU.mult, ALU.add).then_inc(s_m, 1)
                    v.wait_ge(s_m, jb * 3 + 1)
                    v.tensor_tensor(t[:, 0, :], t[:, 0, :], BT[u], ALU.add).then_inc(s_m, 1)
                    v.wait_ge(s_t, jb * ACTH + 1 + ACTH)
                    v.tensor_tensor(t[:, 1, :], t[:, 1, :], BT[u], ALU.add).then_inc(s_m, 1)
                    for h in range(2):
                        v.wait_ge(s_m, jb * 3 + h + 2)
                        v.tensor_tensor(R[:, h, :], R[:, h, :], t[:, h, :], ALU.max).then_inc(s_r, 1)
                    for h in range(PE0, H2):
                        if h == 4 and more:
                            tiles(jb + 1, 1 - u)
                        v.wait_ge(s_t, jb * ACTH + h + ACTH)
                        v.tensor_tensor(R[:, h, :], R[:, h, :], t[:, h % 4, :], ALU.max).then_inc(s_r, 1)
                    v.wait_ge(s_r, jb * H2 + H2 + 4)

                tiles(0, 0)
                with v.Fori(0, NB // 2 - 1) as tt:
                    compare(tt * 2, 0, True)
                    compare(tt * 2 + 1, 1, True)
                compare(NB - 2, 0, True)
                compare(NB - 1, 1, False)

        with k.block() as block, ExitStack() as pctx:
            rt = k.ps(pctx, "l2_rt", [P, 2, N], BF16)
            ro = k.ps(pctx, "l2_ro", [P, N], BF16)

            @block.vector
            def _(v):
                step = k.steps.on(v)
                for h in range(H2):
                    v.wait_ge(s_tr, h + 1)
                    step(v.tensor_reduce(mx[:, h, :], rt[:, h % 2, :].rearrange("p (b q) -> p b q", q=P), AX_X, ALU.max))
                    v.sem_inc(s_red, 1)
                mxv = mx[:, :, :].rearrange("p h b -> p b h")
                step(v.tensor_tensor(rest[:, :, :], srcn[:, :, :], mxv, ALU.add))
                step(v.tensor_tensor(rest[:, :, :], rest[:, :, :], row(w["L2_eb"][:, :]), ALU.add))
                step(v.memset(rn, 0.0))
                step(v.scalar_tensor_tensor(rest[:, :, :], rest[:, :, :], 0.2, rest[:, :, :], ALU.mult, ALU.max))
                step(v.tensor_scalar(rn[:, :, 0:H2], rest[:, :, :], -1.0, None, ALU.mult))
                split_bf16(step, v, srcn[:, :, :], [rn[:, :, ds(H2 * (n + 1), H2)] for n in range(3)], rest[:, :, :])
                v.sem_inc(s_rows, 1)
                step(v.tensor_tensor(ad[:, :, :], ad[:, :, :], row(w["L2_eb"][:, :]), ALU.add))
                v.wait_ge(s_rt, NB)
                v.tensor_copy(rows[:, :], ro[:, :])

            @block.tensor
            def _(pe):
                for h in range(H2):
                    if h >= 2:
                        pe.wait_ge(s_red, h - 1)
                    for b in range(NB):
                        mm = pe.transpose(rt[:, h % 2, ds(b * P, P)], R[:, h, ds(b * P, P)], k.ident_b[:, :])
                    mm.then_inc(s_tr, 1)
                pe.wait_ge(s_rows, 1)
                for b in range(NB):
                    pe.transpose(ro[:, ds(b * P, P)], rn[:, b, :], k.ident_b[:, :]).then_inc(s_rt, 1)


def layer2_attend(k, w, V, ad, srcn, rows, big, hout):
    with ExitStack() as ctx:
        AS0 = k.sb(ctx, "l2_AS", [P, N])
        AS = (AS0[:, :], k.x[:, :, :].rearrange("p b f -> p (b f)"))
        nm = k.sb(ctx, "l2_nm", [P, 2, N], BF16)
        U = k.sb(ctx, "l2_U", [P, 4, HALF])
        Rl = k.sb(ctx, "l2_relu", [P, 2, HALF])
        ad4 = srcn[:, :, :].rearrange("p b h -> p (b h)")
        BEFORE = P - P // 4
        Vs = k.sb(ctx, "l2_Vs", [P, 2, BEFORE + P])
        sums = k.sb(ctx, "l2_sums", [P, CH])
        rden = sums[:, 0:NB]
        fifth = k.sb(ctx, "l2_fifth", [P, P])
        s_no, s_sump = k.sem("l2a_mask_unit3"), k.sem("l2a_leaky_sum_pool")
        s_vs, s_ac, s_tb = (k.sem("l2a_" + n) for n in ("V_placed", "acc_copied", "turned_back"))
        TC = N // (UNITS // 4)
        sel = k.sb(ctx, "l2_sel", [P, 2, H2 * P], BF16)
        selr = U[0:NR, 0:2, :].rearrange("p a i -> p (a i)")
        s_sum = k.sem("l2a_leaky_sum")
        s_sel, s_selc = k.sem("l2a_sel_loaded"), k.sem("l2a_sel_ready")
        Vf = V[:, :, :, :].rearrange("p b h d -> p (b h d)")
        adf = ad[:, :, :].rearrange("p b h -> p (b h)")
        names = ("as_product", "as_ready", "logits", "leaky", "shifted", "exp", "pv", "shift", "mask", "head_summed", "rden", "head_out")
        s_asp, s_as, s_u, s_pre, s_add, s_e, s_pv, s_ps, s_nm, s_hs, s_rd, s_ho = (k.sem("l2a_" + n) for n in names)
        with k.block() as block, ExitStack() as pctx:
            ps = k.ps(pctx, "l2_ps", [P, 2, 2, CH])
            acc = k.ps(pctx, "l2_acc", [P, 2, CH])
            asp = k.ps(pctx, "l2_asp", [P, TC])
            back = k.ps(pctx, "l2_back", [P, 4, P])

            @block.sync
            def _(sp):
                sp.dma_start(selr, k.io["sel_rows"].rearrange("r a n -> r (a n)")).then_inc(s_sel, 16)
                sp.wait_ge(s_sel, 16)

            @block.gpsimd
            def _(pool):
                def mask(h, t, u):
                    pool.wait_ge(s_ps, h * UNITS + t * 4 + u + 1)
                    k.carry(pool, k.pool_waits)
                    pool.tensor_scalar(nm[:, u // 2, ds(u % 2 * HALF, HALF)], k.adj_rows((t * 2 + u // 2) % NB, u % 2 * HALF, HALF), 0.0, None, ALU.is_le).then_inc(s_nm, 1)

                def head(h, more):
                    for t in range(UNITS // 4):
                        ahead = more or t + 1 < UNITS // 4
                        if ahead:
                            mask(h, t + 1, 0)
                        pool.wait_ge(s_pre, h * UNITS + t * 4 + 3)
                        pool.tensor_tensor(U[:, 2, :], U[:, 2, :], Rl[:, 0, :], ALU.add).then_inc(s_sump, 1)
                        if ahead:
                            mask(h, t + 1, 1)
                            mask(h, t + 1, 2)

                for u in range(3):
                    mask(0, 0, u)
                with pool.Fori(0, H2 - 1) as h:
                    head(h, True)
                head(H2 - 1, False)

            @block.tensor
            def _(pe):
                pe.wait_ge(s_selc, 4)
                pe.sem_inc(s_ps, 4)
                pe.sem_inc(s_pv, 4)

                def shift(hp, t, u):
                    h, _ = hp
                    if u < 3:
                        pe.wait_ge(s_nm, h * (UNITS // 4 * 3) + t * 3 + u + 1)
                    else:
                        pe.wait_ge(s_no, h * (UNITS // 4) + t + 1)
                    joined = u % 4 == 0
                    pe.wait_ge(s_add, h * UNITS + t * 4 + u + 1)
                    for q in range(2):
                        i0 = u % 2 * HALF + q * CH
                        pe.matmul(ps[:, u % 2, q, :], sel[:, 0, ds(h * P, P)], rows[:, ds(i0, CH)], start=True, stop=False)
                        mm = pe.matmul(ps[:, u % 2, q, :], big[:, :], nm[:, u // 2 % 2, ds(i0, CH)], start=False, stop=not joined)
                    if joined:
                        pe.wait_ge(s_pre, h * UNITS + t * 4 + u + 1)
                        for q in range(2):
                            mm = pe.matmul(ps[:, u % 2, q, :], fifth[:, :], Rl[:, u % 2, ds(q * CH, CH)], start=False, stop=True)
                    mm.then_inc(s_ps, 1)

                def weigh(hp, t, u):
                    h, p = hp
                    pe.wait_ge(s_vs, h * NB + t * 2 + u // 2 + 1)
                    pe.wait_ge(s_e, h * UNITS + t * 4 + u + 1)
                    for q in range(2):
                        mm = pe.matmul(acc[:, p, :], Vs[:, u // 2, ds(BEFORE - (u % 2 * 2 + q) * (P // 4), P)], U[:, u % 4, ds(q * CH, CH)], start=False, stop=False, skip_group_check=True)
                    mm.then_inc(s_pv, 1)

                def source_terms(h, t):
                    pe.wait_ge(s_as, h * (UNITS // 4) + t + 1)
                    pe.matmul(asp[:, :], sel[:, 1, ds(h * P, P)], rows[:, ds(t * TC, TC)], start=True, stop=True).then_inc(s_asp, 1)

                def turn_back(h):
                    pe.wait_ge(s_ac, h + 3)
                    pe.wait_ge(s_ho, h + 1)
                    for b in range(4):
                        mm = pe.transpose(back[:, b, :], sums[:, ds(b * P, P)], k.ident[:, :])
                    mm.then_inc(s_tb, 1)

                def head(hp, then):
                    h, p = hp
                    pe.wait_ge(s_ac, h + 1)
                    pe.matmul(acc[:, p, :], k.zeros[:, 0:P], k.zeros[:, :], start=True, stop=False, skip_group_check=True)
                    first = isinstance(h, int) and h == 0
                    run_ahead(pe, 2, hp, UNITS // 4, 4, shift, weigh, start=first, follow=then,
                              before=(lambda t: source_terms(then[0], t)) if then else None, peeled=() if first else (lambda: turn_back(h - 1),))

                for t in range(UNITS // 4):
                    source_terms(0, t)
                each_head(pe, head)
                turn_back(H2 - 1)

            @block.scalar
            def _(act):
                act.preload_act_table(ACT.Exp)
                act.sem_inc(s_as, 1)

                def source_terms(hp, t):
                    h, p = hp
                    act.wait_ge(s_asp, h * (UNITS // 4) + t + 1)
                    k.carry(act, k.act_waits)
                    act.activation(AS[p][:, ds(t * TC, TC)], asp[:, :], ACT.Copy).then_inc(s_as, 1)

                def leaky(hp, t, u):
                    h, _ = hp
                    act.wait_ge(s_u, h * UNITS + t * 4 + u + 2)
                    act.wait_ge(s_add, h * UNITS + t * 4 + u + 1)
                    k.carry(act, k.act_waits)
                    act.activation(Rl[:, u % 2, :], U[:, u % 4, :], ACT.Relu, scale=4.0, bias=ad4[:, ds(t * (2 * H2) + u // 2 * H2 + h, 1)]).then_inc(s_pre, 1)

                def exps(hp, t, u):
                    h, _ = hp
                    act.wait_ge(s_add, h * UNITS + t * 4 + u + 3)
                    k.carry(act, k.act_waits)
                    act.activation(U[:, u, :], U[:, u, :], ACT.Exp, bias=adf[:, ds(t * (2 * H2) + u // 2 * H2 + h, 1)]).then_inc(s_e, 1)

                def head(hp, then):
                    run_ahead(act, 1, hp, UNITS // 4, 4, leaky, exps, start=isinstance(hp[0], int) and hp[0] == 0, follow=then,
                              midway=(lambda t: source_terms(then, t)) if then else None)

                for t in range(UNITS // 4):
                    source_terms((0, 0), t)
                each_head(act, head)

            @block.vector
            def _(v):
                k.steps.on(v)(v.memset(Vs[:, :, :], 0.0))
                k.steps(v.tensor_scalar(fifth[:, :], k.ident[:, :], 0.2, None, ALU.mult))
                v.memset(sel[:, :, :], 0.0).then_inc(s_selc, 1)
                v.wait_ge(s_selc, 1)
                v.wait_ge(s_sel, 16)
                v.tensor_copy(sel[0:NR, :, :].rearrange("r a n -> r (a n)"), selr).then_inc(s_selc, 1)
                v.tensor_scalar(ad4, adf, 4.0, None, ALU.mult).then_inc(s_selc, 1)
                v.wait_ge(s_selc, 3)
                v.tensor_scalar(adf, adf, 0.2, None, ALU.mult).then_inc(s_selc, 1)
                v.wait_ge(s_selc, 4)
                v.sem_inc(s_u, 1)
                v.sem_inc(s_add, 2)
                v.sem_inc(s_ho, 1)
                v.sem_inc(s_ac, 2)

                def logits(hp, t, u):
                    h, p = hp
                    if u == 0 and isinstance(t, int):
                        v.wait_ge(s_as, (h + 1) * (UNITS // 4) + 1)
                    v.wait_ge(s_pv, h * UNITS + t * 4 + u + 1)
                    v.scalar_tensor_tensor(U[:, u % 4, :], k.adjT[:, ds(t * (2 * N) + u // 2 * N + u % 2 * HALF, HALF)],
                                           w["L2_eW"][:, ds(h, 1)], AS[p][:, ds(u % 2 * HALF, HALF)], ALU.mult, ALU.add).then_inc(s_u, 1)
                    if u == 1:
                        v.tensor_scalar(nm[:, 1, HALF:], k.adj_rows(t * 2 + 1, HALF, HALF), 0.0, None, ALU.is_le).then_inc(s_no, 1)
                    if u % 2:
                        v.tensor_copy(Vs[:, u // 2, BEFORE:BEFORE + VW], Vf[:, ds(t * (2 * H2 * VW) + u // 2 * (H2 * VW) + h * VW, VW)]).then_inc(s_vs, 1)

                def shifted(hp, t, u):
                    h, _ = hp
                    shift = ps[:, u % 2, :, :].rearrange("p a c -> p (a c)")
                    if u == 0:
                        pass
                    elif u == 2:
                        v.wait_ge(s_sump, h * (UNITS // 4) + t + 1)
                    else:
                        v.wait_ge(s_pre, h * UNITS + t * 4 + u + 1)
                        v.tensor_tensor(U[:, u, :], U[:, u, :], Rl[:, u % 2, :], ALU.add).then_inc(s_sum, 1)
                        v.wait_ge(s_sum, h * (UNITS // 2) + t * 2 + u // 2 + 1)
                    v.wait_ge(s_ps, h * UNITS + t * 4 + u + 5)
                    v.scalar_tensor_tensor(U[:, u, :], U[:, u, :], 0.2, shift, ALU.mult, ALU.add).then_inc(s_add, 1)

                def copy_sums(h, p):
                    v.wait_ge(s_pv, h * UNITS + UNITS + 4)
                    v.wait_ge(s_ho, h + 1)
                    v.tensor_copy(sums[:, :], acc[:, p, :]).then_inc(s_ac, 1)

                def divide(h):
                    v.wait_ge(s_tb, h + 1)
                    av = back[:, :, :].rearrange("p b (c d) -> p c b d", d=P // 4)
                    rv = rden.rearrange("p (c b) -> p c b", b=4)
                    v.reciprocal(rv, av[:, :, :, HD]).then_inc(s_rd, 1)
                    v.wait_ge(s_rd, h + 1)
                    v.tensor_tensor(hout[:, :, ds(h * HD, HD)].rearrange("p (c b) d -> p c b d", b=4), av[:, :, :, 0:HD],
                                    rv.unsqueeze(3).broadcast_to([P, 4, 4, HD]), ALU.mult).then_inc(s_ho, 1)

                def head(hp, then):
                    h, p = hp
                    first = isinstance(h, int) and h == 0
                    run_ahead(v, 1, hp, UNITS // 4, 4, logits, shifted, start=first, follow=then,
                              peeled=() if first else (lambda: copy_sums(h - 1, 1 - p), lambda: divide(h - 1)))

                each_head(v, head)
                copy_sums(H2 - 1, 1)
                divide(H2 - 1)


def layer2_fuse(k, hout):
    with ExitStack() as ctx:
        w = load_weights(k, ctx, [("L2_fuse_WT", [D, D]), ("L2_fuse_b", [P, D]), ("L2_ln_g", [P, D]), ("L2_ln_b", [P, D])])
        s_w = k.sem("l2f_weights")
        hoT = k.sb(ctx, "l2_hoT", [P, N])
        y = k.sb(ctx, "l2_y", [P, NB, D])
        cen = k.sb(ctx, "l2_cen", [P, NB, D])
        mean, var, std = (k.sb(ctx, "l2f_" + n, [P, NB]) for n in ("mean", "var", "std"))
        s_tr, s_hoT, s_y, s_yb, s_var, s_std = (k.sem("l2f_" + n) for n in ("turned", "hoT", "product", "biased", "var", "std"))
        with k.block() as block, ExitStack() as pctx:
            tr = k.ps(pctx, "l2f_tr", [P, 4, CH])
            yp = k.ps(pctx, "l2f_yp", [P, 4, CH])

            @block.sync
            def _(sp):
                for n in w:
                    sp.dma_start(w[n][:, :], k.io[n] if len(k.io[n].shape) > 1 else k.io[n].partition_broadcast(P)).then_inc(s_w, 16)
                sp.wait_ge(s_w, 16 * len(w))
                sp.dma_start(k.x[:, :, :], k.x_kept).then_inc(k.s_x_kept, 16)
                sp.wait_ge(k.s_x_kept, 32)

            @block.tensor
            def _(pe):
                for b in range(NB):
                    pe.transpose(tr[:, b // 4, ds(b % 4 * P, P)], hout[:, b, :], k.ident[:, :]).then_inc(s_tr, 1)
                pe.wait_ge(s_w, 16 * len(w))
                for b in range(NB):
                    pe.wait_ge(s_hoT, b // 4 + 1)
                    pe.matmul(yp[:, b // 4, ds(b % 4 * P, P)], hoT[:, ds(b * P, P)], w["L2_fuse_WT"][:, :], start=True, stop=True).then_inc(s_y, 1)

            @block.scalar
            def _(act):
                for c in range(NC):
                    act.wait_ge(s_tr, 4 * c + 4)
                    act.activation(hoT[:, ds(c * CH, CH)], tr[:, c, :], ACT.Copy).then_inc(s_hoT, 1)
                act.wait_ge(s_var, 1)
                act.activation(std[:, :], var[:, :], ACT.Sqrt, bias=k.eps[:, :], scale=1.0 / D).then_inc(s_std, 1)

            @block.vector
            def _(v):
                step = k.steps.on(v)
                for c in range(4):
                    v.wait_ge(s_y, 4 * c + 4)
                    step(v.tensor_tensor(y[:, 4 * c:4 * c + 4, :], yp[:, c, :].rearrange("p (b f) -> p b f", f=D), row(w["L2_fuse_b"][:, :], 4), ALU.add))
                center_and_sum(v, step, y[:, :, :], cen[:, :, :], y[:, :, :], mean[:, :], var[:, :])
                v.sem_inc(s_var, 1)
                v.wait_ge(s_std, 1)
                step(v.reciprocal(var[:, :], std[:, :]))
                step(v.tensor_tensor(cen[:, :, :], cen[:, :, :], per_block(var[:, :]), ALU.mult))
                step(v.tensor_tensor(cen[:, :, :], cen[:, :, :], row(w["L2_ln_g"][:, :]), ALU.mult))
                step(v.tensor_tensor(cen[:, :, :], cen[:, :, :], row(w["L2_ln_b"][:, :]), ALU.add))
                v.wait_ge(k.s_x_kept, 32)
                step(v.scalar_tensor_tensor(k.x[:, :, :], cen[:, :, :], 0.0, k.x[:, :, :], ALU.max, ALU.add))


NQ = 2 * 3 * H3
UN3 = NB * NC
TINY = 1e-37


def layer3(k):
    with ExitStack() as ctx:
        gru_w = lambda a: [("L3_%s_%s" % (a, n), s) for n, s in (("WihT", [D, 3 * D]), ("WhhT", [D, 3 * D]), ("bih", [D, 3]), ("bhh", [D, 3]))]
        w = load_weights(k, ctx, [("L3_gat_W", [D, H3, D])] + gru_w("node"))
        hT = k.sb(ctx, "l3_hT", [P, N])
        dg = k.sb(ctx, "l3_diag", [P, NB])
        gru_sems = [k.sem("gru_" + n) for n in ("bias", "gates", "r", "z", "n_arg", "n", "out", "turned", "added")]
        e2 = k.sb(ctx, "l3_e", [P, NB, 2, H3])
        with ExitStack() as c1:
            w.update(load_weights(k, c1, [("L3_gat_WT", [D, H3, D]), ("L3_gat_a", [D, H3, 2])] + gru_w("edge")))
            q2 = k.sb(c1, "l3_q", [P, 2, NB, NQ], BF16)
            nsT = k.sb(c1, "l3_nsT", [P, N])
            with ExitStack() as c2:
                h = k.sb(c2, "l3_h", [P, NB, D])
                work = k.sb(c2, "l3_work", [P, NB, D])
                normed_and_turned(k, "l3_", w, h[:, :, :], hT, work[:, :, :])
                layer3_prepare(k, w, h, hT, work, dg, q2, nsT)
            gru(k, "l3e_", w, "L3_edge_", nsT, hT, dg, gru_sems, 0)
            layer3_scores(k, q2, e2)
        rows = k.sb(ctx, "l3_rows", [P, N], BF16)
        sel = k.sb(ctx, "l3_sel", [P, H3 * P], BF16)
        big = k.sb(ctx, "l3_big", [P, P], BF16)
        layer3_maxima(k, e2, rows, sel, big)
        with ExitStack() as c1:
            es = k.sb(c1, "l3_es", [P, NB, D])
            layer3_attend(k, w, hT, e2, rows, sel, big, es)
            layer3_turn(k, es)
            gru(k, "l3n_", w, "L3_node_", es[:, :, :].rearrange("p b f -> p (b f)"), hT, dg, gru_sems, NC)


def layer3_prepare(k, w, h, hT, work, dg, q2, nsT):
    with ExitStack() as ctx:
        wa = k.sb(ctx, "l3_wa", [D, 2 * H3])
        q = k.sb(ctx, "l3_qn", [P, NB, 2 * H3])
        qr = k.sb(ctx, "l3_qr", [P, NB, 2 * H3])
        s_dg, s_wap, s_wa, s_qp, s_ns, s_nsc = (k.sem("l3p_" + n) for n in ("diag_out", "wa_product", "wa", "q_product", "ns_product", "nsT"))
        with k.block() as block, ExitStack() as pctx:
            nsp = k.ps(pctx, "l3_nsp", [P, 4, CH])
            wap = k.ps(pctx, "l3_wap", [P, CH])
            qp = k.ps(pctx, "l3_qp", [P, CH])
            STEP = N + P
            head = k.adjT[:, 0:(NB - 1) * STEP].rearrange("p (b r) -> p b r", r=STEP)[:, :, 0:P]
            tail = k.adjT[:, (NB - 1) * STEP:]

            @block.vector
            def _(v):
                step = k.steps.on(v)
                step(v.tensor_tensor(work[:, 0:NB - 1, :], head, row(k.ident[:, :], NB - 1), ALU.mult))
                step(v.tensor_tensor(work[:, NB - 1, :], tail, k.ident[:, :], ALU.mult))
                step(v.tensor_reduce(dg[:, :], work[:, :, :], AX_X, ALU.add))
                step(v.tensor_tensor(head, head, work[:, 0:NB - 1, :], ALU.subtract))
                v.tensor_tensor(tail, tail, work[:, NB - 1, :], ALU.subtract).then_inc(s_dg, 1)
                v.wait_ge(s_wap, 1)
                v.tensor_copy(wa[:, :], wap[:, 0:2 * H3]).then_inc(s_wa, 1)
                v.wait_ge(s_qp, 1)
                step(v.tensor_copy(q[:, :, :], qp[:, 0:NB * 2 * H3].rearrange("p (b q) -> p b q", q=2 * H3)))
                parts = lambda s: [q2[:, s, :, :].rearrange("p b (s r h) -> p b s r h", s=2, r=3)[:, :, :, r, :] for r in range(3)]
                qv, rv = (t[:, :, :].rearrange("p b (s h) -> p b s h", s=2) for t in (q, qr))
                split_bf16(step, v, qv, parts(0), rv)
                n3 = NQ // 2
                step(v.tensor_copy(q2[:, 1, :, 0:n3], q2[:, 0, :, n3:]))
                step(v.tensor_copy(q2[:, 1, :, n3:], q2[:, 0, :, 0:n3]))

            @block.tensor
            def _(pe):
                for n in range(H3):
                    mm = pe.matmul(wap[:, 0:2 * H3].rearrange("p (a h) -> p h a", a=2)[:, n, :], w["L3_gat_WT"][:, n, :], w["L3_gat_a"][:, n, :], start=True, stop=True)
                mm.then_inc(s_wap, 1)
                pe.wait_ge(s_dg, 1)
                for c in range(NC):
                    for jb in range(NB):
                        mm = pe.matmul(nsp[:, c, :], h[:, jb, :], k.adj_rows(jb, c * CH, CH), start=jb == 0, stop=jb == NB - 1)
                    mm.then_inc(s_ns, 1)
                    if c == 0:
                        pe.wait_ge(s_wa, 1)
                        for b in range(NB):
                            mm = pe.matmul(qp[:, ds(b * 2 * H3, 2 * H3)], hT[:, ds(b * P, P)], wa[:, :], start=True, stop=True)
                        mm.then_inc(s_qp, 1)

            @block.scalar
            def _(act):
                for c in range(NC):
                    act.wait_ge(s_ns, c + 1)
                    act.activation(nsT[:, ds(c * CH, CH)], nsp[:, c, :], ACT.Copy).then_inc(s_nsc, 1)


def gru(k, tag, w, name, xT, hT, dg, sems, done):
    wi, wh, bi, bh = (w[name + n] for n in ("WihT", "WhhT", "bih", "bhh"))
    with ExitStack() as ctx:
        r, z, m, o = (k.sb(ctx, tag + n, [P, 2, CH]) for n in ("r", "z", "m", "o"))
        b2 = k.sb(ctx, tag + "b2", [P, 2])
        s_b, s_g, s_r, s_z, s_na, s_n, s_o, s_tr, s_add = sems
        with k.block() as block, ExitStack() as pctx:
            gp = k.ps(pctx, tag + "gp", [P, 2, 4, CH])

            @block.tensor
            def _(pe):
                for c in range(NC + 1):
                    n, i, g = c + done, ds(c * CH, CH), gp[:, c % 2, :, :]
                    if c < NC:
                        for gate, used in ((0, s_r), (1, s_z)):
                            if c >= 2:
                                pe.wait_ge(used, n - 1)
                            pe.matmul(g[:, gate, :], wi[:, ds(gate * D, D)], xT[:, i], start=True, stop=False)
                            pe.matmul(g[:, gate, :], wh[:, ds(gate * D, D)], hT[:, i], start=False, stop=True).then_inc(s_g, 1)
                        if c >= 2:
                            pe.wait_ge(s_na, n - 1)
                        pe.matmul(g[:, 2, :], wi[:, ds(2 * D, D)], xT[:, i], start=True, stop=True).then_inc(s_g, 1)
                    if c >= 1:
                        pe.wait_ge(s_o, n)
                        for b in range(4):
                            mm = pe.transpose(gp[:, (c - 1) % 2, 3, ds(b * P, P)], o[:, (c - 1) % 2, ds(b * P, P)], k.ident[:, :])
                        mm.then_inc(s_tr, 1)
                    if c < NC:
                        if c >= 2:
                            pe.wait_ge(s_add, 4 * (n - 1))
                        pe.matmul(g[:, 3, :], wh[:, ds(2 * D, D)], hT[:, i], start=True, stop=True).then_inc(s_g, 1)

            @block.scalar
            def _(act):
                act.preload_act_table(ACT.Sigmoid)
                act.wait_ge(s_b, done // NC + 1)
                for c in range(NC + 1):
                    n = c + done
                    if c >= 1:
                        act.wait_ge(s_na, n)
                        act.activation(m[:, (c - 1) % 2, :], m[:, (c - 1) % 2, :], ACT.Tanh, bias=bi[:, 2:3]).then_inc(s_n, 1)
                    if c < NC:
                        for gate, out, ready, used in ((0, r, s_r, s_na), (1, z, s_z, s_o)):
                            act.wait_ge(s_g, 4 * n + gate + 1)
                            if c >= 2:
                                act.wait_ge(used, n - 1)
                            act.activation(out[:, c % 2, :], gp[:, c % 2, gate, :], ACT.Sigmoid, bias=b2[:, gate:gate + 1]).then_inc(ready, 1)

            @block.vector
            def _(v):
                step = k.steps.on(v)
                v.tensor_tensor(b2[:, :], bi[:, 0:2], bh[:, 0:2], ALU.add).then_inc(s_b, 1)

                def argument(c):
                    v.wait_ge(s_r, c + done + 1)
                    v.wait_ge(s_g, 4 * (c + done) + 4)
                    step(v.scalar_tensor_tensor(m[:, c % 2, :], gp[:, c % 2, 3, :], bh[:, 2:3], r[:, c % 2, :], ALU.add, ALU.mult))
                    step(v.tensor_tensor(m[:, c % 2, :], m[:, c % 2, :], gp[:, c % 2, 2, :], ALU.add))
                    v.sem_inc(s_na, 1)

                def blend(c):
                    v.wait_ge(s_n, c + done + 1)
                    v.wait_ge(s_z, c + done + 1)
                    step(v.tensor_tensor(o[:, c % 2, :], hT[:, ds(c * CH, CH)], m[:, c % 2, :], ALU.subtract))
                    step(v.tensor_tensor(o[:, c % 2, :], o[:, c % 2, :], z[:, c % 2, :], ALU.mult))
                    step(v.tensor_tensor(o[:, c % 2, :], o[:, c % 2, :], m[:, c % 2, :], ALU.add))
                    v.sem_inc(s_o, 1)

                def add(c):
                    v.wait_ge(s_tr, c + done + 1)
                    for b in range(4):
                        xb = k.x[:, 4 * c + b, :]
                        v.scalar_tensor_tensor(xb, gp[:, c % 2, 3, ds(b * P, P)], dg[:, 4 * c + b:4 * c + b + 1], xb, ALU.mult, ALU.add).then_inc(s_add, 1)

                for c in range(NC + 2):
                    if c >= 2:
                        add(c - 2)
                    if 1 <= c <= NC:
                        blend(c - 1)
                    if c < NC:
                        argument(c)


def layer3_scores(k, q2, e2):
    with ExitStack() as ctx:
        mk = k.sb(ctx, "l3_mask", [P, 2, 2, N], BF16)
        eq = k.sb(ctx, "l3_eq", [P, NB, 2, 3, H3])
        s_m, s_p = (k.sem("l3s_" + n) for n in ("masks", "summed"))
        with k.block() as block, ExitStack() as pctx:
            ep = k.ps(pctx, "l3_ep", [P, CH])
            qf = q2[:, :, :, :].rearrange("p s b q -> p (s b q)")

            @block.vector
            def _(v):
                step = k.steps.on(v)
                v.sem_inc(s_p, 2)
                with v.Fori(0, NB // 2) as t:
                    for u in range(2):
                        v.wait_ge(s_p, t * 2 + u + 1)
                        v.tensor_scalar(mk[:, u, 0, :], k.adj_rows(t * 2 + u), 0.0, None, ALU.is_gt).then_inc(s_m, 1)
                        v.tensor_scalar(mk[:, u, 1, :], k.adj_rows(t * 2 + u), 0.0, None, ALU.is_lt).then_inc(s_m, 1)
                v.wait_ge(s_p, NB + 2)
                step(v.tensor_copy(eq[:, :, :, :, :].rearrange("p b s r h -> p (b s r h)"), ep[:, 0:NB * NQ]))
                step(v.tensor_tensor(e2[:, :, :, :], eq[:, :, :, 2, :], eq[:, :, :, 1, :], ALU.add))
                step(v.tensor_tensor(e2[:, :, :, :], e2[:, :, :, :], eq[:, :, :, 0, :], ALU.add))
                ef = e2[:, :, :, :].rearrange("p b s h -> p (b s h)")
                step(v.scalar_tensor_tensor(ef, ef, 0.2, ef, ALU.mult, ALU.max))

            @block.tensor
            def _(pe):
                pe.matmul(ep[:, 0:NB * NQ], k.zeros[:, 0:P], k.zeros[:, 0:NB * NQ], start=True, stop=False, skip_group_check=True)
                with pe.Fori(0, NB // 2) as t:
                    for u in range(2):
                        pe.wait_ge(s_m, t * 4 + 2 * u + 2)
                        for b in range(NB):
                            for sign in range(2):
                                mm = pe.matmul(ep[:, ds(b * NQ, NQ)], mk[:, u, sign, ds(b * P, P)], qf[:, ds(t * (2 * NQ) + u * NQ + sign * NB * NQ, NQ)],
                                               start=False, stop=False, skip_group_check=True)
                        mm.then_inc(s_p, 1)


def layer3_maxima(k, e2, rows, sel, big):
    with ExitStack() as ctx:
        R = k.sb(ctx, "l3_R", [P, H3, N], BF16)
        t = k.sb(ctx, "l3_t", [P, H3, N], BF16)
        neg = k.sb(ctx, "l3_neg", [P, 2, N], BF16)
        BT = k.sb(ctx, "l3_BT", [P, 2, N], BF16)
        dI = k.sb(ctx, "l3_dI", [P, 2, H3, P], BF16)
        de = k.sb(ctx, "l3m_de", [P, NB, H3])
        mx = k.sb(ctx, "l3_mx", [P, H3, NB])
        rn = BT[:, 0, :].rearrange("p (b r) -> p b r", r=P)
        selr = k.sb(ctx, "l3_selr", [H3, H3 * P])
        s_sel, s_bt, s_sum, s_t, s_m, s_tr, s_rows, s_rt = (k.sem("l3m_" + n) for n in ("sel", "tiles", "summed", "logits", "maxed", "turned", "rows", "rows_turned"))
        TILES = 2 + H3
        ef = e2[:, :, :, :].rearrange("p b s h -> p (b s h)")
        df = de[:, :, :].rearrange("p b h -> p (b h)")
        with k.block() as block, ExitStack() as pctx:
            masked = k.ps(pctx, "l3_masked", [P, 2, 4, CH])

            @block.sync
            def _(sp):
                sp.dma_start(selr[:, :], k.io["sel_rows3"]).then_inc(s_sel, 16)
                sp.wait_ge(s_sel, 16)
                sp.dma_start(k.x_kept, k.x[:, :, :]).then_inc(k.s_x_stored, 16)
                sp.wait_ge(k.s_x_stored, 16)

            @block.tensor
            def _(pe):
                with pe.Fori(0, NB // 2) as tt:
                    for n in range(2 * H3):
                        u, h = divmod(n, H3)
                        pe.wait_ge(s_bt, tt * (2 * TILES) + (u + 1) * TILES)
                        pe.wait_ge(s_t, tt * (2 * H3) + n + 1)
                        for c in range(NC):
                            i = ds(c * CH, CH)
                            pe.matmul(masked[:, n % 2, c, :], dI[:, u, h, :], neg[:, u, i], start=True, stop=False)
                            mm = pe.matmul(masked[:, n % 2, c, :], k.ident_b[:, :], BT[:, u, i], start=False, stop=True)
                        mm.then_inc(s_sum, 1)

            @block.scalar
            def _(act):
                act.sem_inc(s_t, 2)
                with act.Fori(0, NB // 2) as tt:
                    for n in range(2 * H3):
                        u, h = divmod(n, H3)
                        act.wait_ge(s_sum, tt * (2 * H3) + n + 1)
                        act.wait_ge(s_m, tt * (2 * H3) + n + 1)
                        k.carry(act, k.act_waits)
                        act.activation(t[:, h, :], masked[:, n % 2, :, :].rearrange("p c i -> p (c i)"), ACT.Identity,
                                       bias=ef[:, ds(tt * (4 * H3) + u * (2 * H3) + h, 1)]).then_inc(s_t, 1)

            @block.vector
            def _(v):
                step = k.steps.on(v)
                step(v.memset(sel[:, :], 0.0))
                v.wait_ge(s_sel, 16)
                step(v.tensor_copy(sel[0:H3, :], selr[:, :]))
                step(v.tensor_scalar(big[:, :], k.ident[:, :], -BIG, None, ALU.mult))
                step(v.memset(R[:, :, :], -BIG))
                step(v.tensor_tensor(de[:, :, :], e2[:, :, 1, :], e2[:, :, 0, :], ALU.subtract))
                v.sem_inc(s_m, 3)

                def tiles(jb, u):
                    v.tensor_scalar(BT[:, u, :], k.adj_rows(jb), 0.0, -BIG, ALU.is_equal, ALU.mult).then_inc(s_bt, 1)
                    v.tensor_scalar(neg[:, u, :], k.adj_rows(jb), 0.0, None, ALU.is_lt).then_inc(s_bt, 1)
                    for h in range(H3):
                        v.tensor_scalar(dI[:, u, h, :], k.ident_b[:, :], df[:, ds(jb * H3 + h, 1)], None, ALU.mult).then_inc(s_bt, 1)

                def compare(jb, u, more):
                    for h in range(H3):
                        v.wait_ge(s_t, jb * H3 + h + 3)
                        v.tensor_tensor(R[:, h, :], R[:, h, :], t[:, h, :], ALU.max).then_inc(s_m, 1)
                    v.wait_ge(s_m, jb * H3 + H3 + 3)
                    if more:
                        tiles(jb + 2, u)

                tiles(0, 0)
                tiles(1, 1)
                with v.Fori(0, NB // 2 - 1) as tt:
                    compare(tt * 2, 0, True)
                    compare(tt * 2 + 1, 1, True)
                compare(NB - 2, 0, False)
                compare(NB - 1, 1, False)

        with k.block() as block, ExitStack() as pctx:
            rt = k.ps(pctx, "l3_rt", [P, H3, N], BF16)
            ro = k.ps(pctx, "l3_ro", [P, N], BF16)

            @block.vector
            def _(v):
                step = k.steps.on(v)
                for h in range(H3):
                    v.wait_ge(s_tr, h + 1)
                    step(v.tensor_reduce(mx[:, h, :], rt[:, h, :].rearrange("p (b q) -> p b q", q=P), AX_X, ALU.max))
                step(v.memset(rn, 0.0))
                mf = mx[:, :, :].rearrange("p h b -> p (h b)")
                step(v.scalar_tensor_tensor(mf, mf, -0.5 * BIG, mf, ALU.is_gt, ALU.mult))
                step(v.tensor_scalar(rn[:, :, 0:H3].rearrange("p b h -> p h b"), mx[:, :, :], -1.0, None, ALU.mult))
                v.sem_inc(s_rows, 1)
                v.wait_ge(s_rt, NB)
                v.tensor_copy(rows[:, :], ro[:, :])

            @block.tensor
            def _(pe):
                for h in range(H3):
                    for b in range(NB):
                        mm = pe.transpose(rt[:, h, ds(b * P, P)], R[:, h, ds(b * P, P)], k.ident_b[:, :])
                    mm.then_inc(s_tr, 1)
                pe.wait_ge(s_rows, 1)
                for b in range(NB):
                    pe.transpose(ro[:, ds(b * P, P)], rn[:, b, :], k.ident_b[:, :]).then_inc(s_rt, 1)


def layer3_attend(k, w, hT, e2, rows, sel, big, es):
    with ExitStack() as ctx:
        hW = k.sb(ctx, "l3_hW", [P, NB * D])
        mk = k.sb(ctx, "l3_mk", [P, 2, 2, N], BF16)
        U = k.sb(ctx, "l3_U", [P, 4, CH])
        W = k.sb(ctx, "l3_W", [P, 4, CH])
        rden = k.sb(ctx, "l3_rden", [P, NB])
        de = k.sb(ctx, "l3_de", [P, NB, H3])
        ones = k.sb(ctx, "l3_ones", [P, 1])
        part = W[:, :, :].rearrange("p c (r f) -> p (c r) f", f=D)
        ef = e2[:, :, :, :].rearrange("p b s h -> p (b s h)")
        df = de[:, :, :].rearrange("p b h -> p (b h)")
        S = k.x[:, :, :].rearrange("p (c b) f -> p c (b f)", c=4)
        s_sum, s_zero = k.sem("l3a_exp_summed"), k.sem("l3a_sums_zero")
        names = ("init", "hW_product", "hW", "mask", "negative", "shift", "logits", "exp", "weighed", "summed", "head_summed", "head_out")
        s_i, s_hp, s_hw, s_mo, s_mn, s_ps, s_u, s_e, s_w, s_pv, s_hs, s_ho = (k.sem("l3a_" + n) for n in names)
        with k.block() as block, ExitStack() as pctx:
            ps = k.ps(pctx, "l3_ps", [P, 4, CH])
            acc = k.ps(pctx, "l3_acc", [P, 4, CH])

            @block.gpsimd
            def _(pool):
                pool.sem_inc(s_sum, 4)
                with pool.Fori(0, H3) as h:
                    pool.wait_ge(s_hs, h + 1)
                    k.carry(pool, k.pool_waits)
                    pool.memset(S[:, :, :], 0.0).then_inc(s_zero, 1)
                    with pool.Fori(0, NB) as jb:
                        pool.wait_ge(s_zero, h + 1)
                        for c in range(4):
                            pool.wait_ge(s_sum, h * UN3 + jb * 4 + c + 1)
                            k.carry(pool, k.pool_waits)
                            pool.wait_ge(s_e, h * UN3 + jb * 4 + c + 1)
                            pool.tensor_tensor(S[:, c, :], S[:, c, :], U[:, c, :], ALU.add).then_inc(s_sum, 1)

            @block.tensor
            def _(pe):
                pe.sem_inc(s_ps, 8)
                pe.sem_inc(s_pv, 4)

                def shift(h, t, n):
                    pe.wait_ge(s_mo, h * NB + t * 2 + n // 4 + 1)
                    pe.wait_ge(s_u, h * UN3 + t * 8 + n + 5)
                    i = ds(n % 4 * CH, CH)
                    pe.matmul(ps[:, n % 4, :], sel[:, ds(h * P, P)], rows[:, i], start=True, stop=False)
                    pe.matmul(ps[:, n % 4, :], big[:, :], mk[:, n // 4 % 2, 0, i], start=False, stop=True).then_inc(s_ps, 1)

                def weigh(h, t, n):
                    pe.wait_ge(s_w, h * UN3 + t * 8 + n + 1)
                    for b in range(4):
                        ib = n % 4 * 4 + b
                        mm = pe.matmul(acc[:, ib // 4, ds(ib % 4 * D, D)], W[:, n % 4, ds(b * P, P)], hW[:, ds(t * (2 * D) + n // 4 * D, D)],
                                       start=False, stop=False, skip_group_check=True)
                    mm.then_inc(s_pv, 1)

                pe.sem_inc(s_hs, 1)
                pe.wait_ge(s_i, 2)
                with pe.Fori(0, H3) as h:
                    wk = w["L3_gat_W"][:, :, :].rearrange("p h f -> p (h f)")[:, ds(h * D, D)]
                    for c in range(4):
                        pe.wait_ge(s_hw, h * 4 + c + 1)
                        pe.wait_ge(s_u, h * UN3 + 8)
                        for b in range(4):
                            mm = pe.matmul(ps[:, c % 2, ds(b * P, P)], hT[:, ds((4 * c + b) * P, P)], wk, start=True, stop=True)
                        mm.then_inc(s_hp, 1)
                    pe.wait_ge(s_hw, h * 4 + 4 + 2)
                    pe.wait_ge(s_ho, h + 1)
                    for b in range(4):
                        pe.matmul(acc[:, b, :], k.zeros[:, 0:P], k.zeros[:, :], start=True, stop=False, skip_group_check=True)
                    run_ahead(pe, 3, h, UN3 // 8, 8, shift, weigh)
                    pe.wait_ge(s_sum, h * UN3 + UN3 + 4)
                    for ib in range(NB):
                        mm = pe.matmul(ps[:, 3, ib:ib + 1], S[:, ib // 4, ds(ib % 4 * P, P)], ones[:, :], start=True, stop=True)
                    mm.then_inc(s_hs, 1)

            @block.scalar
            def _(act):
                act.preload_act_table(ACT.Exp)
                act.sem_inc(s_hw, 2)
                with act.Fori(0, H3) as h:
                    for c in range(4):
                        act.wait_ge(s_hp, h * 4 + c + 1)
                        act.wait_ge(s_pv, h * UN3 + 4)
                        act.activation(hW[:, ds(c * CH, CH)], ps[:, c % 2, :], ACT.Copy).then_inc(s_hw, 1)
                    with act.Fori(0, UN3 // 8) as t:
                        for n in range(8):
                            act.wait_ge(s_u, h * UN3 + t * 8 + n + 9)
                            k.carry(act, k.act_waits)
                            act.activation(U[:, n % 4, :], U[:, n % 4, :], ACT.Exp, bias=ef[:, ds(t * (4 * H3) + n // 4 * (2 * H3) + h, 1)]).then_inc(s_e, 1)

            @block.vector
            def _(v):
                step = k.steps.on(v)
                step(v.memset(es[:, :, :], 0.0))
                v.memset(ones[:, :], 1.0).then_inc(s_i, 1)
                step(v.tensor_tensor(de[:, :, :], e2[:, :, 1, :], e2[:, :, 0, :], ALU.subtract))
                v.sem_inc(s_i, 1)
                v.sem_inc(s_u, 8)
                v.sem_inc(s_ho, 1)

                def zero_mask(jb, slot):
                    v.tensor_scalar(mk[:, slot, 0, :], k.adj_rows(jb), 0.0, None, ALU.is_equal).then_inc(s_mo, 1)

                def logits(h, t, n):
                    if n % 4 == 0:
                        v.tensor_scalar(mk[:, n // 4, 1, :], k.adj_rows(t * 2 + n // 4), 0.0, None, ALU.is_lt).then_inc(s_mn, 1)
                        v.wait_ge(s_mn, h * NB + t * 2 + n // 4 + 1)
                    v.wait_ge(s_pv, h * UN3 + t * 8 + n + 1)
                    v.wait_ge(s_sum, h * UN3 + t * 8 + n + 1)
                    if n % 4 == 1 and not (n == 5 and isinstance(t, int)):
                        zero_mask(t * 2 + n // 4 + 1, 1 - n // 4)
                    v.wait_ge(s_ps, h * UN3 + t * 8 + n + 9)
                    v.scalar_tensor_tensor(U[:, n % 4, :], mk[:, n // 4, 1, ds(n % 4 * CH, CH)], df[:, ds(t * (2 * H3) + n // 4 * H3 + h, 1)],
                                           ps[:, n % 4, :], ALU.mult, ALU.add).then_inc(s_u, 1)

                def weighed(h, t, n):
                    v.wait_ge(s_e, h * UN3 + t * 8 + n + 1)
                    v.tensor_tensor(W[:, n % 4, :], U[:, n % 4, :], k.adjT[:, ds(t * (2 * N) + n * CH, CH)], ALU.mult).then_inc(s_w, 1)

                first, PER = step.n, 4
                with v.Fori(0, H3) as h:
                    step.begin(h, PER)
                    zero_mask(0, 0)
                    run_ahead(v, 1, h, UN3 // 8, 8, logits, weighed)
                    v.wait_ge(s_hs, h + 2)
                    step(v.tensor_scalar(rden[:, :], ps[:, 3, 0:NB], TINY, None, ALU.max))
                    step(v.reciprocal(rden[:, :], rden[:, :]))
                    step(v.tensor_tensor(part[:, :, :], acc[:, :, :].rearrange("p c (b f) -> p (c b) f", f=D), per_block(rden[:, :]), ALU.mult))
                    v.sem_inc(s_ho, 1)
                    step(v.scalar_tensor_tensor(es[:, :, :], part[:, :, :], 1.0 / H3, es[:, :, :], ALU.mult, ALU.add))
                    step.end(H3, first, PER)


def layer3_turn(k, es):
    s_tr, s_c = k.sem("l3t_turned"), k.sem("l3t_copied")
    with k.block() as block, ExitStack() as pctx:
        tr = k.ps(pctx, "l3t_tr", [P, 4, CH])

        @block.sync
        def _(sp):
            sp.dma_start(k.x[:, :, :], k.x_kept).then_inc(k.s_x_stored, 16)
            sp.wait_ge(k.s_x_stored, 32)

        @block.tensor
        def _(pe):
            for b in range(NB):
                pe.transpose(tr[:, b // 4, ds(b % 4 * P, P)], es[:, b, :], k.ident[:, :]).then_inc(s_tr, 1)

        @block.scalar
        def _(act):
            for c in range(NC):
                act.wait_ge(s_tr, 4 * c + 4)
                act.activation(es[:, 4 * c:4 * c + 4, :], tr[:, c, :].rearrange("p (b f) -> p b f", f=D), ACT.Copy).then_inc(s_c, 1)


def stage_store(k):
    s_out = k.sem("out_stored")
    with k.block() as block:

        @block.sync
        def _(sp):
            sp.dma_start(k.io["out"].rearrange("(b p) f -> p b f", p=P), k.x[:, :, :]).then_inc(s_out, 16)
            sp.wait_ge(s_out, 16)


def build(nc, io):
    with ExitStack() as ctx:
        k = Core(nc, io, ctx)
        stage_start(k)
        layer0(k)
        layer1(k)
        layer2(k)
        layer3(k)
        stage_store(k)


def selectors():
    s = np.zeros((4, H2, 2, H2, P), np.float32)
    for h in range(H2):
        s[0, h, 0, h, :] = 1.0
        s[1:, h, 1, h, :] = 1.0
    return s.reshape(NR, 2, H2 * P)


def _laid_out(inp):
    f = lambda n: np.asarray(inp[n])
    c = np.ascontiguousarray
    halves = lambda a: c(np.moveaxis(a.reshape(CB, P, *a.shape[1:]), 0, 1))
    return {
        "x": c(f("x")), "adjT": c(f("adj").T),
        "ident": np.eye(P, dtype=np.float32),
        "L2_WT": c(f("L2_gnn_W").T), "L2_src": f("L2_gnn_attn_src").reshape(D, 1), "L2_dst": f("L2_gnn_attn_dst").reshape(D, 1),
        "head_mask": np.repeat(np.eye(H2, dtype=np.float32), HD, axis=0), "sel_rows": selectors(),
        "L2_eW": f("L2_gnn_edge_W").reshape(H2), "L2_eb": f("L2_gnn_edge_b"), "L2_fuse_WT": c(f("L2_gnn_fuse_W").T),
        "L2_fuse_b": f("L2_gnn_fuse_b"), "L2_ln_g": f("L2_gnn_ln_g"), "L2_ln_b": f("L2_gnn_ln_b"),
        "L3_gat_W": c(f("L3_gnn_gat_W").transpose(1, 0, 2)), "L3_gat_WT": c(f("L3_gnn_gat_W").transpose(2, 0, 1)),
        "L3_gat_a": c(f("L3_gnn_gat_a").reshape(H3, 2, D).transpose(2, 0, 1)),
        "sel_rows3": np.repeat(np.eye(H3, dtype=np.float32), P, axis=1),
        **{"L3_%s_W%sT" % (a, b): c(f("L3_gnn_%s_W%s" % (a, b)).T) for a in ("edge", "node") for b in ("ih", "hh")},
        **{"L3_%s_b%s" % (a, b): c(f("L3_gnn_%s_b%s" % (a, b)).reshape(3, D).T) for a in ("edge", "node") for b in ("ih", "hh")},
        "L1_gcn_w": c(f("L1_gnn_gcn_w")), "L1_gcn_b": c(f("L1_gnn_gcn_b")), "L1_w_in": c(f("L1_gnn_w_in")),
        "L1_w_xp": halves(f("L1_gnn_w_xp")), "L1_w_dt": c(f("L1_gnn_w_dt")), "L1_w_out": halves(f("L1_gnn_w_out")),
        "L1_A_log": halves(f("L1_gnn_A_log")).reshape(P, CB * DS), "L1_conv_w": halves(f("L1_gnn_conv_w")),
        "L1_conv_b": halves(f("L1_gnn_conv_b")), "L1_b_dt": halves(f("L1_gnn_b_dt")), "L1_D": halves(f("L1_gnn_D_skip")),
        "L1_ln_g": f("L1_gnn_ln_g").reshape(D, 1), "L1_ln_b": f("L1_gnn_ln_b").reshape(D, 1),
        "L0_WT": c(f("L0_gnn_W").T), "L0_bias": c(f("L0_gnn_bias")), "L0_b": c(f("L0_gnn_b")),
    }


def kernel(**inputs):
    import concourse.bacc as bacc
    from concourse.bass_utils import run_bass_kernel_spmd as run

    arrays = _laid_out(inputs)
    nc = bacc.Bacc("TRN2", target_bir_lowering=False, num_devices=1)
    io = {n: nc.dram_tensor("in_" + n, a.shape, mybir.dt.from_np(a.dtype), kind="ExternalInput").ap() for n, a in arrays.items()}
    io["out"] = nc.dram_tensor("out_x", (N, D), F32, kind="ExternalOutput").ap()
    build(nc, io)
    r = run(nc, [{"in_" + n: a for n, a in arrays.items()}], core_ids=[0])
    return r.results[0]["out_x"]
```
